# Optimizing a Trainium2 kernel written in Bass

```python
import numpy as np
import jax
import jax.numpy as jnp

def _softmax(x, axis=-1):
    return jax.nn.softmax(x, axis=axis)

def _gelu(x):
    return jax.nn.gelu(x, approximate=True)

def _silu(x):
    return jax.nn.silu(x)

def _sigmoid(x):
    return jax.nn.sigmoid(x)

def _layernorm(x, axis=-1, eps=1e-05):
    m = jnp.mean(x, axis=axis, keepdims=True)
    v = jnp.var(x, axis=axis, keepdims=True)
    return (x - m) / jnp.sqrt(v + eps)

def _scatter_add(tgt, idx, src, axis=0):
    return tgt.at[idx].add(src)

def _segment_sum(src, seg, n):
    return jax.ops.segment_sum(src, seg, n)
kernel_name = 'mk_seq_preln_d2_jaxref_r8_07f0ae'

def setup_inputs(seed: int=0):
    np.random.seed(seed)
    _w = jnp.asarray

    def _L0_attn_setup():
        import jax, jax.numpy as jnp
        import numpy as np
        H = 256
        NH = 16
        KD = H // 2
        VD = H // 2
        DK = KD // NH
        DV = VD // NH
        RLOW = 64
        GLOW = 64
        EPS = 1e-05
        B, T = (2, 128)
        key = jax.random.key(seed)
        ks = jax.random.split(key, 18)

        def rn(k, shape, scale=0.02):
            return (jax.random.normal(k, shape) * scale).astype(jnp.float32)
        return {'x': jax.random.normal(ks[0], (B, T, H), dtype=jnp.float32), 'mu_x': rn(ks[1], (H,), 0.5), 'Wx1': rn(ks[2], (H, 5 * RLOW)), 'Wx2': rn(ks[3], (H, 5, RLOW)), 'x_bias': rn(ks[4], (5, H)), 'Wr': rn(ks[5], (H, KD)), 'Wk': rn(ks[6], (H, KD)), 'Wv': rn(ks[7], (H, VD)), 'Ww_a': rn(ks[8], (H, GLOW)), 'Ww_b': rn(ks[9], (GLOW, KD)), 'bw': rn(ks[10], (KD,)), 'Wg_a': rn(ks[11], (H, GLOW)), 'Wg_b': rn(ks[12], (GLOW, VD)), 'bg': rn(ks[13], (VD,)), 'bonus': rn(ks[14], (NH, DK), 0.5), 'ln_w': jnp.ones((DV,), jnp.float32), 'ln_b': jnp.zeros((DV,), jnp.float32), 'Wo': rn(ks[15], (VD, H))}
    _L0_attn_in = _L0_attn_setup()

    def _L0_ffn_setup():
        import jax, jax.numpy as jnp
        import numpy as np
        E = 8
        K = 2
        D = 256
        F = 1024
        R = 16
        SCALING = 32.0 / 16.0

        def gelu_new(x):
            return jax.nn.gelu(x, approximate=True)
        key = jax.random.key(seed)
        ks = jax.random.split(key, 9)
        std = 0.02
        hidden_states = jax.random.normal(ks[0], (1, 128, D), dtype=jnp.float32)
        Wr = jax.random.normal(ks[1], (D, E), dtype=jnp.float32) * std
        br = jnp.zeros((E,), dtype=jnp.float32)
        W1 = jax.random.normal(ks[2], (D, F), dtype=jnp.float32) * std
        b1 = jnp.zeros((F,), dtype=jnp.float32)
        W2 = jax.random.normal(ks[3], (F, D), dtype=jnp.float32) * std
        b2 = jnp.zeros((D,), dtype=jnp.float32)
        A1 = jax.random.normal(ks[4], (E, R, D), dtype=jnp.float32) * std
        B1 = jax.random.normal(ks[5], (E, F, R), dtype=jnp.float32) * std
        A2 = jax.random.normal(ks[6], (E, R, F), dtype=jnp.float32) * std
        B2 = jax.random.normal(ks[7], (E, D, R), dtype=jnp.float32) * std
        return {'hidden_states': hidden_states, 'Wr': Wr, 'br': br, 'W1': W1, 'b1': b1, 'W2': W2, 'b2': b2, 'A1': A1, 'B1': B1, 'A2': A2, 'B2': B2}
    _L0_ffn_in = _L0_ffn_setup()

    def _L1_attn_setup():
        import jax, jax.numpy as jnp
        import numpy as np
        BLOCK = 32
        NUM_HEADS = 16
        HEAD_DIM = 128
        FP4_GRID = jnp.array([0.0, 0.5, 1.0, 1.5, 2.0, 3.0, 4.0, 6.0], dtype=jnp.float32)

        def quantize_to_mxfp4(w, block_size=BLOCK):
            D, F = w.shape
            blocks = w.reshape(D // block_size, block_size, F)
            amax = jnp.max(jnp.abs(blocks), axis=1)
            e = jnp.floor(jnp.log2(jnp.maximum(amax, 1e-12) / 6.0))
            scale = jnp.exp2(e)
            v = blocks / scale[:, None, :]
            idx = jnp.argmin(jnp.abs(jnp.abs(v)[..., None] - FP4_GRID), axis=-1)
            codes = jnp.sign(v) * FP4_GRID[idx]
            return (codes.reshape(D, F).astype(jnp.float32), scale.astype(jnp.float32))

        def _mxfp4_matmul(x, codes, scales, block_size=BLOCK):
            w = codes * jnp.repeat(scales, block_size, axis=0)
            return x @ w
        key = jax.random.key(seed)
        ks = jax.random.split(key, 9)
        B, S, D = (2, 256, 256)
        feat = NUM_HEADS * HEAD_DIM
        x = jax.random.normal(ks[0], (B, S, D), dtype=jnp.float32)

        def make_w(k, din, dout):
            w = jax.random.normal(k, (din, dout), dtype=jnp.float32) * (1.0 / np.sqrt(din))
            return quantize_to_mxfp4(w, BLOCK)
        wq_codes, wq_scales = make_w(ks[1], D, feat)
        wk_codes, wk_scales = make_w(ks[2], D, feat)
        wv_codes, wv_scales = make_w(ks[3], D, feat)
        wo_codes, wo_scales = make_w(ks[4], feat, D)
        bq = jnp.zeros((feat,), jnp.float32)
        bk = jnp.zeros((feat,), jnp.float32)
        bv = jnp.zeros((feat,), jnp.float32)
        bo = jnp.zeros((D,), jnp.float32)
        return {'x': x, 'wq_codes': wq_codes, 'wq_scales': wq_scales, 'bq': bq, 'wk_codes': wk_codes, 'wk_scales': wk_scales, 'bk': bk, 'wv_codes': wv_codes, 'wv_scales': wv_scales, 'bv': bv, 'wo_codes': wo_codes, 'wo_scales': wo_scales, 'bo': bo}
    _L1_attn_in = _L1_attn_setup()

    def _L1_ffn_setup():
        import jax, jax.numpy as jnp
        import numpy as np
        E, H, I = (8, 256, 512)
        TOP_K = 1
        B, S = (1, 256)
        key = jax.random.key(seed)
        ks = jax.random.split(key, 7)
        std = 0.02
        return {'hidden_states': jax.random.normal(ks[0], (B, S, H), dtype=jnp.float32), 'router_w': jax.random.normal(ks[1], (E, H), dtype=jnp.float32) * std, 'gate_up_proj': jax.random.normal(ks[2], (E, H, 2 * I), dtype=jnp.float32) * std, 'down_proj': jax.random.normal(ks[3], (E, I, H), dtype=jnp.float32) * std, 'shared_gate_w': jax.random.normal(ks[4], (H, I), dtype=jnp.float32) * std, 'shared_up_w': jax.random.normal(ks[5], (H, I), dtype=jnp.float32) * std, 'shared_down_w': jax.random.normal(ks[6], (I, H), dtype=jnp.float32) * std}
    _L1_ffn_in = _L1_ffn_setup()
    _d = {'L0_attn_x': _L0_attn_in['x'], 'L0_attn_mu_x': _L0_attn_in['mu_x'], 'L0_attn_Wx1': _L0_attn_in['Wx1'], 'L0_attn_Wx2': _L0_attn_in['Wx2'], 'L0_attn_x_bias': _L0_attn_in['x_bias'], 'L0_attn_Wr': _L0_attn_in['Wr'], 'L0_attn_Wk': _L0_attn_in['Wk'], 'L0_attn_Wv': _L0_attn_in['Wv'], 'L0_attn_Ww_a': _L0_attn_in['Ww_a'], 'L0_attn_Ww_b': _L0_attn_in['Ww_b'], 'L0_attn_bw': _L0_attn_in['bw'], 'L0_attn_Wg_a': _L0_attn_in['Wg_a'], 'L0_attn_Wg_b': _L0_attn_in['Wg_b'], 'L0_attn_bg': _L0_attn_in['bg'], 'L0_attn_bonus': _L0_attn_in['bonus'], 'L0_attn_ln_w': _L0_attn_in['ln_w'], 'L0_attn_ln_b': _L0_attn_in['ln_b'], 'L0_attn_Wo': _L0_attn_in['Wo'], 'L0_ffn_Wr': _L0_ffn_in['Wr'], 'L0_ffn_br': _L0_ffn_in['br'], 'L0_ffn_W1': _L0_ffn_in['W1'], 'L0_ffn_b1': _L0_ffn_in['b1'], 'L0_ffn_W2': _L0_ffn_in['W2'], 'L0_ffn_b2': _L0_ffn_in['b2'], 'L0_ffn_A1': _L0_ffn_in['A1'], 'L0_ffn_B1': _L0_ffn_in['B1'], 'L0_ffn_A2': _L0_ffn_in['A2'], 'L0_ffn_B2': _L0_ffn_in['B2'], 'L1_attn_wq_codes': _L1_attn_in['wq_codes'], 'L1_attn_wq_scales': _L1_attn_in['wq_scales'], 'L1_attn_bq': _L1_attn_in['bq'], 'L1_attn_wk_codes': _L1_attn_in['wk_codes'], 'L1_attn_wk_scales': _L1_attn_in['wk_scales'], 'L1_attn_bk': _L1_attn_in['bk'], 'L1_attn_wv_codes': _L1_attn_in['wv_codes'], 'L1_attn_wv_scales': _L1_attn_in['wv_scales'], 'L1_attn_bv': _L1_attn_in['bv'], 'L1_attn_wo_codes': _L1_attn_in['wo_codes'], 'L1_attn_wo_scales': _L1_attn_in['wo_scales'], 'L1_attn_bo': _L1_attn_in['bo'], 'L1_ffn_router_w': _L1_ffn_in['router_w'], 'L1_ffn_gate_up_proj': _L1_ffn_in['gate_up_proj'], 'L1_ffn_down_proj': _L1_ffn_in['down_proj'], 'L1_ffn_shared_gate_w': _L1_ffn_in['shared_gate_w'], 'L1_ffn_shared_up_w': _L1_ffn_in['shared_up_w'], 'L1_ffn_shared_down_w': _L1_ffn_in['shared_down_w']}
    _x0 = _d['L0_attn_x']
    _d['L0_attn_x'] = jax.random.normal(jax.random.fold_in(jax.random.key(seed), 1), (1, 2048, 256), dtype=_x0.dtype)
    del _x0
    return _d

def reference(L0_attn_x, L0_attn_mu_x, L0_attn_Wx1, L0_attn_Wx2, L0_attn_x_bias, L0_attn_Wr, L0_attn_Wk, L0_attn_Wv, L0_attn_Ww_a, L0_attn_Ww_b, L0_attn_bw, L0_attn_Wg_a, L0_attn_Wg_b, L0_attn_bg, L0_attn_bonus, L0_attn_ln_w, L0_attn_ln_b, L0_attn_Wo, L0_ffn_Wr, L0_ffn_br, L0_ffn_W1, L0_ffn_b1, L0_ffn_W2, L0_ffn_b2, L0_ffn_A1, L0_ffn_B1, L0_ffn_A2, L0_ffn_B2, L1_attn_wq_codes, L1_attn_wq_scales, L1_attn_bq, L1_attn_wk_codes, L1_attn_wk_scales, L1_attn_bk, L1_attn_wv_codes, L1_attn_wv_scales, L1_attn_bv, L1_attn_wo_codes, L1_attn_wo_scales, L1_attn_bo, L1_ffn_router_w, L1_ffn_gate_up_proj, L1_ffn_down_proj, L1_ffn_shared_gate_w, L1_ffn_shared_up_w, L1_ffn_shared_down_w):

    def _L0_attn_ref(x, mu_x, Wx1, Wx2, x_bias, Wr, Wk, Wv, Ww_a, Ww_b, bw, Wg_a, Wg_b, bg, bonus, ln_w, ln_b, Wo):
        import jax, jax.numpy as jnp
        import numpy as np
        H = 256
        NH = 16
        KD = H // 2
        VD = H // 2
        DK = KD // NH
        DV = VD // NH
        RLOW = 64
        GLOW = 64
        EPS = 1e-05
        B, T = (2, 128)
        b, t, _ = x.shape
        shifted = jnp.pad(x, ((0, 0), (1, 0), (0, 0)))[:, :t]
        delta = shifted - x
        lr = jnp.tanh(((x + delta * mu_x) @ Wx1).reshape(b, t, 5, RLOW))
        mus = jnp.einsum('btnr,hnr->btnh', lr, Wx2) + x_bias
        mr, mw, mk, mv, mg = (mus[:, :, i] for i in range(5))
        r = (x + delta * mr) @ Wr
        w = jnp.tanh((x + delta * mw) @ Ww_a) @ Ww_b + bw
        k = (x + delta * mk) @ Wk
        v = (x + delta * mv) @ Wv
        g = jnp.tanh((x + delta * mg) @ Wg_a) @ Wg_b + bg
        r = r.reshape(b, t, NH, DK)
        k = k.reshape(b, t, NH, DK)
        v = v.reshape(b, t, NH, DV)
        decay = jnp.exp(-jnp.exp(w.reshape(b, t, NH, DK)))
        xs = (jnp.moveaxis(r, 1, 0), jnp.moveaxis(k, 1, 0), jnp.moveaxis(v, 1, 0), jnp.moveaxis(decay, 1, 0))
        S0 = jnp.zeros((b, NH, DK, DV), x.dtype)

        def step(S, inp):
            rt, kt, vt, dt = inp
            kv = kt[..., :, None] * vt[..., None, :]
            ot = jnp.einsum('bhk,bhkv->bhv', rt, S + bonus[None, :, :, None] * kv)
            S = dt[..., None] * S + kv
            return (S, ot)
        _, o = jax.lax.scan(step, S0, xs)
        o = jnp.moveaxis(o, 0, 1)
        g = g.reshape(b, t, NH, DV)
        mean = o.mean(-1, keepdims=True)
        var = o.var(-1, keepdims=True)
        on = (o - mean) * jax.lax.rsqrt(var + EPS) * ln_w + ln_b
        o = on * g * jax.nn.sigmoid(g)
        return o.reshape(b, t, VD) @ Wo

    def _L0_ffn_ref(hidden_states, Wr, br, W1, b1, W2, b2, A1, B1, A2, B2):
        import jax, jax.numpy as jnp
        import numpy as np
        E = 8
        K = 2
        D = 256
        F = 1024
        R = 16
        SCALING = 32.0 / 16.0

        def gelu_new(x):
            return jax.nn.gelu(x, approximate=True)
        B, S, Dm = hidden_states.shape
        x = hidden_states.reshape(-1, Dm)
        probs = jax.nn.softmax(x @ Wr + br, axis=-1)
        w, idx = jax.lax.top_k(probs, K)
        combine = jnp.einsum('tk,tke->te', w, jax.nn.one_hot(idx, E, dtype=x.dtype))
        base_h1 = x @ W1 + b1
        t1 = jnp.einsum('td,erd->ter', x, A1)
        l1 = jnp.einsum('ter,efr->tef', t1, B1) * SCALING
        a = gelu_new(base_h1[:, None, :] + l1)
        ca = a * combine[:, :, None]
        mix = ca.sum(axis=1)
        t2 = jnp.einsum('tef,erf->ter', ca, A2)
        l2 = jnp.einsum('ter,edr->td', t2, B2) * SCALING
        out = mix @ W2 + combine.sum(-1, keepdims=True) * b2 + l2
        return out.reshape(B, S, Dm)

    def _L1_attn_ref(x, wq_codes, wq_scales, bq, wk_codes, wk_scales, bk, wv_codes, wv_scales, bv, wo_codes, wo_scales, bo):
        import jax, jax.numpy as jnp
        import numpy as np
        BLOCK = 32
        NUM_HEADS = 16
        HEAD_DIM = 128
        FP4_GRID = jnp.array([0.0, 0.5, 1.0, 1.5, 2.0, 3.0, 4.0, 6.0], dtype=jnp.float32)

        def quantize_to_mxfp4(w, block_size=BLOCK):
            D, F = w.shape
            blocks = w.reshape(D // block_size, block_size, F)
            amax = jnp.max(jnp.abs(blocks), axis=1)
            e = jnp.floor(jnp.log2(jnp.maximum(amax, 1e-12) / 6.0))
            scale = jnp.exp2(e)
            v = blocks / scale[:, None, :]
            idx = jnp.argmin(jnp.abs(jnp.abs(v)[..., None] - FP4_GRID), axis=-1)
            codes = jnp.sign(v) * FP4_GRID[idx]
            return (codes.reshape(D, F).astype(jnp.float32), scale.astype(jnp.float32))

        def _mxfp4_matmul(x, codes, scales, block_size=BLOCK):
            w = codes * jnp.repeat(scales, block_size, axis=0)
            return x @ w
        B, S, D = x.shape
        q = _mxfp4_matmul(x, wq_codes, wq_scales) + bq
        k = _mxfp4_matmul(x, wk_codes, wk_scales) + bk
        v = _mxfp4_matmul(x, wv_codes, wv_scales) + bv
        q = q.reshape(B, S, NUM_HEADS, HEAD_DIM)
        k = k.reshape(B, S, NUM_HEADS, HEAD_DIM)
        v = v.reshape(B, S, NUM_HEADS, HEAD_DIM)
        scores = jnp.einsum('bqhd,bkhd->bhqk', q, k) / jnp.sqrt(jnp.float32(HEAD_DIM))
        attn = jax.nn.softmax(scores, axis=-1)
        out = jnp.einsum('bhqk,bkhd->bqhd', attn, v).reshape(B, S, NUM_HEADS * HEAD_DIM)
        return _mxfp4_matmul(out, wo_codes, wo_scales) + bo

    def _L1_ffn_ref(hidden_states, router_w, gate_up_proj, down_proj, shared_gate_w, shared_up_w, shared_down_w):
        import jax, jax.numpy as jnp
        import numpy as np
        E, H, I = (8, 256, 512)
        TOP_K = 1
        B, S = (1, 256)
        orig_shape = hidden_states.shape
        x = hidden_states.reshape(-1, H)
        T = x.shape[0]
        logits = x @ router_w.T
        top_vals, top_idx = jax.lax.top_k(logits, TOP_K)
        scores = jnp.full_like(logits, -jnp.inf)
        scores = scores.at[jnp.arange(T)[:, None], top_idx].set(top_vals)
        scores = jax.nn.sigmoid(scores.astype(jnp.float32)).astype(logits.dtype)
        xr = x[None, :, :] * scores.T[:, :, None]
        gate_up = jnp.einsum('eth,ehf->etf', xr, gate_up_proj)
        gate, up = jnp.split(gate_up, 2, axis=-1)
        routed = jnp.einsum('etf,efh->eth', up * jax.nn.silu(gate), down_proj)
        routed_sum = routed.sum(axis=0)
        shared = jax.nn.silu(x @ shared_gate_w) * (x @ shared_up_w) @ shared_down_w
        return (shared + routed_sum).reshape(orig_shape)
    x = L0_attn_x
    x = x + _L0_attn_ref(_layernorm(x, axis=-1), L0_attn_mu_x, L0_attn_Wx1, L0_attn_Wx2, L0_attn_x_bias, L0_attn_Wr, L0_attn_Wk, L0_attn_Wv, L0_attn_Ww_a, L0_attn_Ww_b, L0_attn_bw, L0_attn_Wg_a, L0_attn_Wg_b, L0_attn_bg, L0_attn_bonus, L0_attn_ln_w, L0_attn_ln_b, L0_attn_Wo)
    x = x + _L0_ffn_ref(_layernorm(x, axis=-1), L0_ffn_Wr, L0_ffn_br, L0_ffn_W1, L0_ffn_b1, L0_ffn_W2, L0_ffn_b2, L0_ffn_A1, L0_ffn_B1, L0_ffn_A2, L0_ffn_B2)
    x = x + _L1_attn_ref(_layernorm(x, axis=-1), L1_attn_wq_codes, L1_attn_wq_scales, L1_attn_bq, L1_attn_wk_codes, L1_attn_wk_scales, L1_attn_bk, L1_attn_wv_codes, L1_attn_wv_scales, L1_attn_bv, L1_attn_wo_codes, L1_attn_wo_scales, L1_attn_bo)
    x = x + _L1_ffn_ref(_layernorm(x, axis=-1), L1_ffn_router_w, L1_ffn_gate_up_proj, L1_ffn_down_proj, L1_ffn_shared_gate_w, L1_ffn_shared_up_w, L1_ffn_shared_down_w)
    return x

_drawn_inputs = setup_inputs


def setup_inputs(seed=0):
    import zlib

    import numpy as np

    out = dict(_drawn_inputs(seed))
    spreads = {'L0_attn_ln_w': (1.0, 0.6),
     'L0_attn_ln_b': (0.0, 0.8),
     'L0_ffn_br': (0.0, 0.8),
     'L0_ffn_b1': (0.0, 0.496),
     'L0_ffn_b2': (0.0, 0.1),
     'L1_attn_bq': (0.0, 0.8),
     'L1_attn_bk': (0.0, 2.0),
     'L1_attn_bv': (0.0, 0.1),
     'L1_attn_bo': (0.0, 0.1)}
    factors = {'L0_attn_mu_x': 8.0,
     'L0_attn_Wx1': 8.0,
     'L0_attn_Wx2': 8.0,
     'L0_attn_x_bias': 8.0,
     'L0_attn_Wr': 8.0,
     'L0_attn_Wk': 8.0,
     'L0_attn_Wv': 8.0,
     'L0_attn_Ww_a': 8.0,
     'L0_attn_Ww_b': 8.0,
     'L0_attn_bw': 8.0,
     'L0_attn_Wg_a': 8.0,
     'L0_attn_Wg_b': 8.0,
     'L0_attn_bg': 8.0,
     'L0_attn_bonus': 8.0,
     'L0_attn_Wo': 8.0,
     'L0_ffn_Wr': 7.052,
     'L0_ffn_A1': 8.0,
     'L0_ffn_B1': 8.0,
     'L0_ffn_A2': 8.0,
     'L0_ffn_B2': 8.0,
     'L1_attn_wq_scales': 5.12,
     'L1_attn_wk_scales': 5.137,
     'L1_attn_wv_scales': 4.271,
     'L1_ffn_router_w': 6.794,
     'L1_ffn_gate_up_proj': 6.244,
     'L1_ffn_down_proj': 6.233,
     'L1_ffn_shared_gate_w': 8.0,
     'L1_ffn_shared_up_w': 8.0,
     'L1_ffn_shared_down_w': 8.0}
    for name, (base, spread) in spreads.items():
        noise = np.random.default_rng([zlib.crc32(name.encode()), seed]).standard_normal(out[name].shape)
        drawn = base * np.exp(spread * noise) if base else spread * noise
        out[name] = jnp.asarray(drawn.astype(out[name].dtype))
    for name, factor in factors.items():
        out[name] = (out[name] * factor).astype(out[name].dtype)
    return out
```

```python
import concourse.bass as bass
from concourse import mybir
from contextlib import ExitStack

F32 = mybir.dt.float32
F32R = mybir.dt.float32r
ALU = mybir.AluOpType
ACT = mybir.ActivationFunctionType
AX = mybir.AxisListType

P = 128
T = 2048
D = 256
NT = T // P
NC = D // P
BT = 512
NB = T // BT
TPB = BT // P
EPS = 1e-5


class Steps:

    def __init__(self, sem):
        self.sem, self.n = sem, 0

    def add(self, instruction, by=1):
        instruction.then_inc(self.sem, by)
        self.n += by
        return self.n


def layer_norm_tokens(nc, semaphore, alloc, tag, x_tok, ident, x_norm, psum_t, emit,
                      loads=(), loaded=None):
    stats = alloc(f"{tag}_stats", [P, NT, 6], F32)
    mean_var = alloc(f"{tag}_mean_var", [P, NT, 2], F32)
    std = alloc(f"{tag}_std", [P, NT], F32)
    rstd = alloc(f"{tag}_rstd", [P, NT], F32)
    stats_ready = semaphore(f"{tag}_stats_ready")
    moments_ready = semaphore(f"{tag}_moments_ready")
    var_eps_ready = semaphore(f"{tag}_var_eps_ready")
    std_ready = semaphore(f"{tag}_std_ready")
    rstd_ready = semaphore(f"{tag}_rstd_ready")
    norm_ready = semaphore(f"{tag}_norm_ready")
    transposed = semaphore(f"{tag}_transposed")

    with nc.Block() as block:
        @block.sync
        def _(sp):
            for dst, src in loads:
                sp.dma_start(dst, src).then_inc(loaded, 16)
            if loads:
                sp.wait_ge(loaded, 16 * len(loads))

        @block.vector
        def _(dve):
            with dve.Fori(0, NT) as i:
                nc.vector.bn_stats(stats[:, i, :], x_tok[:, i, :]).then_inc(stats_ready, 1)
            dve.wait_ge(stats_ready, NT)
            for i in range(NT):
                nc.vector.bn_aggr(mean_var[:, i, :], stats[:, i, :]).then_inc(moments_ready, 1)
            dve.wait_ge(moments_ready, NT)
            nc.vector.tensor_scalar(std[:], mean_var[:, :, 1], EPS, None, ALU.add).then_inc(var_eps_ready, 1)
            dve.wait_ge(std_ready, 1)
            nc.vector.reciprocal(rstd[:], std[:]).then_inc(rstd_ready, 1)
            dve.wait_ge(rstd_ready, 1)
            with dve.Fori(0, NT) as i:
                nc.vector.tensor_scalar(x_norm[:, i, :], x_tok[:, i, :], mean_var[:, i, 0:1], rstd[:, bass.ds(i, 1)],
                                        ALU.subtract, ALU.mult).then_inc(norm_ready, 1)
            for bank in range(2 * NB):
                emit("vector", dve, bank, psum_t, transposed, TPB * (bank % NB + 1))

        @block.scalar
        def _(act):
            act.wait_ge(var_eps_ready, 1)
            nc.scalar.activation(std[:], std[:], ACT.Sqrt).then_inc(std_ready, 1)
            for bank in range(2 * NB):
                emit("scalar", act, bank, psum_t, transposed, TPB * (bank % NB + 1))

        @block.tensor
        def _(pe):
            for i in range(NT):
                pe.wait_ge(norm_ready, i + 1)
                nc.tensor.transpose(psum_t[:, 0, bass.ts(i, P)], x_norm[:, i, 0:P], ident[:])
                nc.tensor.transpose(psum_t[:, 1, bass.ts(i, P)], x_norm[:, i, P:D], ident[:]).then_inc(transposed, 1)


def time_mix(nc, w, x_tok, ident):
    with ExitStack() as ctx:
        def alloc(name, shape, dt):
            return ctx.enter_context(nc.sbuf_tensor(name, shape, dt))

        def semaphore(name):
            return ctx.enter_context(nc.semaphore(name))

        NM = 5
        RL = 64
        H, K, V = 16, 8, 8
        OUT_W = [P, RL, P, P, RL]
        shifted = alloc("tm_x_shifted", [P, NC, T + 1], F32)
        wx1 = alloc("tm_wx1", [P, NC, NM * RL], F32)
        wx2 = alloc("tm_wx2", [P, 3, D], F32)
        proj = alloc("tm_proj", [P, NC, sum(OUT_W)], F32)
        wwb = alloc("tm_wwb", [RL, P], F32)
        wgb = alloc("tm_wgb", [RL, P], F32)
        wo = alloc("tm_wo", [P, D], F32)
        cols = alloc("tm_cols", [P, 17], F32)
        spread = alloc("tm_spread", [P, V, P], F32)
        gather = alloc("tm_gather", [P, V, P], F32)
        heads = alloc("tm_heads", [P, P], F32)
        rT = alloc("tm_r", [P, T], F32)
        kT = alloc("tm_k", [P, T], F32)
        vT = alloc("tm_v", [P, T], F32)
        decay = alloc("tm_decay", [P, T], F32)
        gT = alloc("tm_g", [P, T], F32)
        oT = alloc("tm_o", [P, T], F32)
        MU, XB, BW, BG, BONUS, LNW, LNB = 0, 2, 12, 13, 14, 15, 16

        weights_loaded = semaphore("tm_weights_loaded")
        N_LOADS = 15
        with ExitStack() as inner:
            x_norm = inner.enter_context(nc.sbuf_tensor("tm_x_norm", [P, NT, D], F32))
            psum_t = inner.enter_context(nc.psum_tensor("tm_psum_t", [P, NC, T], F32))
            zeroed = semaphore("tm_zeroed")
            copied = semaphore("tm_copied")

            with nc.Block() as block:
                @block.sync
                def _(sp):
                    for dst, src in (
                        (wx1[:], w["L0_attn_Wx1"].rearrange("(c p) n -> p c n", p=P)),
                        (wx2[:, 0:2, :], w["Wx2T"][0:2 * P].rearrange("(c p) n -> p c n", p=P)),
                        (wx2[0:RL, 2, :], w["Wx2T"][2 * P:NM * RL]),
                        (proj[:], w["tm_proj"].rearrange("(c p) n -> p c n", p=P)),
                        (wwb[:], w["L0_attn_Ww_b"]),
                        (wgb[:], w["L0_attn_Wg_b"]),
                        (wo[:], w["L0_attn_Wo"]),
                        (cols[:], w["tm_cols"]),
                        (spread[:], w["c_spread"]),
                        (gather[:], w["c_gather"]),
                        (heads[:], w["c_heads"]),
                    ):
                        sp.dma_start(dst, src).then_inc(weights_loaded, 16)
                    sp.wait_ge(weights_loaded, 16 * 11)

                @block.vector
                def _(dve):
                    nc.vector.memset(shifted[:, :, 0:1], 0.0).then_inc(zeroed, 1)

            def emit(name, eng, bank, psum_t, transposed, value):
                c, b = divmod(bank, NB)
                if (bank % 2 == 0) != (name == "vector"):
                    return
                eng.wait_ge(transposed, value)
                dst, src = shifted[:, c, 1 + b * BT:1 + (b + 1) * BT], psum_t[:, c, bass.ts(b, BT)]
                if name == "vector":
                    nc.vector.tensor_copy(dst, src).then_inc(copied, 1)
                else:
                    nc.scalar.activation(dst, src, ACT.Copy).then_inc(copied, 1)

            layer_norm_tokens(nc, semaphore, lambda n, s, d: inner.enter_context(nc.sbuf_tensor(n, s, d)), "tm_ln", x_tok, ident, x_norm, psum_t, emit)

        with ExitStack() as inner:
            def sb(name, shape):
                return inner.enter_context(nc.sbuf_tensor(name, shape, F32))

            def ps(name, shape):
                return inner.enter_context(nc.psum_tensor(name, shape, F32))

            delta = sb("tm_delta", [P, NC, BT])
            x_mu = sb("tm_x_mu", [P, NC, BT])
            lr = sb("tm_lr", [P, 3, BT])
            mixed = sb("tm_mixed", [P, 2, NC, BT])
            low = sb("tm_low", [RL, 2, BT])
            exp_w = sb("tm_exp_w", [P, BT])
            psum_lr = ps("tm_psum_lr", [P, 3, BT])
            psum_mu = ps("tm_psum_mu", [P, NC, BT])
            psum_proj = ps("tm_psum_proj", [P, 2, BT])
            psum_up = ps("tm_psum_up", [P, BT])
            delta_ready = semaphore("tm_delta_ready")
            x_mu_ready = semaphore("tm_x_mu_ready")
            lr_psum_ready = semaphore("tm_lr_psum_ready")
            lr_ready = semaphore("tm_lr_ready")
            mu_psum_ready = semaphore("tm_mu_psum_ready")
            moved_ready = semaphore("tm_moved_ready")
            mixed_ready = semaphore("tm_mixed_ready")
            proj_psum_ready = semaphore("tm_proj_psum_ready")
            proj_out = semaphore("tm_proj_out")
            up_psum_ready = semaphore("tm_up_psum_ready")
            exp_w_ready = semaphore("tm_exp_w_ready")
            up_out = semaphore("tm_up_out")

            with nc.Block() as block:
                @block.vector
                def _(dve):
                    with dve.Fori(0, NB) as b:
                        now = shifted[:, :, bass.ds(b * BT + 1, BT)]
                        before = shifted[:, :, bass.ds(b * BT, BT)]
                        nc.vector.tensor_tensor(delta[:], before, now, ALU.subtract).then_inc(delta_ready, 1)
                        dve.wait_ge(delta_ready, b + 1)
                        for c in range(NC):
                            nc.vector.scalar_tensor_tensor(
                                x_mu[:, c, :], delta[:, c, :], cols[:, MU + c:MU + c + 1],
                                shifted[:, c, bass.ds(b * BT + 1, BT)], ALU.mult, ALU.add).then_inc(x_mu_ready, 1)
                        for n in range(NM):
                            for c in range(NC):
                                col = XB + 2 * n + c
                                dve.wait_ge(mu_psum_ready, b * NM * NC + n * NC + c + 1)
                                if n >= 2:
                                    dve.wait_ge(proj_psum_ready, b * NM + n - 1)
                                nc.vector.scalar_tensor_tensor(
                                    mixed[:, n % 2, c, :], psum_mu[:, c, :], cols[:, col:col + 1], delta[:, c, :],
                                    ALU.add, ALU.mult).then_inc(moved_ready, 1)
                                dve.wait_ge(moved_ready, b * NM * NC + n * NC + c + 1)
                                nc.vector.tensor_tensor(mixed[:, n % 2, c, :], mixed[:, n % 2, c, :],
                                                        shifted[:, c, bass.ds(b * BT + 1, BT)],
                                                        ALU.add).then_inc(mixed_ready, 1)
                        dve.wait_ge(proj_psum_ready, b * NM + NM)

                @block.scalar
                def _(act):
                    with act.Fori(0, NB) as b:
                        tok = bass.ts(b, BT)
                        act.wait_ge(lr_psum_ready, b + 1)
                        nc.scalar.activation(lr[:, 0:2, :], psum_lr[:, 0:2, :], ACT.Tanh).then_inc(lr_ready, 1)
                        nc.scalar.activation(lr[0:RL, 2, :], psum_lr[0:RL, 2, :], ACT.Tanh).then_inc(lr_ready, 1)
                        for n in range(NM):
                            act.wait_ge(proj_psum_ready, b * NM + n + 1)
                            src = psum_proj[0:OUT_W[n], n % 2, :]
                            if OUT_W[n] == RL:
                                nc.scalar.activation(low[:, n // 4, :], src, ACT.Tanh).then_inc(proj_out, 1)
                            else:
                                dst = {0: rT, 2: kT, 3: vT}[n]
                                nc.scalar.activation(dst[:, tok], src, ACT.Copy).then_inc(proj_out, 1)
                            if n == 1:
                                act.wait_ge(up_psum_ready, 2 * b + 1)
                                nc.scalar.activation(exp_w[:], psum_up[:], ACT.Exp,
                                                     bias=cols[:, BW:BW + 1]).then_inc(exp_w_ready, 1)
                                act.wait_ge(exp_w_ready, b + 1)
                                nc.scalar.activation(decay[:, tok], exp_w[:], ACT.Exp, scale=-1.0).then_inc(up_out, 1)
                            if n == 4:
                                act.wait_ge(up_psum_ready, 2 * b + 2)
                                nc.scalar.activation(gT[:, tok], psum_up[:], ACT.Identity,
                                                     bias=cols[:, BG:BG + 1]).then_inc(up_out, 1)

                @block.tensor
                def _(pe):
                    with pe.Fori(0, NB) as b:
                        for c in range(NC):
                            pe.wait_ge(x_mu_ready, b * NC + c + 1)
                            for m, width in enumerate((P, P, RL)):
                                last = nc.tensor.matmul(psum_lr[0:width, m, :], wx1[:, c, m * P:m * P + width],
                                                        x_mu[:, c, :], start=(c == 0), stop=(c == NC - 1))
                        last.then_inc(lr_psum_ready, 1)
                        pe.wait_ge(lr_ready, 2 * b + 2)
                        off = 0

                        def mixing(n):
                            chunk, row = divmod(n * RL, P)
                            for c in range(NC):
                                if n >= 1:
                                    pe.wait_ge(moved_ready, b * NM * NC + (n - 1) * NC + c + 1)
                                nc.tensor.matmul(psum_mu[:, c, :], wx2[row:row + RL, chunk, bass.ts(c, P)],
                                                 lr[row:row + RL, chunk, :], start=True, stop=True
                                                 ).then_inc(mu_psum_ready, 1)

                        mixing(0)
                        for n in range(NM):
                            if n + 1 < NM:
                                mixing(n + 1)
                            if n >= 2:
                                pe.wait_ge(proj_out, b * NM + n - 1)
                            for c in range(NC):
                                pe.wait_ge(mixed_ready, b * NM * NC + n * NC + c + 1)
                                last = nc.tensor.matmul(psum_proj[0:OUT_W[n], n % 2, :], proj[:, c, off:off + OUT_W[n]],
                                                        mixed[:, n % 2, c, :], start=(c == 0), stop=(c == NC - 1))
                            last.then_inc(proj_psum_ready, 1)
                            off += OUT_W[n]
                            if n in (1, 4):
                                pe.wait_ge(proj_out, b * NM + n + 1)
                                if n == 4:
                                    pe.wait_ge(exp_w_ready, b + 1)
                                nc.tensor.matmul(psum_up[:], (wwb, wgb)[n // 4][:], low[:, n // 4, :],
                                                 start=True, stop=True).then_inc(up_psum_ready, 1)
                        pe.wait_ge(proj_out, b * NM + NM)
                        pe.wait_ge(up_out, 2 * b + 2)

        with ExitStack() as inner:
            def sb(name, shape):
                return inner.enter_context(nc.sbuf_tensor(name, shape, F32))

            def ps(name, shape):
                return inner.enter_context(nc.psum_tensor(name, shape, F32))

            kv = sb("tm_kv", [P, 2, T])
            state = sb("tm_state", [P, 2, T + 1])
            read = sb("tm_read", [P, 2, T])
            rk = sb("tm_rk", [P, T])
            own = sb("tm_own", [P, T])
            psum_o = ps("tm_psum_o", [P, T])
            psum_v = ps("tm_psum_v", [P, 2, BT])
            psum_rk = ps("tm_psum_rk", [P, 2, BT])
            rk_ready = semaphore("tm_rk_ready")
            v_spread = semaphore("tm_v_spread")
            kv_ready = semaphore("tm_kv_ready")
            state_zero = semaphore("tm_state_zero")
            scanned = semaphore("tm_scanned")
            read_ready = semaphore("tm_read_ready")
            o_summed = semaphore("tm_o_summed")
            rk_summed = semaphore("tm_rk_summed")
            own_ready = semaphore("tm_own_ready")
            o_ready = semaphore("tm_o_ready")

            with nc.Block() as block:
                @block.tensor
                def _(pe):
                    def spread_v(v):
                        for b in range(NB):
                            n = v * NB + b
                            if b >= 2:
                                pe.wait_ge(kv_ready, n - 1)
                            elif not isinstance(v, int) or v > 0:
                                pe.wait_ge(kv_ready, n - 1)
                            nc.tensor.matmul(psum_v[:, b % 2, :], spread[:, v, :], vT[:, bass.ts(b, BT)],
                                             start=True, stop=True).then_inc(v_spread, 1)

                    def sum_o(v, first, last):
                        pe.wait_ge(read_ready, v + 1)
                        for b in range(NB):
                            mm = nc.tensor.matmul(psum_o[:, bass.ts(b, BT)], gather[:, v, :],
                                                  read[:, v % 2, bass.ts(b, BT)], start=first, stop=last)
                        mm.then_inc(o_summed, 1)

                    spread_v(0)
                    for v in range(1, V):
                        spread_v(v)
                        sum_o(v - 1, v == 1, False)
                    pe.wait_ge(rk_ready, 1)
                    for b in range(NB):
                        if b >= 2:
                            pe.wait_ge(own_ready, b - 1)
                        nc.tensor.matmul(psum_rk[:, b % 2, :], heads[:], rk[:, bass.ts(b, BT)],
                                         start=True, stop=True).then_inc(rk_summed, 1)
                    sum_o(V - 1, False, True)

                @block.gpsimd
                def _(pool):
                    for v in range(V):
                        pool.wait_ge(scanned, v + 1)
                        if v >= 2:
                            pool.wait_ge(o_summed, v - 1)
                        nc.gpsimd.tensor_tensor(read[:, v % 2, :], rT[:], state[:, v % 2, 0:T],
                                                ALU.mult).then_inc(read_ready, 1)

                @block.vector
                def _(dve):
                    for j in range(2):
                        nc.vector.memset(state[:, j, 0:1], 0.0).then_inc(state_zero, 1)
                    nc.vector.scalar_tensor_tensor(rk[:], rT[:], cols[:, BONUS:BONUS + 1], kT[:],
                                                   ALU.mult, ALU.mult).then_inc(rk_ready, 1)
                    dve.wait_ge(state_zero, 2)
                    for v in range(V):
                        for b in range(NB):
                            dve.wait_ge(v_spread, v * NB + b + 1)
                            if v >= 2:
                                dve.wait_ge(scanned, v - 1)
                            nc.vector.tensor_tensor(kv[:, v % 2, bass.ts(b, BT)], psum_v[:, b % 2, :],
                                                    kT[:, bass.ts(b, BT)], ALU.mult).then_inc(kv_ready, 1)
                        dve.wait_ge(kv_ready, (v + 1) * NB)
                        if v >= 2:
                            dve.wait_ge(read_ready, v - 1)
                        nc.vector.tensor_tensor_scan(state[:, v % 2, 1:T + 1], decay[:], kv[:, v % 2, :], 0.0,
                                                     ALU.mult, ALU.add).then_inc(scanned, 1)
                    for b in range(NB):
                        dve.wait_ge(rk_summed, b + 1)
                        nc.vector.tensor_tensor(own[:, bass.ts(b, BT)], psum_rk[:, b % 2, :], vT[:, bass.ts(b, BT)],
                                                ALU.mult).then_inc(own_ready, 1)
                    dve.wait_ge(own_ready, NB)
                    dve.wait_ge(o_summed, V)
                    nc.vector.tensor_tensor(oT[:], psum_o[:], own[:], ALU.add).then_inc(o_ready, 1)

        with ExitStack() as inner:
            def sb(name, shape):
                return inner.enter_context(nc.sbuf_tensor(name, shape, F32))

            def ps(name, shape):
                return inner.enter_context(nc.psum_tensor(name, shape, F32))

            centred = sb("tm_centred", [P, T])
            square = sb("tm_square", [P, T])
            std = sb("tm_gn_std", [P, T])
            sig = sb("tm_sig", [P, T])
            gate = sb("tm_gate", [P, T])
            psum_s = ps("tm_psum_s", [P, NB, BT])
            psum_x = ps("tm_psum_x", [P, 4, BT])
            sums_ready = semaphore("tm_sums_ready")
            centred_ready = semaphore("tm_centred_ready")
            square_ready = semaphore("tm_square_ready")
            squares_summed = semaphore("tm_squares_summed")
            var_ready = semaphore("tm_var_ready")
            std_ready = semaphore("tm_gn_std_ready")
            sig_ready = semaphore("tm_sig_ready")
            gate_ready = semaphore("tm_gate_ready")
            norm_steps = semaphore("tm_norm_steps")
            z_ready = semaphore("tm_z_ready")
            wo_done = semaphore("tm_wo_done")
            added = semaphore("tm_added")

            with nc.Block() as block:
                @block.tensor
                def _(pe):
                    for b in range(NB):
                        nc.tensor.matmul(psum_s[:, b, :], heads[:], oT[:, bass.ts(b, BT)],
                                         start=True, stop=True).then_inc(sums_ready, 1)
                    for b in range(NB):
                        pe.wait_ge(centred_ready, b + 1)
                        pe.wait_ge(square_ready, b + 1)
                        nc.tensor.matmul(psum_s[:, b, :], heads[:], square[:, bass.ts(b, BT)],
                                         start=True, stop=True).then_inc(squares_summed, 1)
                    for g in range(NT // 4):
                        pe.wait_ge(z_ready, g + 1)
                        for j in range(4):
                            nc.tensor.matmul(psum_x[:, j, 0:D], oT[:, bass.ds(g * BT + j * P, P)], wo[:],
                                             start=True, stop=True).then_inc(wo_done, 1)
                        pe.wait_ge(added, g * 4 + 4)

                @block.scalar
                def _(act):
                    nc.scalar.activation(sig[:], gT[:], ACT.Sigmoid).then_inc(sig_ready, 1)
                    for b in range(NB):
                        act.wait_ge(centred_ready, b + 1)
                        nc.scalar.activation(square[:, bass.ts(b, BT)], centred[:, bass.ts(b, BT)],
                                             ACT.Square).then_inc(square_ready, 1)
                    for b in range(NB):
                        act.wait_ge(var_ready, b + 1)
                        nc.scalar.activation(std[:, bass.ts(b, BT)], std[:, bass.ts(b, BT)],
                                             ACT.Sqrt).then_inc(std_ready, 1)

                @block.gpsimd
                def _(pool):
                    pool.wait_ge(sig_ready, 1)
                    nc.gpsimd.tensor_tensor(gate[:], sig[:], gT[:], ALU.mult).then_inc(gate_ready, 1)

                @block.vector
                def _(dve):
                    for b in range(NB):
                        dve.wait_ge(sums_ready, b + 1)
                        nc.vector.scalar_tensor_tensor(centred[:, bass.ts(b, BT)], psum_s[:, b, :], -1.0 / V,
                                                       oT[:, bass.ts(b, BT)], ALU.mult, ALU.add
                                                       ).then_inc(centred_ready, 1)
                    for b in range(NB):
                        dve.wait_ge(squares_summed, b + 1)
                        nc.vector.tensor_scalar(std[:, bass.ts(b, BT)], psum_s[:, b, :], 1.0 / V, EPS,
                                                ALU.mult, ALU.add).then_inc(var_ready, 1)
                    dve.wait_ge(gate_ready, 1)
                    for b in range(NB):
                        tok = bass.ts(b, BT)
                        dve.wait_ge(std_ready, b + 1)
                        nc.vector.reciprocal(std[:, tok], std[:, tok]).then_inc(norm_steps, 1)
                        dve.wait_ge(norm_steps, 3 * b + 1)
                        nc.vector.tensor_tensor(centred[:, tok], centred[:, tok], std[:, tok],
                                                ALU.mult).then_inc(norm_steps, 1)
                        dve.wait_ge(norm_steps, 3 * b + 2)
                        nc.vector.tensor_scalar(centred[:, tok], centred[:, tok], cols[:, LNW:LNW + 1],
                                                cols[:, LNB:LNB + 1], ALU.mult, ALU.add).then_inc(norm_steps, 1)
                        dve.wait_ge(norm_steps, 3 * b + 3)
                        nc.vector.tensor_tensor(oT[:, tok], centred[:, tok], gate[:, tok],
                                                ALU.mult).then_inc(z_ready, 1)
                    with dve.Fori(0, NT // 4) as g:
                        for j in range(4):
                            dve.wait_ge(wo_done, g * 4 + j + 1)
                            xt = x_tok[:, bass.ds(g * 4 + j, 1), :].rearrange("p a d -> p (a d)")
                            nc.vector.tensor_tensor(xt, psum_x[:, j, 0:D], xt, ALU.add).then_inc(added, 1)


def copy_banks(nc, dst, copied):
    def emit(name, eng, bank, psum_t, transposed, value):
        if (bank % 2 == 0) != (name == "vector"):
            return
        c, b = divmod(bank, NB)
        eng.wait_ge(transposed, value)
        to, of = dst[:, c, bass.ts(b, BT)], psum_t[:, c, bass.ts(b, BT)]
        if name == "vector":
            nc.vector.tensor_copy(to, of).then_inc(copied, 1)
        else:
            nc.scalar.activation(to, of, ACT.Copy).then_inc(copied, 1)
    return emit


def choose_largest(nc, dve, steps, p, order, top, hit, rank, best):
    def after(instruction):
        dve.wait_ge(steps.sem, steps.add(instruction))

    E = p.shape[-1]
    wide = [P, NT, E]
    after(nc.vector.tensor_reduce(top, p, AX.X, ALU.max))
    after(nc.vector.tensor_tensor(rank, p, top.unsqueeze(2).to_broadcast(wide), ALU.is_equal))
    after(nc.vector.tensor_tensor(rank, rank, order.unsqueeze(1).to_broadcast(wide), ALU.mult))
    after(nc.vector.tensor_reduce(best, rank, AX.X, ALU.max))
    after(nc.vector.tensor_tensor(hit, rank, best.unsqueeze(2).to_broadcast(wide), ALU.is_equal))


def lora_ffn(nc, w, x_tok, ident):
    E, R, F = 8, 16, 1024
    NF = F // P
    SCALING = 2.0
    ER = E * R
    with ExitStack() as ctx:
        def alloc(name, shape, dt=F32):
            return ctx.enter_context(nc.sbuf_tensor(name, shape, dt))

        def semaphore(name):
            return ctx.enter_context(nc.semaphore(name))

        xT = alloc("lf_xT", [P, NC, T])
        router_a1 = alloc("lf_router_a1", [P, NC, E + ER])
        w1 = alloc("lf_w1", [P, NC, F])
        b1 = alloc("lf_b1", [P, NF])
        b1t = alloc("lf_B1T", [P, F])
        w2_a2 = alloc("lf_w2_a2", [P, NF, D + ER])
        b2t = alloc("lf_B2T", [P, D])
        br = alloc("lf_br", [P, E])
        b2 = alloc("lf_b2", [P, D])
        order = alloc("lf_order", [P, E])
        low = alloc("lf_low", [P, 2, T])
        weight = alloc("lf_weight", [P, 2, NT])
        wsum = alloc("lf_wsum", [P, NT])
        mask = alloc("lf_mask", [P, 2, NT, E])
        loaded = semaphore("lf_loaded")
        copied = semaphore("lf_copied")

        with ExitStack() as inner:
            def sb(name, shape, dt=F32):
                return inner.enter_context(nc.sbuf_tensor(name, shape, dt))

            x_norm = sb("lf_x_norm", [P, NT, D])
            with inner.enter_context(ExitStack()) as ps_ctx:
                psum_t = ps_ctx.enter_context(nc.psum_tensor("lf_psum_t", [P, NC, T], F32))
                loads = (
                    (router_a1[:], w["lf_router_a1"].rearrange("(c p) n -> p c n", p=P)),
                    (w1[:], w["L0_ffn_W1"].rearrange("(c p) n -> p c n", p=P)),
                    (b1[:], w["lf_b1"]),
                    (b1t[:], w["lf_B1T"]),
                    (w2_a2[:], w["lf_w2_a2"].rearrange("(c p) n -> p c n", p=P)),
                    (b2t[:], w["lf_B2T"]),
                    (br[:], w["lf_br"][0, :].partition_broadcast(P)),
                    (b2[:], w["lf_b2"][0, :].partition_broadcast(P)),
                    (order[:], w["c_order"][0, :].partition_broadcast(P)),
                )
                layer_norm_tokens(nc, semaphore, sb, "lf_ln", x_tok, ident, x_norm, psum_t,
                                  copy_banks(nc, xT, copied), loads, loaded)

        with ExitStack() as inner:
            def sb(name, shape, dt=F32):
                return inner.enter_context(nc.sbuf_tensor(name, shape, dt))

            routed = sb("lf_routed", [P, NT, E + ER])
            prob = sb("lf_prob", [P, NT, E])
            rest = sb("lf_rest", [P, NT, E])
            hit = sb("lf_hit", [P, 2, NT, E])
            rank = sb("lf_rank", [P, NT, E])
            best = sb("lf_best", [P, NT])
            total = sb("lf_total", [P, NT])
            diff = sb("lf_diff", [P, NT, E])
            masked = sb("lf_masked", [P, 2, NT, ER])
            rt_ready = semaphore("lf_rt_ready")
            rt_copied = semaphore("lf_rt_copied")
            shifted_ready = semaphore("lf_shifted_ready")
            exp_ready = semaphore("lf_exp_ready")
            chain = semaphore("lf_chain")
            masked_ready = semaphore("lf_masked_ready")
            low_psum = semaphore("lf_low_psum")
            low_ready = semaphore("lf_low_ready")
            with ExitStack() as ps_ctx:
                psum_rt = ps_ctx.enter_context(nc.psum_tensor("lf_psum_rt", [P, 4, BT], F32))
                with nc.Block() as block:
                    @block.tensor
                    def _(pe):
                        for i in range(NT):
                            if i >= 4:
                                pe.wait_ge(rt_copied, i - 3)
                            for c in range(NC):
                                last = nc.tensor.matmul(psum_rt[:, i % 4, 0:E + ER], xT[:, c, bass.ts(i, P)],
                                                        router_a1[:, c, :], start=(c == 0), stop=(c == NC - 1))
                            last.then_inc(rt_ready, 1)

                    @block.scalar
                    def _(act):
                        for i in range(NT):
                            act.wait_ge(rt_ready, i + 1)
                            nc.scalar.activation(routed[:, i, :], psum_rt[:, i % 4, 0:E + ER],
                                                 ACT.Copy).then_inc(rt_copied, 1)
                        act.wait_ge(shifted_ready, 1)
                        nc.scalar.activation(prob[:], prob[:], ACT.Exp).then_inc(exp_ready, 1)

                    @block.vector
                    def _(dve):
                        steps = Steps(chain)

                        def after(instruction):
                            dve.wait_ge(steps.sem, steps.add(instruction))

                        wide = [P, NT, E]
                        dve.wait_ge(rt_copied, NT)
                        after(nc.vector.tensor_tensor(prob[:], routed[:, :, 0:E],
                                                      br[:].unsqueeze(1).to_broadcast(wide), ALU.add))
                        after(nc.vector.tensor_reduce(best[:], prob[:], AX.X, ALU.max))
                        nc.vector.tensor_tensor(prob[:], prob[:], best[:].unsqueeze(2).to_broadcast(wide),
                                                ALU.subtract).then_inc(shifted_ready, 1)
                        dve.wait_ge(exp_ready, 1)
                        after(nc.vector.tensor_reduce(total[:], prob[:], AX.X, ALU.add))
                        after(nc.vector.reciprocal(total[:], total[:]))
                        after(nc.vector.tensor_tensor(prob[:], prob[:], total[:].unsqueeze(2).to_broadcast(wide),
                                                      ALU.mult))
                        choose_largest(nc, dve, steps, prob[:], order[:], weight[:, 0, :], hit[:, 0], rank[:], best[:])
                        after(nc.vector.scalar_tensor_tensor(rest[:], hit[:, 0], -2.0, prob[:], ALU.mult, ALU.add))
                        choose_largest(nc, dve, steps, rest[:], order[:], weight[:, 1, :], hit[:, 1], rank[:], best[:])
                        after(nc.vector.tensor_tensor(diff[:], hit[:, 1], hit[:, 0], ALU.subtract))
                        for j in range(2):
                            after(nc.vector.scalar_tensor_tensor(
                                mask[:, j], hit[:, j], SCALING, weight[:, j, :].unsqueeze(2).to_broadcast(wide),
                                ALU.mult, ALU.mult))
                        after(nc.vector.tensor_tensor(wsum[:], weight[:, 0, :], weight[:, 1, :], ALU.add))
                        for j in range(2):
                            for i in range(NT):
                                pick = (hit[:, 0, i, :], diff[:, i, :])[j]
                                nc.vector.scalar_tensor_tensor(
                                    masked[:, j, i, :].rearrange("p (e r) -> p e r", e=E),
                                    routed[:, i, E:E + ER].rearrange("p (e r) -> p e r", e=E), SCALING,
                                    pick.unsqueeze(2).to_broadcast([P, E, R]), ALU.mult, ALU.mult
                                ).then_inc(masked_ready, 1)

            with ExitStack() as ps_ctx:
                psum_low = ps_ctx.enter_context(nc.psum_tensor("lf_psum_low", [P, 2, T], F32))
                with nc.Block() as block:
                    @block.tensor
                    def _(pe):
                        for j in range(2):
                            for i in range(NT):
                                nc.tensor.transpose(psum_low[:, j, bass.ts(i, P)], masked[:, j, i, :],
                                                    ident[:]).then_inc(low_psum, 1)

                    @block.scalar
                    def _(act):
                        for b in range(NB):
                            act.wait_ge(low_psum, (b + 1) * TPB)
                            nc.scalar.activation(low[:, 0, bass.ts(b, BT)], psum_low[:, 0, bass.ts(b, BT)],
                                                 ACT.Copy).then_inc(low_ready, 1)

                    @block.vector
                    def _(dve):
                        for b in range(NB):
                            dve.wait_ge(low_psum, NT + (b + 1) * TPB)
                            nc.vector.tensor_copy(low[:, 1, bass.ts(b, BT)],
                                                  psum_low[:, 1, bass.ts(b, BT)]).then_inc(low_ready, 1)

        with ExitStack() as inner:
            def sb(name, shape, dt=F32):
                return inner.enter_context(nc.sbuf_tensor(name, shape, dt))

            def ps(name, shape):
                return inner.enter_context(nc.psum_tensor(name, shape, F32))

            hidden = sb("lf_hidden", [P, 2, NF, BT])
            t2 = sb("lf_t2", [P, 2, 2, ER])
            t2T = sb("lf_t2T", [P, 2, P])
            psum_h = ps("lf_psum_h", [P, 4, BT])
            psum_d = ps("lf_psum_d", [P, 2, BT])
            psum_t2 = ps("lf_psum_t2", [P, BT])
            psum_l2 = ps("lf_psum_l2", [P, BT])
            h_psum = semaphore("lf_h_psum")
            h_ready = semaphore("lf_h_ready")
            d_psum = semaphore("lf_d_psum")
            x_steps = semaphore("lf_x_steps")
            t2_steps = semaphore("lf_t2_steps")
            t2_transposed = semaphore("lf_t2_transposed")
            t2T_ready = semaphore("lf_t2T_ready")
            l2_psum = semaphore("lf_l2_psum")
            biased = semaphore("lf_biased")

            with nc.Block() as block:
                @block.gpsimd
                def _(pool):
                    bias = inner.enter_context(nc.sbuf_tensor("lf_bias", [P, NT, D], F32))
                    biased_rows = semaphore("lf_biased_rows")
                    for i in range(NT):
                        nc.gpsimd.tensor_scalar(bias[:, i, :], b2[:], wsum[:, i:i + 1], None,
                                                ALU.mult).then_inc(biased_rows, 1)
                    pool.wait_ge(biased_rows, NT)
                    nc.gpsimd.tensor_tensor(x_tok[:], x_tok[:], bias[:], ALU.add).then_inc(biased, 1)

                @block.tensor
                def _(pe):
                    with pe.Fori(0, NB) as b:
                        tok = bass.ts(b, BT)

                        def first(f):
                            if f >= 4:
                                pe.wait_ge(h_ready, b * 2 * NF + 2 * (f - 4) + 2)
                            for c in range(NC):
                                nc.tensor.matmul(psum_h[:, f % 4, :], w1[:, c, bass.ts(f, P)], xT[:, c, tok],
                                                 start=(c == 0), stop=False)
                            nc.tensor.matmul(psum_h[:, f % 4, :], b1t[:, bass.ts(f, P)], low[:, 0, tok],
                                             start=False, stop=True).then_inc(h_psum, 1)

                        def second(f):
                            pe.wait_ge(h_ready, b * 2 * NF + 2 * f + 1)
                            nc.tensor.matmul(psum_h[:, f % 4, :], b1t[:, bass.ts(f, P)], low[:, 1, tok],
                                             start=False, stop=True, skip_group_check=True).then_inc(h_psum, 1)

                        first(0)
                        for f in range(NF):
                            if f + 1 < NF:
                                first(f + 1)
                            second(f)
                        pe.wait_ge(h_ready, b * 2 * NF + 2 * NF)
                        for i in range(TPB):
                            for j in range(2):
                                if i >= 1:
                                    pe.wait_ge(t2_steps, b * 3 * TPB + 3 * (i - 1) + 1 + j)
                                    pe.wait_ge(x_steps, b * 3 * TPB + 3 * (i - 1) + 1 + j)
                                for f in range(NF):
                                    last = nc.tensor.matmul(psum_d[:, j, 0:D + ER], hidden[:, j, f, bass.ts(i, P)],
                                                            w2_a2[:, f, :], start=(f == 0), stop=(f == NF - 1))
                                last.then_inc(d_psum, 1)
                            pe.wait_ge(t2_steps, b * 3 * TPB + 3 * i + 3)
                            nc.tensor.transpose(psum_t2[:, 0:P], t2[:, i % 2, 0, :], ident[:]).then_inc(t2_transposed, 1)
                            pe.wait_ge(t2T_ready, b * TPB + i + 1)
                            if i >= 1:
                                pe.wait_ge(x_steps, b * 3 * TPB + 3 * i)
                            nc.tensor.matmul(psum_l2[:, 0:D], t2T[:, i % 2, :], b2t[:],
                                             start=True, stop=True).then_inc(l2_psum, 1)
                        pe.wait_ge(x_steps, b * 3 * TPB + 3 * TPB)

                @block.scalar
                def _(act):
                    with act.Fori(0, NB) as b:
                        def gelu(n, f, j):
                            act.wait_ge(h_psum, b * 2 * NF + n + 1)
                            nc.scalar.activation(hidden[:, j, f, :], psum_h[:, f % 4, :], ACT.Gelu_apprx_tanh,
                                                 bias=b1[:, f:f + 1]).then_inc(h_ready, 1)

                        for f in range(NF):
                            gelu_first = 0 if f == 0 else 2 * f - 1
                            gelu(gelu_first, f, 0)
                            gelu(2 * f + 2 if f + 1 < NF else 2 * NF - 1, f, 1)
                        for i in range(TPB):
                            act.wait_ge(t2_transposed, b * TPB + i + 1)
                            nc.scalar.activation(t2T[:, i % 2, :], psum_t2[:, 0:P], ACT.Copy).then_inc(t2T_ready, 1)

                @block.vector
                def _(dve):
                    dve.wait_ge(biased, 1)
                    with dve.Fori(0, NB) as b:
                        for i in range(TPB):
                            row = x_tok[:, bass.ds(b * TPB + i, 1), :].rearrange("p a d -> p (a d)")
                            for j in range(2):
                                n = b * 3 * TPB + 3 * i + j
                                dve.wait_ge(d_psum, b * 2 * TPB + 2 * i + j + 1)
                                m = mask[:, j, bass.ds(b * TPB + i, 1), :].rearrange("p a e -> p (a e)")
                                nc.vector.tensor_tensor(
                                    t2[:, i % 2, j, :].rearrange("p (e r) -> p e r", e=E),
                                    psum_d[:, j, D:D + ER].rearrange("p (e r) -> p e r", e=E),
                                    m.unsqueeze(2).to_broadcast([P, E, R]), ALU.mult).then_inc(t2_steps, 1)
                                if j == 1:
                                    dve.wait_ge(t2_steps, n + 1)
                                    nc.vector.tensor_tensor(t2[:, i % 2, 0, :], t2[:, i % 2, 0, :], t2[:, i % 2, 1, :],
                                                            ALU.add).then_inc(t2_steps, 1)
                                    dve.wait_ge(x_steps, n)
                                nc.vector.scalar_tensor_tensor(
                                    row, psum_d[:, j, 0:D], weight[:, j, bass.ds(b * TPB + i, 1)], row,
                                    ALU.mult, ALU.add).then_inc(x_steps, 1)
                            dve.wait_ge(l2_psum, b * TPB + i + 1)
                            dve.wait_ge(x_steps, b * 3 * TPB + 3 * i + 2)
                            nc.vector.tensor_tensor(row, psum_l2[:, 0:D], row, ALU.add).then_inc(x_steps, 1)


def attention(nc, w, x_tok, ident):
    NH, HD = 16, 128
    SCALE = 1.0 / float(HD) ** 0.5
    BLK = 32
    NSC = P // BLK
    QT = T // P
    KT = T // P
    BQ = BT // P
    KPT = KT // BQ
    LAG = 5
    NPROB = 8
    with ExitStack() as ctx:
        def alloc(name, shape, dt=F32):
            return ctx.enter_context(nc.sbuf_tensor(name, shape, dt))

        def semaphore(name):
            return ctx.enter_context(nc.semaphore(name))

        x_hi = alloc("at_x_hi", [P, NC, T], F32R)
        x_lo = alloc("at_x_lo", [P, NC, T], F32R)
        cols = alloc("at_cols", [P, 3, NH])
        loaded = semaphore("at_loaded")
        hi_copied = semaphore("at_hi_copied")
        lo_copied = semaphore("at_lo_copied")

        with ExitStack() as inner:
            def sb(name, shape, dt=F32):
                return inner.enter_context(nc.sbuf_tensor(name, shape, dt))

            x_norm = sb("at_x_norm", [P, NT, D])
            wo_codes = sb("at_wo_codes", [P, NH, D])
            wo_scales = sb("at_wo_scales", [P, NH, D])
            bv_wide = sb("at_bv_wide", [P, NH, P])
            bo = sb("at_bo", [P, D])
            loads = [
                (cols[:], w["at_cols"].rearrange("p (m h) -> p m h", m=3)),
                (bo[:], w["at_bo"][0, :].partition_broadcast(P)),
                (wo_codes[:], w["at_wo_codes"].rearrange("(h p) n -> p h n", p=P)),
            ]
            scales_o = w["at_wo_scales"].rearrange("(h q) n -> q h n", q=NSC)
            for q in range(NSC):
                loads.append((wo_scales[q * BLK:(q + 1) * BLK], scales_o[q].partition_broadcast(BLK)))

            def emit(name, eng, bank, psum_t, transposed, value):
                c, b = divmod(bank, NB)
                src = psum_t[:, c, bass.ts(b, BT)]
                hi, lo = x_hi[:, c, bass.ts(b, BT)], x_lo[:, c, bass.ts(b, BT)]
                if name == "scalar":
                    eng.wait_ge(transposed, value)
                    nc.scalar.activation(hi, src, ACT.Copy).then_inc(hi_copied, 1)
                else:
                    eng.wait_ge(hi_copied, bank + 1)
                    nc.vector.tensor_tensor(lo, src, hi.bitcast(F32), ALU.subtract).then_inc(lo_copied, 1)

            with ExitStack() as ps_ctx:
                psum_t = ps_ctx.enter_context(nc.psum_tensor("at_psum_t", [P, NC, T], F32))
                layer_norm_tokens(nc, semaphore, sb, "at_ln", x_tok, ident, x_norm, psum_t, emit, loads, loaded)

            with ExitStack() as ps_ctx:
                psum_b = ps_ctx.enter_context(nc.psum_tensor("at_psum_b", [P, BT], F32))
                wo_scaled = semaphore("at_wo_scaled")
                bv_spread = semaphore("at_bv_spread")
                bv_psum = semaphore("at_bv_psum")
                bias_ready = semaphore("at_bias_ready")
                biased = semaphore("at_biased")
                with nc.Block() as block:
                    @block.vector
                    def _(dve):
                        nc.vector.tensor_tensor(wo_codes[:], wo_codes[:], wo_scales[:], ALU.mult).then_inc(wo_scaled, 1)
                        dve.wait_ge(bv_psum, 1)
                        nc.vector.tensor_tensor(bo[:], psum_b[:, 0:D], bo[:], ALU.add).then_inc(bias_ready, 1)
                        dve.wait_ge(bias_ready, 1)
                        nc.vector.tensor_tensor(x_tok[:], x_tok[:], bo[:].unsqueeze(1).to_broadcast([P, NT, D]),
                                                ALU.add).then_inc(biased, 1)

                    @block.gpsimd
                    def _(pool):
                        nc.gpsimd.tensor_copy(bv_wide[:], cols[:, 2, :].unsqueeze(2).to_broadcast([P, NH, P])
                                              ).then_inc(bv_spread, 1)

                    @block.tensor
                    def _(pe):
                        pe.wait_ge(bv_spread, 1)
                        pe.wait_ge(wo_scaled, 1)
                        for h in range(NH):
                            last = nc.tensor.matmul(psum_b[:, 0:D], bv_wide[:, h, :], wo_codes[:, h, :],
                                                    start=(h == 0), stop=(h == NH - 1))
                        last.then_inc(bv_psum, 1)

        with ExitStack() as inner:
            def sb(name, shape, dt=F32):
                return inner.enter_context(nc.sbuf_tensor(name, shape, dt))

            def ps(name, shape):
                return inner.enter_context(nc.psum_tensor(name, shape, F32))

            codes, scales = sb("at_codes", [P, 2, NC, HD]), sb("at_scales", [P, 2, NC, HD])
            w_hi, w_lo = sb("at_w_hi", [P, 2, NC, HD], F32R), sb("at_w_lo", [P, 2, NC, HD], F32R)
            v_codes, v_scales = (t[:].rearrange("p m c n -> p (m c n)").rearrange("p (c n) -> p c n", c=NC)
                                 for t in (codes, scales))
            wv_hi, wv_lo = sb("at_wv_hi", [P, NC, 2 * HD], F32R), sb("at_wv_lo", [P, NC, 2 * HD], F32R)
            o_codes, o_scales = sb("at_o_codes", [P, D]), sb("at_o_scales", [P, D])
            wo_hi, wo_lo = sb("at_wo_hi", [P, D], F32R), sb("at_wo_lo", [P, D], F32R)
            bias = sb("at_bias", [P, 2])
            q_hi, q_lo = sb("at_q_hi", [P, T], F32R), sb("at_q_lo", [P, T], F32R)
            k_hi, k_lo = sb("at_k_hi", [P, T], F32R), sb("at_k_lo", [P, T], F32R)
            v_hi, v_lo = sb("at_v_hi", [P, KT, 2 * HD], F32R), sb("at_v_lo", [P, KT, 2 * HD], F32R)
            prob = [sb(f"at_prob{j}", [P, T]) for j in range(NPROB)]
            pT_hi, pT_lo = sb("at_pT_hi", [P, 2, BT], F32R), sb("at_pT_lo", [P, 2, BT], F32R)
            oT_hi, oT_lo = sb("at_oT_hi", [P, BT], F32R), sb("at_oT_lo", [P, BT], F32R)
            part_max = sb("at_part_max", [P, 2, 5])
            shift = sb("at_shift", [P, 2])
            half_sum = sb("at_half_sum", [P, QT, 2])
            rsum = sb("at_rsum", [P, QT])
            psum_s = ps("at_psum_s", [P, 4, BT])
            psum_p = ps("at_psum_p", [P, 2, BT])
            psum_o = ps("at_psum_o", [P, BT])
            psum_x = ps("at_psum_x", [P, BT])

            w_loaded = semaphore("at_w_loaded")
            wv_loaded = semaphore("at_wv_loaded")
            w_split = semaphore("at_w_split")
            wv_split = semaphore("at_wv_split")
            wo_split = semaphore("at_wo_split")
            bias_ready = semaphore("at_bias_copied")
            qk_psum = semaphore("at_qk_psum")
            qk_hi = semaphore("at_qk_hi")
            qk_lo = semaphore("at_qk_lo")
            v_psum = semaphore("at_v_psum")
            v_hi_ready = semaphore("at_v_hi_ready")
            v_lo_ready = semaphore("at_v_lo_ready")
            scored = semaphore("at_scored")
            max_steps = semaphore("at_max_steps")
            exp_done = semaphore("at_exp_done")
            sum_steps = semaphore("at_sum_steps")
            p_transposed = semaphore("at_p_transposed")
            pT_hi_ready = semaphore("at_pT_hi_ready")
            pT_lo_ready = semaphore("at_pT_lo_ready")
            pv_done = semaphore("at_pv_done")
            oT_hi_ready = semaphore("at_oT_hi_ready")
            oT_lo_ready = semaphore("at_oT_lo_ready")
            wo_psum = semaphore("at_wo_psum")
            added = semaphore("at_added")
            N_W = (2 + 1) * (1 + NSC)
            N_WV = 1 + NSC
            NQK = 2 * NB
            NV = KT // 2

            def run(eng, slot, finish):
                def lower(hu, hs, odd):
                    for i in range(LAG):
                        slot(i, hs, None if hu is None else QT - LAG + i, hu, odd, True, None)

                def upper(h, begun, odd, v):
                    for i in range(LAG, QT):
                        slot(i, h, i - LAG, h, odd, begun, v if i == LAG else None)

                def pair(g, begun):
                    upper(g * 2, begun, 0, g)
                    lower(g * 2, g * 2 + 1, 0)
                    upper(g * 2 + 1, True, 1, None)

                lower(None, 0, 1)
                pair(0, False)
                with eng.Fori(1, NH // 2) as g:
                    lower(g * 2 - 1, g * 2, 1)
                    pair(g, True)
                lower(NH - 1, None, 1)
                finish(NH - 1)

            with nc.Block() as block:
                @block.sync
                def _(sp):
                    def load_v(g):
                        col = bass.ts(g, 2 * HD)
                        sp.dma_start(v_codes, w["at_wv_codes"].rearrange("(c p) n -> p c n", p=P)[:, :, col]
                                     ).then_inc(wv_loaded, 16)
                        sc = w["at_wv_scales"].rearrange("(c q) n -> q c n", q=NSC)
                        for q in range(NSC):
                            sp.dma_start(v_scales[q * BLK:(q + 1) * BLK],
                                         sc[q][:, col].partition_broadcast(BLK)).then_inc(wv_loaded, 16)

                    def load(h):
                        col = bass.ts(h, HD)
                        for m, name in enumerate("qk"):
                            sp.dma_start(codes[:, m], w[f"at_w{name}_codes"].rearrange("(c p) n -> p c n", p=P)[:, :, col]
                                         ).then_inc(w_loaded, 16)
                            sc = w[f"at_w{name}_scales"].rearrange("(c q) n -> q c n", q=NSC)
                            for q in range(NSC):
                                sp.dma_start(scales[q * BLK:(q + 1) * BLK, m],
                                             sc[q][:, col].partition_broadcast(BLK)).then_inc(w_loaded, 16)
                        sp.dma_start(o_codes[:], w["at_wo_codes"][bass.ts(h, HD), :]).then_inc(w_loaded, 16)
                        for q in range(NSC):
                            sp.dma_start(o_scales[q * BLK:(q + 1) * BLK, :],
                                         w["at_wo_scales"][bass.ds(h * NSC + q, 1), :].rearrange("a n -> (a n)")
                                         .partition_broadcast(BLK)).then_inc(w_loaded, 16)

                    load(0)
                    sp.wait_ge(w_split, 3)
                    load_v(0)
                    sp.wait_ge(wo_split, 3)
                    load(1)
                    with sp.Fori(1, NH // 2) as g:
                        sp.wait_ge(wo_split, g * 6)
                        load(g * 2)
                        sp.wait_ge(w_split, g * 6 + 3)
                        load_v(g)
                        sp.wait_ge(wo_split, g * 6 + 3)
                        load(g * 2 + 1)

                @block.gpsimd
                def _(pool):
                    def split(whole_hi, whole, scale, lo, steps, n):
                        nc.gpsimd.tensor_tensor(whole_hi, whole, scale, ALU.mult).then_inc(steps, 1)
                        nc.gpsimd.tensor_tensor(whole, whole, scale, ALU.mult).then_inc(steps, 1)
                        pool.wait_ge(steps, n + 2)
                        nc.gpsimd.tensor_tensor(lo, whole, whole_hi.bitcast(F32), ALU.subtract).then_inc(steps, 1)

                    def split_head(h, first, g=None):
                        pool.wait_ge(w_loaded, h * (16 * N_W) + 16 * N_W)
                        if not first:
                            pool.wait_ge(qk_psum, h * NQK)
                        split(w_hi[:], codes[:], scales[:], w_lo[:], w_split, h * 3)
                        if g is not None:
                            pool.wait_ge(wv_loaded, g * (16 * N_WV) + 16 * N_WV)
                            if not first:
                                pool.wait_ge(v_psum, g * NV)
                            split(wv_hi[:], v_codes, v_scales, wv_lo[:], wv_split, g * 3)
                        if not first:
                            pool.wait_ge(wo_psum, h * QT)
                        split(wo_hi[:], o_codes[:], o_scales[:], wo_lo[:], wo_split, h * 3)

                    split_head(0, True, 0)
                    split_head(1, False)
                    with pool.Fori(1, NH // 2) as g:
                        split_head(g * 2, False, g)
                        split_head(g * 2 + 1, False)

                @block.tensor
                def _(pe):
                    def three(out, a_hi, a_lo, b_hi, b_lo, start=True, stop=True):
                        nc.tensor.matmul(out, a_hi, b_hi, start=start, stop=False)
                        nc.tensor.matmul(out, a_hi, b_lo, start=False, stop=False)
                        return nc.tensor.matmul(out, a_lo, b_hi, start=False, stop=stop)

                    def qk(h, first):
                        pe.wait_ge(w_split, h * 3 + 3)
                        for m in range(2):
                            for b in range(NB):
                                if m == 1:
                                    pe.wait_ge(qk_lo, h * NQK + b + 1)
                                elif b % 2 == 0 and not first:
                                    pe.wait_ge(exp_done, h * (2 * QT) - 1 + b // 2)
                                for c in range(NC):
                                    last = three(psum_s[:, b, :], w_hi[:, m, c, :], w_lo[:, m, c, :],
                                                 x_hi[:, c, bass.ts(b, BT)], x_lo[:, c, bass.ts(b, BT)],
                                                 start=(c == 0), stop=(c == NC - 1))
                                last.then_inc(qk_psum, 1)

                    def v_pair(g):
                        pe.wait_ge(wv_split, g * 3 + 3)
                        for n in range(NV):
                            b = n % NB
                            if n >= NB:
                                pe.wait_ge(v_lo_ready, g * NV + n - NB + 1)
                            elif b % 2 == 0:
                                pe.wait_ge(exp_done, g * (4 * QT) + 2 * LAG - 1 + b // 2)
                            for j in range(2):
                                i = n * 2 + j
                                for c in range(NC):
                                    last = three(psum_s[:, b, bass.ts(j, 2 * HD)], x_hi[:, c, bass.ts(i, P)],
                                                 x_lo[:, c, bass.ts(i, P)], wv_hi[:, c, :], wv_lo[:, c, :],
                                                 start=(c == 0), stop=(c == NC - 1))
                            last.then_inc(v_psum, 1)

                    def score(i, h, n, v):
                        if i == 0:
                            if n == 0:
                                pe.wait_ge(qk_lo, h * NQK + NQK)
                        elif v is not None:
                            pe.wait_ge(v_lo_ready, v * NV + NV - NB + n + 1)
                        else:
                            pe.wait_ge(exp_done, h * (2 * QT) + (2 * i - 1 + n // 2))
                        three(psum_s[:, n, :], q_hi[:, bass.ts(i, P)], q_lo[:, bass.ts(i, P)],
                              k_hi[:, bass.ts(n, BT)], k_lo[:, bass.ts(n, BT)]).then_inc(scored, 1)

                    def turn(m, h, j):
                        if m % BQ == 0 and j == 0:
                            pe.wait_ge(exp_done, h * (2 * QT) + 2 * (m + BQ))
                        kk = (m % BQ) * KPT + j
                        for t in range(BQ):
                            buf = prob[(m - m % BQ + t) % NPROB]
                            last = nc.tensor.transpose(psum_p[:, j % 2, bass.ts(t, P)], buf[:, bass.ts(kk, P)], ident[:])
                        last.then_inc(p_transposed, 1)

                    def weigh(m, h, j, odd):
                        pe.wait_ge(pT_lo_ready, h * (QT * KPT) + (m * KPT + j + 1))
                        kk = (m % BQ) * KPT + j
                        if kk == 0:
                            pe.wait_ge(oT_lo_ready, h * (QT // BQ) + m // BQ)
                        half = bass.ts(odd, HD)
                        three(psum_o[:], v_hi[:, kk, half], v_lo[:, kk, half], pT_hi[:, j % 2, :], pT_lo[:, j % 2, :],
                              start=(kk == 0), stop=(kk == KT - 1)).then_inc(pv_done, 1)

                    def project(i, h):
                        b = i // BQ
                        pe.wait_ge(oT_lo_ready, h * (QT // BQ) + b + 1)
                        pe.wait_ge(added, h * QT + i)
                        if i == 0:
                            pe.wait_ge(wo_split, h * 3 + 3)
                        tile = bass.ts(i % BQ, P)
                        three(psum_x[:, 0:D], oT_hi[:, tile], oT_lo[:, tile], wo_hi[:], wo_lo[:]).then_inc(wo_psum, 1)

                    def slot(i, hs, m, hu, odd, begun, v):
                        projects = v is not None or (i == 0 and hs is not None)
                        if hu is not None:
                            turn(m, hu, 0)
                        if hs is not None and not projects:
                            score(i, hs, 0, v)
                            score(i, hs, 1, v)
                        if hu is not None:
                            if m > 0:
                                weigh(m - 1, hu, KPT - 1, odd)
                            elif begun:
                                weigh(QT - 1, hu - 1, KPT - 1, 1 - odd)
                        if projects:
                            if v is not None:
                                v_pair(v)
                            else:
                                qk(hs, hu is None)
                            if hu is not None:
                                turn(m, hu, 1)
                                weigh(m, hu, 0, odd)
                                turn(m, hu, 2)
                            for n in range(4):
                                score(i, hs, n, v)
                        else:
                            if hs is not None:
                                score(i, hs, 2, v)
                            if hu is not None:
                                turn(m, hu, 1)
                            if hs is not None:
                                score(i, hs, 3, v)
                            if hu is not None:
                                weigh(m, hu, 0, odd)
                                turn(m, hu, 2)
                        if hu is not None:
                            if m >= BQ:
                                project(m - BQ, hu)
                            elif begun:
                                project(QT - BQ + m, hu - 1)
                            weigh(m, hu, 1, odd)
                            turn(m, hu, 3)
                            weigh(m, hu, 2, odd)

                    def finish(h):
                        weigh(QT - 1, h, KPT - 1, 1)
                        for t in range(BQ):
                            project(QT - BQ + t, h)

                    run(pe, slot, finish)

                @block.scalar
                def _(act):
                    def qk(h):
                        nc.scalar.activation(bias[:], cols[:, 0:2, bass.ds(h, 1)].rearrange("p m a -> p (m a)"),
                                             ACT.Copy).then_inc(bias_ready, 1)
                        act.wait_ge(bias_ready, h + 1)
                        for m in range(2):
                            for b in range(NB):
                                act.wait_ge(qk_psum, h * NQK + (m * NB + b + 1))
                                nc.scalar.activation((q_hi, k_hi)[m][:, bass.ts(b, BT)], psum_s[:, b, :],
                                                     ACT.Identity, bias=bias[:, m:m + 1]).then_inc(qk_hi, 1)

                    def v_pair(g):
                        for n in range(NV):
                            act.wait_ge(v_psum, g * NV + n + 1)
                            nc.scalar.activation(v_hi[:, 2 * n:2 * n + 2, :],
                                                 psum_s[:, n % NB, :].rearrange("p (j d) -> p j d", j=2),
                                                 ACT.Copy).then_inc(v_hi_ready, 1)

                    def hi(m, h, j):
                        act.wait_ge(p_transposed, h * (QT * KPT) + (m * KPT + j + 1))
                        nc.scalar.activation(pT_hi[:, j % 2, :], psum_p[:, j % 2, :], ACT.Copy).then_inc(pT_hi_ready, 1)

                    def out_hi(b, h):
                        act.wait_ge(pv_done, h * (QT * KPT) + (b + 1) * KT)
                        act.wait_ge(wo_psum, h * QT + b * BQ)
                        nc.scalar.activation(oT_hi[:], psum_o[:], ACT.Copy).then_inc(oT_hi_ready, 1)

                    def exp(i, h, half):
                        act.wait_ge(max_steps, h * (6 * QT) + 6 * (i + 1))
                        nc.scalar.activation(prob[i % NPROB][:, bass.ts(half, T // 2)],
                                             psum_s[:, 2 * half:2 * half + 2, :].rearrange("p a b -> p (a b)"),
                                             ACT.Exp, bias=shift[:, i % 2:i % 2 + 1], scale=SCALE,
                                             accum_out=half_sum[:, i, half:half + 1]).then_inc(exp_done, 1)

                    def slot(i, hs, m, hu, odd, begun, v):
                        if hu is not None:
                            hi(m, hu, 0)
                            if m >= BQ and m % BQ == 0:
                                out_hi(m // BQ - 1, hu)
                            elif m == 0 and begun:
                                out_hi(QT // BQ - 1, hu - 1)
                        if v is not None:
                            v_pair(v)
                        elif i == 0 and hs is not None:
                            qk(hs)
                        if hu is not None:
                            hi(m, hu, 1)
                            hi(m, hu, 2)
                        if hs is not None:
                            exp(i, hs, 0)
                        if hu is not None:
                            hi(m, hu, 3)
                        if hs is not None:
                            exp(i, hs, 1)

                    def finish(h):
                        out_hi(QT // BQ - 1, h)

                    run(act, slot, finish)

                @block.vector
                def _(dve):
                    def qk(h):
                        for m in range(2):
                            hi, lo = ((q_hi, q_lo), (k_hi, k_lo))[m]
                            for b in range(NB):
                                tok = bass.ts(b, BT)
                                dve.wait_ge(qk_hi, h * NQK + (m * NB + b + 1))
                                nc.vector.scalar_tensor_tensor(lo[:, tok], psum_s[:, b, :], bias[:, m:m + 1],
                                                               hi[:, tok].bitcast(F32), ALU.add,
                                                               ALU.subtract).then_inc(qk_lo, 1)

                    def v_pair(g):
                        for n in range(NV):
                            part = slice(2 * n, 2 * n + 2)
                            dve.wait_ge(v_hi_ready, g * NV + n + 1)
                            nc.vector.tensor_tensor(v_lo[:, part, :], psum_s[:, n % NB, :].rearrange("p (j d) -> p j d", j=2),
                                                    v_hi[:, part, :].bitcast(F32), ALU.subtract).then_inc(v_lo_ready, 1)

                    def lo(m, h, j):
                        dve.wait_ge(pT_hi_ready, h * (QT * KPT) + (m * KPT + j + 1))
                        nc.vector.tensor_tensor(pT_lo[:, j % 2, :], psum_p[:, j % 2, :], pT_hi[:, j % 2, :].bitcast(F32),
                                                ALU.subtract).then_inc(pT_lo_ready, 1)

                    def out_lo(b, h):
                        dve.wait_ge(oT_hi_ready, h * (QT // BQ) + b + 1)
                        nc.vector.tensor_tensor(oT_lo[:], psum_o[:], oT_hi[:].bitcast(F32),
                                                ALU.subtract).then_inc(oT_lo_ready, 1)

                    def largest(i, h, n):
                        dve.wait_ge(scored, h * (4 * QT) + (4 * i + n + 1))
                        nc.vector.tensor_reduce(part_max[:, i % 2, n:n + 1], psum_s[:, n, :], AX.X,
                                                ALU.max).then_inc(max_steps, 1)

                    def three_largest(i, h):
                        dve.wait_ge(max_steps, h * (6 * QT) + (6 * i + 3))
                        nc.vector.tensor_reduce(part_max[:, i % 2, 4:5], part_max[:, i % 2, 0:3], AX.X,
                                                ALU.max).then_inc(max_steps, 1)

                    def row_shift(i, h):
                        dve.wait_ge(max_steps, h * (6 * QT) + (6 * i + 5))
                        nc.vector.tensor_scalar(shift[:, i % 2:i % 2 + 1], part_max[:, i % 2, 3:4],
                                                part_max[:, i % 2, 4:5], -SCALE, ALU.max, ALU.mult
                                                ).then_inc(max_steps, 1)

                    def row_sum(i, h):
                        dve.wait_ge(exp_done, h * (2 * QT) + 2 * (i + 1))
                        nc.vector.tensor_tensor(rsum[:, i:i + 1], half_sum[:, i, 0:1], half_sum[:, i, 1:2],
                                                ALU.add).then_inc(sum_steps, 1)
                        dve.wait_ge(sum_steps, h * (2 * QT) + (2 * i + 1))
                        nc.vector.reciprocal(rsum[:, i:i + 1], rsum[:, i:i + 1]).then_inc(sum_steps, 1)

                    def add(i, h):
                        dve.wait_ge(wo_psum, h * QT + i + 1)
                        nc.vector.scalar_tensor_tensor(x_tok[:, i, :], psum_x[:, 0:D], rsum[:, i:i + 1], x_tok[:, i, :],
                                                       ALU.mult, ALU.add).then_inc(added, 1)

                    def slot(i, hs, m, hu, odd, begun, v):
                        projects = v is not None or (i == 0 and hs is not None)

                        def first_sums():
                            if hs is not None and i > 0:
                                row_sum(i - 1, hs)
                            elif hu is not None and i == 0:
                                row_sum(QT - 1, hu)

                        def first_turn():
                            if hu is not None:
                                lo(m, hu, 0)
                                if m >= BQ and m % BQ == 0:
                                    out_lo(m // BQ - 1, hu)
                                elif m == 0 and begun:
                                    out_lo(QT // BQ - 1, hu - 1)

                        if projects:
                            first_turn()
                            first_sums()
                            if v is not None:
                                v_pair(v)
                            else:
                                qk(hs)
                            if hu is not None:
                                lo(m, hu, 1)
                            for n in range(4):
                                largest(i, hs, n)
                                if n == 2:
                                    three_largest(i, hs)
                            row_shift(i, hs)
                        else:
                            if hs is not None:
                                largest(i, hs, 0)
                                largest(i, hs, 1)
                            first_sums()
                            first_turn()
                            if hs is not None:
                                largest(i, hs, 2)
                                three_largest(i, hs)
                            if hu is not None:
                                lo(m, hu, 1)
                            if hs is not None:
                                largest(i, hs, 3)
                                row_shift(i, hs)
                        if hu is not None:
                            lo(m, hu, 2)
                            if m >= BQ:
                                add(m - BQ, hu)
                            elif begun:
                                add(QT - BQ + m, hu - 1)
                            lo(m, hu, 3)

                    def finish(h):
                        out_lo(QT // BQ - 1, h)
                        for t in range(BQ):
                            add(QT - BQ + t, h)

                    run(dve, slot, finish)


def expert_ffn(nc, w, x_tok, ident):
    E, F = 8, 512
    NF = F // P
    NBK = NT + E - 1
    with ExitStack() as ctx:
        def alloc(name, shape, dt=F32):
            return ctx.enter_context(nc.sbuf_tensor(name, shape, dt))

        def semaphore(name):
            return ctx.enter_context(nc.semaphore(name))

        rows_in = nc.dram_tensor("ef_rows_in", (NBK * P, D), F32, kind="Internal").ap()
        rows_out = nc.dram_tensor("ef_rows_out", (NBK * P, D), F32, kind="Internal").ap()
        x_norm = alloc("ef_x_norm", [P, NT, D])
        gate_up = alloc("ef_gate_up", [P, E, NC, 2 * F])
        down = alloc("ef_down", [P, E, NF, D])
        slot = alloc("ef_slot", [P, NT], mybir.dt.int32)
        block_expert = alloc("ef_block_expert", [P, NBK], mybir.dt.int32)
        experts_loaded = semaphore("ef_experts_loaded")
        rows_zeroed = semaphore("ef_rows_zeroed")
        scattered = semaphore("ef_scattered")

        with ExitStack() as mid:
            def mb(name, shape, dt=F32):
                return mid.enter_context(nc.sbuf_tensor(name, shape, dt))

            xT = mb("ef_xT", [P, NC, T])
            router = mb("ef_router", [P, NC, E])
            shared_gu = mb("ef_shared_gu", [P, NC, 2 * F])
            shared_down = mb("ef_shared_down", [P, NF, D])
            order = mb("ef_order", [P, E])
            earlier = mb("ef_earlier", [P, P])
            ones = mb("ef_ones", [P, P])
            limits = mb("ef_limits", [P, NT])
            numbers = mb("ef_numbers", [P, NBK])
            loaded = semaphore("ef_loaded")
            copied = semaphore("ef_copied")
            loads = (
                (router[:], w["ef_router"].rearrange("(c p) n -> p c n", p=P)),
                (shared_gu[:], w["ef_shared_gate_up"].rearrange("(c p) n -> p c n", p=P)),
                (shared_down[:], w["ef_shared_down"].rearrange("(c p) n -> p c n", p=P)),
                (order[:], w["c_order"][0, :].partition_broadcast(P)),
                (earlier[:], w["c_earlier"]),
                (ones[:], w["c_ones"]),
                (limits[:], w["c_limits"][0, :].partition_broadcast(P)),
                (numbers[:], w["c_numbers"][0, :].partition_broadcast(P)),
            )
            with ExitStack() as inner:
                psum_t = inner.enter_context(nc.psum_tensor("ef_psum_t", [P, NC, T], F32))
                layer_norm_tokens(nc, semaphore,
                                  lambda n, s, d: inner.enter_context(nc.sbuf_tensor(n, s, d)),
                                  "ef_ln", x_tok, ident, x_norm, psum_t, copy_banks(nc, xT, copied), loads, loaded)

            with ExitStack() as inner:
                def sb(name, shape, dt=F32):
                    return inner.enter_context(nc.sbuf_tensor(name, shape, dt))

                def ps(name, shape):
                    return inner.enter_context(nc.psum_tensor(name, shape, F32))

                zeros = sb("ef_zeros", [P, D])
                logits = sb("ef_logits", [P, NT, E])
                hit = sb("ef_hit", [P, NT, E])
                rank = sb("ef_rank", [P, NT, E])
                best = sb("ef_best", [P, NT])
                top = sb("ef_top", [P, NT])
                score = sb("ef_score", [P, NT])
                ends = sb("ef_ends", [P, E, NT])
                place = sb("ef_place", [P, NT, E])
                wide_e = sb("ef_wide_e", [P, E, NT])
                blocks = sb("ef_blocks", [P, E])
                block_ends = sb("ef_block_ends", [P, E])
                first_row = sb("ef_first_row", [P, E])
                ones_e = sb("ef_ones_e", [P, NT])
                slot_f = sb("ef_slot_f", [P, NT])
                past = sb("ef_past", [P, NBK, E])
                expert_f = sb("ef_expert_f", [P, NBK])
                silu_g = sb("ef_silu_g", [P, 2, BT])
                hidden = sb("ef_hidden", [P, NF, BT])
                psum_r = ps("ef_psum_r", [P, NT, E])
                psum_k = ps("ef_psum_k", [P, 2, NT * E])
                psum_g = ps("ef_psum_g", [P, 2, BT])
                psum_u = ps("ef_psum_u", [P, 2, BT])
                psum_y = ps("ef_psum_y", [P, BT])
                zeros_ready = semaphore("ef_zeros_ready")
                ones_ready = semaphore("ef_ones_ready")
                routed = semaphore("ef_routed")
                chain = semaphore("ef_chain")
                hit_ready = semaphore("ef_hit_ready")
                top_ready = semaphore("ef_top_ready")
                counted = semaphore("ef_counted")
                scored = semaphore("ef_scored")
                scaled = semaphore("ef_scaled")
                slots_ready = semaphore("ef_slots_ready")
                gu_psum = semaphore("ef_gu_psum")
                silu_ready = semaphore("ef_silu_ready")
                hidden_ready = semaphore("ef_hidden_ready")
                y_psum = semaphore("ef_y_psum")
                y_added = semaphore("ef_y_added")

                with nc.Block() as block:
                    @block.sync
                    def _(sp):
                        sp.wait_ge(zeros_ready, 1)
                        for j in range(NBK):
                            sp.dma_start(rows_in[j * P:(j + 1) * P, :], zeros[:]).then_inc(rows_zeroed, 16)
                        for e in range(E):
                            sp.dma_start(gate_up[:, e], w["ef_gate_up"][e].rearrange("(c p) n -> p c n", p=P)
                                         ).then_inc(experts_loaded, 16)
                            sp.dma_start(down[:, e], w["ef_down"][e].rearrange("(c p) n -> p c n", p=P)
                                         ).then_inc(experts_loaded, 16)

                    @block.gpsimd
                    def _(pool):
                        nc.gpsimd.memset(zeros[:], 0.0).then_inc(zeros_ready, 1)
                        nc.gpsimd.memset(ones_e[:], 1.0).then_inc(ones_ready, 1)
                        pool.wait_ge(scored, 1)
                        for i in range(NT):
                            nc.gpsimd.tensor_scalar(x_norm[:, i, :], x_norm[:, i, :], score[:, i:i + 1], None,
                                                    ALU.mult).then_inc(scaled, 1)
                        pool.wait_ge(rows_zeroed, 16 * NBK)
                        pool.wait_ge(slots_ready, 1)
                        for i in range(NT):
                            pool.wait_ge(scaled, i + 1)
                            pool.indirect_dma_start(
                                out=rows_in, out_offset=bass.IndirectOffsetOnAxis(ap=slot[:, i:i + 1], axis=0),
                                in_=x_norm[:, i, :], in_offset=None, bounds_check=NBK * P - 1
                            ).then_inc(scattered, 16)

                    @block.scalar
                    def _(act):
                        act.wait_ge(top_ready, 1)
                        nc.scalar.activation(score[:], top[:], ACT.Sigmoid).then_inc(scored, 1)
                        with act.Fori(0, NB) as b:
                            for f in range(NF):
                                act.wait_ge(gu_psum, b * NF + f + 1)
                                nc.scalar.activation(silu_g[:, f % 2, :], psum_g[:, f % 2, :],
                                                     ACT.Silu).then_inc(silu_ready, 1)

                    @block.vector
                    def _(dve):
                        steps = Steps(chain)

                        def after(instruction):
                            dve.wait_ge(steps.sem, steps.add(instruction))

                        wide = [P, NT, E]
                        dve.wait_ge(routed, 1)
                        after(nc.vector.tensor_copy(logits[:], psum_r[:]))
                        choose_largest(nc, dve, steps, logits[:], order[:], top[:], hit[:], rank[:], best[:])
                        nc.vector.tensor_copy(top[:], top[:]).then_inc(top_ready, 1)
                        nc.vector.tensor_copy(hit[:], hit[:]).then_inc(hit_ready, 1)
                        dve.wait_ge(counted, 1)
                        dve.wait_ge(ones_ready, 1)
                        counts = psum_k[:, 1, :].rearrange("p (i e) -> p e i", e=E)
                        for e in range(E):
                            nc.vector.tensor_tensor_scan(ends[:, e, :], ones_e[:], counts[:, e, :], 0.0,
                                                         ALU.mult, ALU.add).then_inc(steps.sem, 1)
                            steps.n += 1
                        dve.wait_ge(steps.sem, steps.n)
                        after(nc.vector.tensor_tensor(place[:], ends[:].rearrange("p e i -> p i e"),
                                                      psum_k[:, 1, :].rearrange("p (i e) -> p i e", e=E), ALU.subtract))
                        after(nc.vector.tensor_tensor(place[:], psum_k[:, 0, :].rearrange("p (i e) -> p i e", e=E),
                                                      place[:], ALU.add))
                        after(nc.vector.tensor_tensor(wide_e[:], ends[:, :, NT - 1:NT].to_broadcast([P, E, NT]),
                                                      limits[:].unsqueeze(1).to_broadcast([P, E, NT]), ALU.is_gt))
                        after(nc.vector.tensor_reduce(blocks[:], wide_e[:], AX.X, ALU.add))
                        after(nc.vector.tensor_tensor_scan(block_ends[:], ones_e[:, 0:E], blocks[:], 0.0,
                                                           ALU.mult, ALU.add))
                        after(nc.vector.tensor_tensor(first_row[:], block_ends[:], blocks[:], ALU.subtract))
                        after(nc.vector.scalar_tensor_tensor(
                            place[:], first_row[:].unsqueeze(1).to_broadcast(wide), float(P), place[:],
                            ALU.mult, ALU.add))
                        after(nc.vector.tensor_tensor(place[:], place[:], hit[:], ALU.mult))
                        after(nc.vector.tensor_reduce(slot_f[:], place[:], AX.X, ALU.add))
                        nc.vector.tensor_copy(slot[:], slot_f[:]).then_inc(slots_ready, 1)
                        after(nc.vector.tensor_tensor(
                            past[:], block_ends[:].unsqueeze(1).to_broadcast([P, NBK, E]),
                            numbers[:].unsqueeze(2).to_broadcast([P, NBK, E]), ALU.is_le))
                        after(nc.vector.tensor_reduce(expert_f[:], past[:], AX.X, ALU.add))
                        after(nc.vector.tensor_scalar(block_expert[:], expert_f[:], float(E - 1), None, ALU.min))
                        with dve.Fori(0, NB) as b:
                            for f in range(NF):
                                dve.wait_ge(silu_ready, b * NF + f + 1)
                                nc.vector.tensor_tensor(hidden[:, f, :], psum_u[:, f % 2, :], silu_g[:, f % 2, :],
                                                        ALU.mult).then_inc(hidden_ready, 1)
                            for j in range(TPB):
                                dve.wait_ge(y_psum, b * TPB + j + 1)
                                row = x_tok[:, bass.ds(b * TPB + j, 1), :].rearrange("p a d -> p (a d)")
                                nc.vector.tensor_tensor(row, psum_y[:, 0:D], row, ALU.add).then_inc(y_added, 1)

                    @block.tensor
                    def _(pe):
                        for i in range(NT):
                            for c in range(NC):
                                last = nc.tensor.matmul(psum_r[:, i, :], xT[:, c, bass.ts(i, P)], router[:, c, :],
                                                        start=(c == 0), stop=(c == NC - 1))
                        last.then_inc(routed, 1)

                        def up(b, f):
                            if f >= 2:
                                pe.wait_ge(hidden_ready, b * NF + f - 1)
                            for out, off in ((psum_g, 0), (psum_u, F)):
                                for c in range(NC):
                                    last = nc.tensor.matmul(out[:, f % 2, :], shared_gu[:, c, off + f * P:off + (f + 1) * P],
                                                            xT[:, c, bass.ts(b, BT)], start=(c == 0), stop=(c == NC - 1))
                            last.then_inc(gu_psum, 1)

                        pe.wait_ge(hit_ready, 1)
                        hits = hit[:].rearrange("p i e -> p (i e)")
                        nc.tensor.matmul(psum_k[:, 0, :], earlier[:], hits, start=True, stop=True)
                        nc.tensor.matmul(psum_k[:, 1, :], ones[:], hits, start=True, stop=True).then_inc(counted, 1)
                        with pe.Fori(0, NB) as b:
                            for f in range(NF):
                                up(b, f)
                            for j in range(TPB):
                                pe.wait_ge(hidden_ready, b * NF + NF)
                                if j >= 1:
                                    pe.wait_ge(y_added, b * TPB + j)
                                for f in range(NF):
                                    last = nc.tensor.matmul(psum_y[:, 0:D], hidden[:, f, bass.ts(j, P)],
                                                            shared_down[:, f, :], start=(f == 0), stop=(f == NF - 1))
                                last.then_inc(y_psum, 1)
                            pe.wait_ge(y_added, b * TPB + TPB)

        with ExitStack() as inner:
            def sb(name, shape, dt=F32):
                return inner.enter_context(nc.sbuf_tensor(name, shape, dt))

            def ps(name, shape):
                return inner.enter_context(nc.psum_tensor(name, shape, F32))

            rows = sb("ef_rows", [P, 2, D])
            rowsT = sb("ef_rowsT", [P, 2, NC, P])
            silu_g = sb("ef_silu_x", [P, 2, F])
            hidden = sb("ef_hidden_x", [P, 2, F])
            hiddenT = sb("ef_hiddenT", [P, 2, NF, P])
            result = sb("ef_result", [P, 2, D])
            back = x_norm
            psum_xt = ps("ef_psum_xt", [P, NC, P])
            psum_gu = ps("ef_psum_gu", [P, 2, 2, F])
            psum_ht = ps("ef_psum_ht", [P, NF, P])
            psum_d = ps("ef_psum_d", [P, BT])
            rows_loaded = [semaphore(f"ef_rows_loaded{k}") for k in range(2)]
            x_transposed = semaphore("ef_x_transposed")
            rowsT_ready = semaphore("ef_rowsT_ready")
            gu_psum = semaphore("ef_gu_psum_x")
            silu_ready = semaphore("ef_silu_x_ready")
            hidden_ready = semaphore("ef_hidden_x_ready")
            h_transposed = semaphore("ef_h_transposed")
            hiddenT_ready = semaphore("ef_hiddenT_ready")
            d_psum = semaphore("ef_d_psum")
            result_ready = semaphore("ef_result_ready")
            rows_stored = [semaphore(f"ef_rows_stored{k}") for k in range(2)]
            gathered = [semaphore(f"ef_gathered{g}") for g in range(NB)]
            added = semaphore("ef_added")

            def blocks(eng, body):
                with eng.Fori(0, NBK // 2) as pair:
                    body(pair * 2, 0)
                    body(pair * 2 + 1, 1)
                body(NBK - 1, 0)

            with nc.Block() as block:
                @block.sync
                def _(sp):
                    def load(j, k):
                        sp.dma_start(rows[:, k, :], rows_in[bass.ts(j, P), :]).then_inc(rows_loaded[k], 16)

                    sp.wait_ge(scattered, 16 * NT)
                    load(0, 0)
                    load(1, 1)
                    with sp.Fori(1, NBK // 2) as pair:
                        for k in range(2):
                            sp.wait_ge(x_transposed, pair * 2 + (k - 1))
                            load(pair * 2 + k, k)
                    sp.wait_ge(x_transposed, NBK - 2)
                    load(NBK - 1, 0)

                @block.tensor
                def _(pe):
                    pe.wait_ge(experts_loaded, 16 * 2 * E)

                    def up(j, k, count):
                        e = pe.value_load(block_expert[0:1, bass.ds(j, 1)], min_val=0, max_val=E - 1)
                        pe.wait_ge(rows_loaded[k], count)
                        for c in range(NC):
                            last = nc.tensor.transpose(psum_xt[:, c, :], rows[:, k, bass.ts(c, P)], ident[:])
                        last.then_inc(x_transposed, 1)
                        pe.wait_ge(rowsT_ready, j + 1)
                        for half in range(2):
                            for c in range(NC):
                                wt = gate_up[:, bass.ds(e, 1), c, bass.ts(half, F)].rearrange("p a n -> p (a n)")
                                last = nc.tensor.matmul(psum_gu[:, k, half, :], rowsT[:, k, c, :], wt,
                                                        start=(c == 0), stop=(c == NC - 1))
                        last.then_inc(gu_psum, 1)
                        return e

                    def dn(j, k, e):
                        pe.wait_ge(hidden_ready, j + 1)
                        for c in range(NF):
                            last = nc.tensor.transpose(psum_ht[:, c, :], hidden[:, k, bass.ts(c, P)], ident[:])
                        last.then_inc(h_transposed, 1)
                        pe.wait_ge(hiddenT_ready, j + 1)
                        if k == 1:
                            pe.wait_ge(result_ready, j)
                        for c in range(NF):
                            wt = down[:, bass.ds(e, 1), c, :].rearrange("p a n -> p (a n)")
                            last = nc.tensor.matmul(psum_d[:, 0:D], hiddenT[:, k, c, :], wt,
                                                    start=(c == 0), stop=(c == NF - 1))
                        last.then_inc(d_psum, 1)

                    with pe.Fori(0, NBK // 2) as pair:
                        e0 = up(pair * 2, 0, pair * 16 + 16)
                        e1 = up(pair * 2 + 1, 1, pair * 16 + 16)
                        dn(pair * 2, 0, e0)
                        dn(pair * 2 + 1, 1, e1)
                        pe.wait_ge(result_ready, pair * 2 + 2)
                    dn(NBK - 1, 0, up(NBK - 1, 0, 16 * (NBK // 2 + 1)))

                @block.scalar
                def _(act):
                    def up(j, k):
                        act.wait_ge(x_transposed, j + 1)
                        nc.scalar.activation(rowsT[:, k], psum_xt[:], ACT.Copy).then_inc(rowsT_ready, 1)
                        act.wait_ge(gu_psum, j + 1)
                        nc.scalar.activation(silu_g[:, k, :], psum_gu[:, k, 0, :], ACT.Silu).then_inc(silu_ready, 1)

                    def dn(j, k):
                        act.wait_ge(h_transposed, j + 1)
                        nc.scalar.activation(hiddenT[:, k], psum_ht[:], ACT.Copy).then_inc(hiddenT_ready, 1)

                    with act.Fori(0, NBK // 2) as pair:
                        up(pair * 2, 0)
                        up(pair * 2 + 1, 1)
                        dn(pair * 2, 0)
                        dn(pair * 2 + 1, 1)
                    up(NBK - 1, 0)
                    dn(NBK - 1, 0)

                @block.vector
                def _(dve):
                    def up(j, k):
                        dve.wait_ge(silu_ready, j + 1)
                        nc.vector.tensor_tensor(hidden[:, k, :], psum_gu[:, k, 1, :], silu_g[:, k, :],
                                                ALU.mult).then_inc(hidden_ready, 1)

                    def dn(j, k, stored):
                        dve.wait_ge(d_psum, j + 1)
                        if stored is not None:
                            dve.wait_ge(rows_stored[k], stored)
                        nc.vector.tensor_copy(result[:, k, :], psum_d[:, 0:D]).then_inc(result_ready, 1)

                    up(0, 0)
                    up(1, 1)
                    dn(0, 0, None)
                    dn(1, 1, None)
                    with dve.Fori(1, NBK // 2) as pair:
                        up(pair * 2, 0)
                        up(pair * 2 + 1, 1)
                        dn(pair * 2, 0, pair * 16)
                        dn(pair * 2 + 1, 1, pair * 16)
                    up(NBK - 1, 0)
                    dn(NBK - 1, 0, 16 * (NBK // 2))
                    for g in range(NB):
                        tiles = slice(g * TPB, (g + 1) * TPB)
                        dve.wait_ge(gathered[g], 16 * TPB)
                        nc.vector.tensor_tensor(x_tok[:, tiles, :], x_tok[:, tiles, :], back[:, tiles, :],
                                                ALU.add).then_inc(added, 1)

                @block.gpsimd
                def _(pool):
                    def store(j, k):
                        pool.wait_ge(result_ready, j + 1)
                        pool.dma_start(rows_out[bass.ts(j, P), :], result[:, k, :]).then_inc(rows_stored[k], 16)

                    blocks(pool, store)
                    for k in range(2):
                        pool.wait_ge(rows_stored[k], 16 * ((NBK + 1 - k) // 2))
                    for i in range(NT):
                        pool.indirect_dma_start(
                            out=back[:, i, :], out_offset=None, in_=rows_out,
                            in_offset=bass.IndirectOffsetOnAxis(ap=slot[:, i:i + 1], axis=0),
                            bounds_check=NBK * P - 1).then_inc(gathered[i // TPB], 16)


def build(nc, w, out, parts=(1, 2, 3, 4)):
    with ExitStack() as ctx:
        x_tok = ctx.enter_context(nc.sbuf_tensor("x_tok", [P, NT, D], F32))
        ident = ctx.enter_context(nc.sbuf_tensor("ident", [P, P], F32))
        x_loaded = ctx.enter_context(nc.semaphore("x_loaded"))
        stored = ctx.enter_context(nc.semaphore("stored"))
        with nc.Block() as block:
            @block.sync
            def _(sp):
                sp.dma_start(x_tok[:], w["L0_attn_x"].rearrange("(i p) d -> p i d", p=P)).then_inc(x_loaded, 16)
                sp.dma_start(ident[:], w["c_ident"]).then_inc(x_loaded, 16)
                sp.wait_ge(x_loaded, 32)

        if 1 in parts:
            time_mix(nc, w, x_tok, ident)
        if 2 in parts:
            lora_ffn(nc, w, x_tok, ident)
        if 3 in parts:
            attention(nc, w, x_tok, ident)
        if 4 in parts:
            expert_ffn(nc, w, x_tok, ident)

        with nc.Block() as block:
            @block.sync
            def _(sp):
                sp.dma_start(out.rearrange("(i p) d -> p i d", p=P), x_tok[:]).then_inc(stored, 16)
                sp.wait_ge(stored, 16)


def lay_out(inputs):
    import numpy as np

    a = {k: np.asarray(v) for k, v in inputs.items()}
    H, K, V, E, R, F = 16, 8, 8, 8, 16, 1024

    def col(x):
        return x.reshape(-1, P).T

    w = {"L0_attn_x": a["L0_attn_x"].reshape(T, D)}
    for k in ("L0_attn_Wx1", "L0_attn_Ww_b", "L0_attn_Wg_b", "L0_attn_Wo"):
        w[k] = a[k]
    w["Wx2T"] = a["L0_attn_Wx2"].transpose(1, 2, 0).reshape(-1, D)
    w["tm_proj"] = np.concatenate([a["L0_attn_" + k] for k in ("Wr", "Ww_a", "Wk", "Wv", "Wg_a")], axis=1)
    w["tm_cols"] = np.concatenate(
        [col(a["L0_attn_mu_x"]), col(a["L0_attn_x_bias"]), col(a["L0_attn_bw"]), col(a["L0_attn_bg"]),
         col(a["L0_attn_bonus"]), np.tile(a["L0_attn_ln_w"], H)[:, None], np.tile(a["L0_attn_ln_b"], H)[:, None]], axis=1)
    same = np.kron(np.eye(H), np.ones((V, K))).astype(np.float32)
    pick = np.zeros((P, V, P), np.float32)
    for v in range(V):
        pick[v::V, v, :] = same[v::V, :]
    w["c_spread"] = pick
    w["c_gather"] = pick.transpose(2, 1, 0)
    w["c_heads"] = same
    w["c_ident"] = np.eye(P, dtype=np.float32)
    w["lf_router_a1"] = np.concatenate([a["L0_ffn_Wr"], a["L0_ffn_A1"].transpose(2, 0, 1).reshape(D, E * R)], axis=1)
    w["lf_br"] = a["L0_ffn_br"][None, :]
    w["L0_ffn_W1"] = a["L0_ffn_W1"]
    w["lf_b1"] = col(a["L0_ffn_b1"])
    w["lf_B1T"] = a["L0_ffn_B1"].transpose(0, 2, 1).reshape(E * R, F)
    w["lf_w2_a2"] = np.concatenate([a["L0_ffn_W2"], a["L0_ffn_A2"].transpose(2, 0, 1).reshape(F, E * R)], axis=1)
    w["lf_b2"] = a["L0_ffn_b2"][None, :]
    w["lf_B2T"] = a["L0_ffn_B2"].transpose(0, 2, 1).reshape(E * R, D)
    for n in "qkvo":
        w[f"at_w{n}_codes"] = a[f"L1_attn_w{n}_codes"]
        w[f"at_w{n}_scales"] = a[f"L1_attn_w{n}_scales"]
    w["at_cols"] = np.concatenate([col(a["L1_attn_b" + n]) for n in "qkv"], axis=1)
    w["at_bo"] = a["L1_attn_bo"][None, :]
    w["ef_router"] = a["L1_ffn_router_w"].T
    w["ef_gate_up"] = a["L1_ffn_gate_up_proj"]
    w["ef_down"] = a["L1_ffn_down_proj"]
    w["ef_shared_gate_up"] = np.concatenate([a["L1_ffn_shared_gate_w"], a["L1_ffn_shared_up_w"]], axis=1)
    w["ef_shared_down"] = a["L1_ffn_shared_down_w"]
    w["c_earlier"] = np.triu(np.ones((P, P), np.float32), 1)
    w["c_limits"] = np.arange(0, T, P, dtype=np.float32)[None, :]
    w["c_numbers"] = np.arange(NT + E - 1, dtype=np.float32)[None, :]
    w["c_order"] = np.arange(E, 0, -1, dtype=np.float32)[None, :]
    w["c_ones"] = np.ones((P, P), np.float32)
    return {k: np.ascontiguousarray(v) for k, v in w.items()}


def kernel(**inputs):
    import concourse.bacc as _bacc
    from concourse.bass_utils import run_bass_kernel_spmd as _run

    nc = _bacc.Bacc("TRN2", target_bir_lowering=False, num_devices=1)
    arrays = lay_out(inputs)
    w = {k: nc.dram_tensor(f"in_{k}", v.shape, mybir.dt.from_np(v.dtype), kind="ExternalInput").ap()
         for k, v in arrays.items()}
    out = nc.dram_tensor("out_dram", (T, D), F32, kind="ExternalOutput").ap()
    build(nc, w, out)
    r = _run(nc, [{f"in_{k}": v for k, v in arrays.items()}], core_ids=[0])
    return r.results[0]["out_dram"].reshape(1, T, D)
```

```python
import concourse.bass as bass
from concourse import mybir
from contextlib import ExitStack

F32 = mybir.dt.float32
F32R = mybir.dt.float32r
ALU = mybir.AluOpType
ACT = mybir.ActivationFunctionType
AX = mybir.AxisListType

P = 128
T = 2048
D = 256
NT = T // P
NC = D // P
BT = 512
NB = T // BT
TPB = BT // P
EPS = 1e-5


class Steps:

    def __init__(self, sem):
        self.sem, self.n = sem, 0

    def add(self, instruction, by=1):
        instruction.then_inc(self.sem, by)
        self.n += by
        return self.n


class LayerNorms:

    def __init__(self, semaphore):
        self.before = 0
        self.stats_ready = semaphore("ln_stats_ready")
        self.moments_ready = semaphore("ln_moments_ready")
        self.var_eps_ready = semaphore("ln_var_eps_ready")
        self.std_ready = semaphore("ln_std_ready")
        self.rstd_ready = semaphore("ln_rstd_ready")
        self.norm_ready = semaphore("ln_norm_ready")
        self.transposed = semaphore("ln_transposed")


def layer_norm_tokens(nc, ln, alloc, tag, x_tok, ident, x_norm, psum_t, emit,
                      loads=(), loaded=None, pool_work=None):
    stats = alloc(f"{tag}_stats", [P, NT, 6], F32)
    mean_var = alloc(f"{tag}_mean_var", [P, NT, 2], F32)
    std = alloc(f"{tag}_std", [P, NT], F32)
    rstd = alloc(f"{tag}_rstd", [P, NT], F32)
    tiles_before = ln.before * NT
    steps_before = ln.before
    ln.before += 1

    with nc.Block() as block:
        @block.sync
        def _(sp):
            for dst, src in loads:
                sp.dma_start(dst, src).then_inc(loaded, 16)
            if loads:
                sp.wait_ge(loaded, 16 * len(loads))

        @block.vector
        def _(dve):
            with dve.Fori(0, NT) as i:
                nc.vector.bn_stats(stats[:, i, :], x_tok[:, i, :]).then_inc(ln.stats_ready, 1)
            dve.wait_ge(ln.stats_ready, tiles_before + NT)
            for i in range(NT):
                nc.vector.bn_aggr(mean_var[:, i, :], stats[:, i, :]).then_inc(ln.moments_ready, 1)
            dve.wait_ge(ln.moments_ready, tiles_before + NT)
            nc.vector.tensor_scalar(std[:], mean_var[:, :, 1], EPS, None, ALU.add).then_inc(ln.var_eps_ready, 1)
            dve.wait_ge(ln.std_ready, steps_before + 1)
            nc.vector.reciprocal(rstd[:], std[:]).then_inc(ln.rstd_ready, 1)
            dve.wait_ge(ln.rstd_ready, steps_before + 1)
            with dve.Fori(0, NT) as i:
                nc.vector.tensor_scalar(x_norm[:, i, :], x_tok[:, i, :], mean_var[:, i, 0:1], rstd[:, bass.ds(i, 1)],
                                        ALU.subtract, ALU.mult).then_inc(ln.norm_ready, 1)
            for bank in range(2 * NB):
                emit("vector", dve, bank, psum_t, ln.transposed, tiles_before + TPB * (bank % NB + 1))

        @block.scalar
        def _(act):
            act.wait_ge(ln.var_eps_ready, steps_before + 1)
            nc.scalar.activation(std[:], std[:], ACT.Sqrt).then_inc(ln.std_ready, 1)
            for bank in range(2 * NB):
                emit("scalar", act, bank, psum_t, ln.transposed, tiles_before + TPB * (bank % NB + 1))

        @block.gpsimd
        def _(pool):
            if pool_work:
                pool_work(pool)

        @block.tensor
        def _(pe):
            for i in range(NT):
                pe.wait_ge(ln.norm_ready, tiles_before + i + 1)
                nc.tensor.transpose(psum_t[:, 0, bass.ts(i, P)], x_norm[:, i, 0:P], ident[:])
                nc.tensor.transpose(psum_t[:, 1, bass.ts(i, P)], x_norm[:, i, P:D],
                                    ident[:]).then_inc(ln.transposed, 1)


def time_mix(nc, w, x_tok, ident, ln):
    with ExitStack() as ctx:
        def alloc(name, shape, dt):
            return ctx.enter_context(nc.sbuf_tensor(name, shape, dt))

        def semaphore(name):
            return ctx.enter_context(nc.semaphore(name))

        NM = 5
        RL = 64
        H, K, V = 16, 8, 8
        OUT_W = [P, RL, P, P, RL]
        shifted = alloc("tm_x_shifted", [P, NC, T + 1], F32)
        wx1 = alloc("tm_wx1", [P, NC, NM * RL], F32)
        wx2 = alloc("tm_wx2", [P, 3, D], F32)
        proj = alloc("tm_proj", [P, NC, sum(OUT_W)], F32)
        wwb = alloc("tm_wwb", [RL, P], F32)
        wgb = alloc("tm_wgb", [RL, P], F32)
        wo = alloc("tm_wo", [P, D], F32)
        cols = alloc("tm_cols", [P, 17], F32)
        spread = alloc("tm_spread", [P, V, P], F32)
        gather = alloc("tm_gather", [P, V, P], F32)
        heads = alloc("tm_heads", [P, P], F32)
        rT = alloc("tm_r", [P, T], F32)
        kT = alloc("tm_k", [P, T], F32)
        vT = alloc("tm_v", [P, T], F32)
        decay = alloc("tm_decay", [P, T], F32)
        gT = alloc("tm_g", [P, T], F32)
        oT = alloc("tm_o", [P, T], F32)
        MU, XB, BW, BG, BONUS, LNW, LNB = 0, 2, 12, 13, 14, 15, 16

        weights_loaded = semaphore("tm_weights_loaded")
        N_LOADS = 15
        with ExitStack() as inner:
            x_norm = inner.enter_context(nc.sbuf_tensor("tm_x_norm", [P, NT, D], F32))
            psum_t = inner.enter_context(nc.psum_tensor("tm_psum_t", [P, NC, T], F32))
            zeroed = semaphore("tm_zeroed")
            copied = semaphore("tm_copied")

            with nc.Block() as block:
                @block.sync
                def _(sp):
                    for dst, src in (
                        (wx1[:], w["L0_attn_Wx1"].rearrange("(c p) n -> p c n", p=P)),
                        (wx2[:, 0:2, :], w["Wx2T"][0:2 * P].rearrange("(c p) n -> p c n", p=P)),
                        (wx2[0:RL, 2, :], w["Wx2T"][2 * P:NM * RL]),
                        (proj[:], w["tm_proj"].rearrange("(c p) n -> p c n", p=P)),
                        (wwb[:], w["L0_attn_Ww_b"]),
                        (wgb[:], w["L0_attn_Wg_b"]),
                        (wo[:], w["L0_attn_Wo"]),
                        (cols[:], w["tm_cols"]),
                        (spread[:], w["c_spread"]),
                        (gather[:], w["c_gather"]),
                        (heads[:], w["c_heads"]),
                    ):
                        sp.dma_start(dst, src).then_inc(weights_loaded, 16)
                    sp.wait_ge(weights_loaded, 16 * 11)

                @block.vector
                def _(dve):
                    nc.vector.memset(shifted[:, :, 0:1], 0.0).then_inc(zeroed, 1)

            def emit(name, eng, bank, psum_t, transposed, value):
                c, b = divmod(bank, NB)
                if (bank % 2 == 0) != (name == "vector"):
                    return
                eng.wait_ge(transposed, value)
                dst, src = shifted[:, c, 1 + b * BT:1 + (b + 1) * BT], psum_t[:, c, bass.ts(b, BT)]
                if name == "vector":
                    nc.vector.tensor_copy(dst, src).then_inc(copied, 1)
                else:
                    nc.scalar.activation(dst, src, ACT.Copy).then_inc(copied, 1)

            layer_norm_tokens(nc, ln, lambda n, s, d: inner.enter_context(nc.sbuf_tensor(n, s, d)), "tm_ln", x_tok, ident, x_norm, psum_t, emit)

        with ExitStack() as inner:
            def sb(name, shape):
                return inner.enter_context(nc.sbuf_tensor(name, shape, F32))

            def ps(name, shape):
                return inner.enter_context(nc.psum_tensor(name, shape, F32))

            delta = sb("tm_delta", [P, NC, BT])
            x_mu = sb("tm_x_mu", [P, NC, BT])
            lr = sb("tm_lr", [P, 3, BT])
            mixed = sb("tm_mixed", [P, 2, NC, BT])
            low = sb("tm_low", [RL, 2, BT])
            exp_w = sb("tm_exp_w", [P, BT])
            psum_lr = ps("tm_psum_lr", [P, 3, BT])
            psum_mu = ps("tm_psum_mu", [P, NC, BT])
            psum_proj = ps("tm_psum_proj", [P, 2, BT])
            psum_up = ps("tm_psum_up", [P, BT])
            delta_ready = semaphore("tm_delta_ready")
            x_mu_ready = semaphore("tm_x_mu_ready")
            lr_psum_ready = semaphore("tm_lr_psum_ready")
            lr_ready = semaphore("tm_lr_ready")
            mu_psum_ready = semaphore("tm_mu_psum_ready")
            moved_ready = semaphore("tm_moved_ready")
            mixed_ready = semaphore("tm_mixed_ready")
            proj_psum_ready = semaphore("tm_proj_psum_ready")
            proj_out = semaphore("tm_proj_out")
            up_psum_ready = semaphore("tm_up_psum_ready")
            exp_w_ready = semaphore("tm_exp_w_ready")
            up_out = semaphore("tm_up_out")

            with nc.Block() as block:
                @block.vector
                def _(dve):
                    with dve.Fori(0, NB) as b:
                        now = shifted[:, :, bass.ds(b * BT + 1, BT)]
                        before = shifted[:, :, bass.ds(b * BT, BT)]
                        nc.vector.tensor_tensor(delta[:], before, now, ALU.subtract).then_inc(delta_ready, 1)
                        dve.wait_ge(delta_ready, b + 1)
                        for c in range(NC):
                            nc.vector.scalar_tensor_tensor(
                                x_mu[:, c, :], delta[:, c, :], cols[:, MU + c:MU + c + 1],
                                shifted[:, c, bass.ds(b * BT + 1, BT)], ALU.mult, ALU.add).then_inc(x_mu_ready, 1)
                        for n in range(NM):
                            for c in range(NC):
                                col = XB + 2 * n + c
                                dve.wait_ge(mu_psum_ready, b * NM * NC + n * NC + c + 1)
                                if n >= 2:
                                    dve.wait_ge(proj_psum_ready, b * NM + n - 1)
                                nc.vector.scalar_tensor_tensor(
                                    mixed[:, n % 2, c, :], psum_mu[:, c, :], cols[:, col:col + 1], delta[:, c, :],
                                    ALU.add, ALU.mult).then_inc(moved_ready, 1)
                                dve.wait_ge(moved_ready, b * NM * NC + n * NC + c + 1)
                                nc.vector.tensor_tensor(mixed[:, n % 2, c, :], mixed[:, n % 2, c, :],
                                                        shifted[:, c, bass.ds(b * BT + 1, BT)],
                                                        ALU.add).then_inc(mixed_ready, 1)
                        dve.wait_ge(proj_psum_ready, b * NM + NM)

                @block.scalar
                def _(act):
                    with act.Fori(0, NB) as b:
                        tok = bass.ts(b, BT)
                        act.wait_ge(lr_psum_ready, b + 1)
                        nc.scalar.activation(lr[:, 0:2, :], psum_lr[:, 0:2, :], ACT.Tanh).then_inc(lr_ready, 1)
                        nc.scalar.activation(lr[0:RL, 2, :], psum_lr[0:RL, 2, :], ACT.Tanh).then_inc(lr_ready, 1)
                        for n in range(NM):
                            act.wait_ge(proj_psum_ready, b * NM + n + 1)
                            src = psum_proj[0:OUT_W[n], n % 2, :]
                            if OUT_W[n] == RL:
                                nc.scalar.activation(low[:, n // 4, :], src, ACT.Tanh).then_inc(proj_out, 1)
                            else:
                                dst = {0: rT, 2: kT, 3: vT}[n]
                                nc.scalar.activation(dst[:, tok], src, ACT.Copy).then_inc(proj_out, 1)
                            if n == 1:
                                act.wait_ge(up_psum_ready, 2 * b + 1)
                                nc.scalar.activation(exp_w[:], psum_up[:], ACT.Exp,
                                                     bias=cols[:, BW:BW + 1]).then_inc(exp_w_ready, 1)
                                act.wait_ge(exp_w_ready, b + 1)
                                nc.scalar.activation(decay[:, tok], exp_w[:], ACT.Exp, scale=-1.0).then_inc(up_out, 1)
                            if n == 4:
                                act.wait_ge(up_psum_ready, 2 * b + 2)
                                nc.scalar.activation(gT[:, tok], psum_up[:], ACT.Identity,
                                                     bias=cols[:, BG:BG + 1]).then_inc(up_out, 1)

                @block.tensor
                def _(pe):
                    with pe.Fori(0, NB) as b:
                        for c in range(NC):
                            pe.wait_ge(x_mu_ready, b * NC + c + 1)
                            for m, width in enumerate((P, P, RL)):
                                last = nc.tensor.matmul(psum_lr[0:width, m, :], wx1[:, c, m * P:m * P + width],
                                                        x_mu[:, c, :], start=(c == 0), stop=(c == NC - 1))
                        last.then_inc(lr_psum_ready, 1)
                        pe.wait_ge(lr_ready, 2 * b + 2)
                        off = 0

                        def mixing(n):
                            chunk, row = divmod(n * RL, P)
                            for c in range(NC):
                                if n >= 1:
                                    pe.wait_ge(moved_ready, b * NM * NC + (n - 1) * NC + c + 1)
                                nc.tensor.matmul(psum_mu[:, c, :], wx2[row:row + RL, chunk, bass.ts(c, P)],
                                                 lr[row:row + RL, chunk, :], start=True, stop=True
                                                 ).then_inc(mu_psum_ready, 1)

                        mixing(0)
                        for n in range(NM):
                            if n + 1 < NM:
                                mixing(n + 1)
                            if n >= 2:
                                pe.wait_ge(proj_out, b * NM + n - 1)
                            for c in range(NC):
                                pe.wait_ge(mixed_ready, b * NM * NC + n * NC + c + 1)
                                last = nc.tensor.matmul(psum_proj[0:OUT_W[n], n % 2, :], proj[:, c, off:off + OUT_W[n]],
                                                        mixed[:, n % 2, c, :], start=(c == 0), stop=(c == NC - 1))
                            last.then_inc(proj_psum_ready, 1)
                            off += OUT_W[n]
                            if n in (1, 4):
                                pe.wait_ge(proj_out, b * NM + n + 1)
                                if n == 4:
                                    pe.wait_ge(exp_w_ready, b + 1)
                                nc.tensor.matmul(psum_up[:], (wwb, wgb)[n // 4][:], low[:, n // 4, :],
                                                 start=True, stop=True).then_inc(up_psum_ready, 1)
                        pe.wait_ge(proj_out, b * NM + NM)
                        pe.wait_ge(up_out, 2 * b + 2)

        with ExitStack() as inner:
            def sb(name, shape):
                return inner.enter_context(nc.sbuf_tensor(name, shape, F32))

            def ps(name, shape):
                return inner.enter_context(nc.psum_tensor(name, shape, F32))

            kv = sb("tm_kv", [P, 2, T])
            state = sb("tm_state", [P, 2, T + 1])
            read = sb("tm_read", [P, 2, T])
            rk = sb("tm_rk", [P, T])
            own = sb("tm_own", [P, T])
            psum_o = ps("tm_psum_o", [P, T])
            psum_v = ps("tm_psum_v", [P, 2, BT])
            psum_rk = ps("tm_psum_rk", [P, 2, BT])
            rk_ready = semaphore("tm_rk_ready")
            v_spread = semaphore("tm_v_spread")
            kv_ready = semaphore("tm_kv_ready")
            state_zero = semaphore("tm_state_zero")
            scanned = semaphore("tm_scanned")
            read_ready = semaphore("tm_read_ready")
            o_summed = semaphore("tm_o_summed")
            rk_summed = semaphore("tm_rk_summed")
            own_ready = semaphore("tm_own_ready")
            o_ready = semaphore("tm_o_ready")

            with nc.Block() as block:
                @block.tensor
                def _(pe):
                    def spread_v(v):
                        for b in range(NB):
                            n = v * NB + b
                            if b >= 2:
                                pe.wait_ge(kv_ready, n - 1)
                            elif not isinstance(v, int) or v > 0:
                                pe.wait_ge(kv_ready, n - 1)
                            nc.tensor.matmul(psum_v[:, b % 2, :], spread[:, v, :], vT[:, bass.ts(b, BT)],
                                             start=True, stop=True).then_inc(v_spread, 1)

                    def sum_o(v, first, last):
                        pe.wait_ge(read_ready, v + 1)
                        for b in range(NB):
                            mm = nc.tensor.matmul(psum_o[:, bass.ts(b, BT)], gather[:, v, :],
                                                  read[:, v % 2, bass.ts(b, BT)], start=first, stop=last)
                        mm.then_inc(o_summed, 1)

                    spread_v(0)
                    for v in range(1, V):
                        spread_v(v)
                        sum_o(v - 1, v == 1, False)
                    pe.wait_ge(rk_ready, 1)
                    for b in range(NB):
                        if b >= 2:
                            pe.wait_ge(own_ready, b - 1)
                        nc.tensor.matmul(psum_rk[:, b % 2, :], heads[:], rk[:, bass.ts(b, BT)],
                                         start=True, stop=True).then_inc(rk_summed, 1)
                    sum_o(V - 1, False, True)

                @block.gpsimd
                def _(pool):
                    for v in range(V):
                        pool.wait_ge(scanned, v + 1)
                        if v >= 2:
                            pool.wait_ge(o_summed, v - 1)
                        nc.gpsimd.tensor_tensor(read[:, v % 2, :], rT[:], state[:, v % 2, 0:T],
                                                ALU.mult).then_inc(read_ready, 1)

                @block.vector
                def _(dve):
                    for j in range(2):
                        nc.vector.memset(state[:, j, 0:1], 0.0).then_inc(state_zero, 1)
                    nc.vector.scalar_tensor_tensor(rk[:], rT[:], cols[:, BONUS:BONUS + 1], kT[:],
                                                   ALU.mult, ALU.mult).then_inc(rk_ready, 1)
                    dve.wait_ge(state_zero, 2)
                    for v in range(V):
                        for b in range(NB):
                            dve.wait_ge(v_spread, v * NB + b + 1)
                            if v >= 2:
                                dve.wait_ge(scanned, v - 1)
                            nc.vector.tensor_tensor(kv[:, v % 2, bass.ts(b, BT)], psum_v[:, b % 2, :],
                                                    kT[:, bass.ts(b, BT)], ALU.mult).then_inc(kv_ready, 1)
                        dve.wait_ge(kv_ready, (v + 1) * NB)
                        if v >= 2:
                            dve.wait_ge(read_ready, v - 1)
                        nc.vector.tensor_tensor_scan(state[:, v % 2, 1:T + 1], decay[:], kv[:, v % 2, :], 0.0,
                                                     ALU.mult, ALU.add).then_inc(scanned, 1)
                    for b in range(NB):
                        dve.wait_ge(rk_summed, b + 1)
                        nc.vector.tensor_tensor(own[:, bass.ts(b, BT)], psum_rk[:, b % 2, :], vT[:, bass.ts(b, BT)],
                                                ALU.mult).then_inc(own_ready, 1)
                    dve.wait_ge(own_ready, NB)
                    dve.wait_ge(o_summed, V)
                    nc.vector.tensor_tensor(oT[:], psum_o[:], own[:], ALU.add).then_inc(o_ready, 1)

        with ExitStack() as inner:
            def sb(name, shape):
                return inner.enter_context(nc.sbuf_tensor(name, shape, F32))

            def ps(name, shape):
                return inner.enter_context(nc.psum_tensor(name, shape, F32))

            centred = sb("tm_centred", [P, T])
            square = sb("tm_square", [P, T])
            std = sb("tm_gn_std", [P, T])
            sig = sb("tm_sig", [P, T])
            gate = sb("tm_gate", [P, T])
            psum_s = ps("tm_psum_s", [P, NB, BT])
            psum_x = ps("tm_psum_x", [P, 4, BT])
            sums_ready = semaphore("tm_sums_ready")
            centred_ready = semaphore("tm_centred_ready")
            square_ready = semaphore("tm_square_ready")
            squares_summed = semaphore("tm_squares_summed")
            var_ready = semaphore("tm_var_ready")
            std_ready = semaphore("tm_gn_std_ready")
            sig_ready = semaphore("tm_sig_ready")
            gate_ready = semaphore("tm_gate_ready")
            norm_steps = semaphore("tm_norm_steps")
            z_ready = semaphore("tm_z_ready")
            wo_done = semaphore("tm_wo_done")
            added = semaphore("tm_added")

            with nc.Block() as block:
                @block.tensor
                def _(pe):
                    for b in range(NB):
                        nc.tensor.matmul(psum_s[:, b, :], heads[:], oT[:, bass.ts(b, BT)],
                                         start=True, stop=True).then_inc(sums_ready, 1)
                    for b in range(NB):
                        pe.wait_ge(centred_ready, b + 1)
                        pe.wait_ge(square_ready, b + 1)
                        nc.tensor.matmul(psum_s[:, b, :], heads[:], square[:, bass.ts(b, BT)],
                                         start=True, stop=True).then_inc(squares_summed, 1)
                    for g in range(NT // 4):
                        pe.wait_ge(z_ready, g + 1)
                        for j in range(4):
                            nc.tensor.matmul(psum_x[:, j, 0:D], oT[:, bass.ds(g * BT + j * P, P)], wo[:],
                                             start=True, stop=True).then_inc(wo_done, 1)
                        pe.wait_ge(added, g * 4 + 4)

                @block.scalar
                def _(act):
                    nc.scalar.activation(sig[:], gT[:], ACT.Sigmoid).then_inc(sig_ready, 1)
                    for b in range(NB):
                        act.wait_ge(centred_ready, b + 1)
                        nc.scalar.activation(square[:, bass.ts(b, BT)], centred[:, bass.ts(b, BT)],
                                             ACT.Square).then_inc(square_ready, 1)
                    for b in range(NB):
                        act.wait_ge(var_ready, b + 1)
                        nc.scalar.activation(std[:, bass.ts(b, BT)], std[:, bass.ts(b, BT)],
                                             ACT.Sqrt).then_inc(std_ready, 1)

                @block.gpsimd
                def _(pool):
                    pool.wait_ge(sig_ready, 1)
                    nc.gpsimd.tensor_tensor(gate[:], sig[:], gT[:], ALU.mult).then_inc(gate_ready, 1)

                @block.vector
                def _(dve):
                    for b in range(NB):
                        dve.wait_ge(sums_ready, b + 1)
                        nc.vector.scalar_tensor_tensor(centred[:, bass.ts(b, BT)], psum_s[:, b, :], -1.0 / V,
                                                       oT[:, bass.ts(b, BT)], ALU.mult, ALU.add
                                                       ).then_inc(centred_ready, 1)
                    for b in range(NB):
                        dve.wait_ge(squares_summed, b + 1)
                        nc.vector.tensor_scalar(std[:, bass.ts(b, BT)], psum_s[:, b, :], 1.0 / V, EPS,
                                                ALU.mult, ALU.add).then_inc(var_ready, 1)
                    dve.wait_ge(gate_ready, 1)
                    for b in range(NB):
                        tok = bass.ts(b, BT)
                        dve.wait_ge(std_ready, b + 1)
                        nc.vector.reciprocal(std[:, tok], std[:, tok]).then_inc(norm_steps, 1)
                        dve.wait_ge(norm_steps, 3 * b + 1)
                        nc.vector.tensor_tensor(centred[:, tok], centred[:, tok], std[:, tok],
                                                ALU.mult).then_inc(norm_steps, 1)
                        dve.wait_ge(norm_steps, 3 * b + 2)
                        nc.vector.tensor_scalar(centred[:, tok], centred[:, tok], cols[:, LNW:LNW + 1],
                                                cols[:, LNB:LNB + 1], ALU.mult, ALU.add).then_inc(norm_steps, 1)
                        dve.wait_ge(norm_steps, 3 * b + 3)
                        nc.vector.tensor_tensor(oT[:, tok], centred[:, tok], gate[:, tok],
                                                ALU.mult).then_inc(z_ready, 1)
                    with dve.Fori(0, NT // 4) as g:
                        for j in range(4):
                            dve.wait_ge(wo_done, g * 4 + j + 1)
                            xt = x_tok[:, bass.ds(g * 4 + j, 1), :].rearrange("p a d -> p (a d)")
                            nc.vector.tensor_tensor(xt, psum_x[:, j, 0:D], xt, ALU.add).then_inc(added, 1)


def copy_banks(nc, dst, copied):
    def emit(name, eng, bank, psum_t, transposed, value):
        if (bank % 2 == 0) != (name == "vector"):
            return
        c, b = divmod(bank, NB)
        eng.wait_ge(transposed, value)
        to, of = dst[:, c, bass.ts(b, BT)], psum_t[:, c, bass.ts(b, BT)]
        if name == "vector":
            nc.vector.tensor_copy(to, of).then_inc(copied, 1)
        else:
            nc.scalar.activation(to, of, ACT.Copy).then_inc(copied, 1)
    return emit


def choose_largest(nc, dve, steps, p, order, top, hit, rank, best):
    def after(instruction):
        dve.wait_ge(steps.sem, steps.add(instruction))

    E = p.shape[-1]
    wide = [P, NT, E]
    after(nc.vector.tensor_reduce(top, p, AX.X, ALU.max))
    after(nc.vector.tensor_tensor(rank, p, top.unsqueeze(2).to_broadcast(wide), ALU.is_equal))
    after(nc.vector.tensor_tensor(rank, rank, order.unsqueeze(1).to_broadcast(wide), ALU.mult))
    after(nc.vector.tensor_reduce(best, rank, AX.X, ALU.max))
    after(nc.vector.tensor_tensor(hit, rank, best.unsqueeze(2).to_broadcast(wide), ALU.is_equal))


def copy_split(nc, hi, lo, hi_copied, lo_copied):
    def emit(name, eng, bank, psum_t, transposed, value):
        c, b = divmod(bank, NB)
        src = psum_t[:, c, bass.ts(b, BT)]
        hi_part, lo_part = hi[:, c, bass.ts(b, BT)], lo[:, c, bass.ts(b, BT)]
        if name == "scalar":
            eng.wait_ge(transposed, value)
            nc.scalar.activation(hi_part, src, ACT.Copy).then_inc(hi_copied, 1)
        else:
            eng.wait_ge(hi_copied, bank + 1)
            nc.vector.tensor_tensor(lo_part, src, hi_part.bitcast(F32), ALU.subtract).then_inc(lo_copied, 1)
    return emit


def three(nc, out, a_hi, a_lo, b_hi, b_lo, start=True, stop=True, **kw):
    nc.tensor.matmul(out, a_hi, b_hi, start=start, stop=False, **kw)
    nc.tensor.matmul(out, a_hi, b_lo, start=False, stop=False, **kw)
    return nc.tensor.matmul(out, a_lo, b_hi, start=False, stop=stop, **kw)


def lora_ffn(nc, w, x_tok, ident, ln):
    E, R, F = 8, 16, 1024
    NF = F // P
    SCALING = 2.0
    ER = E * R
    NQ = 4 * E
    with ExitStack() as ctx:
        def alloc(name, shape, dt=F32):
            return ctx.enter_context(nc.sbuf_tensor(name, shape, dt))

        def semaphore(name):
            return ctx.enter_context(nc.semaphore(name))

        x_hi, x_lo = alloc("lf_x_hi", [P, NC, T], F32R), alloc("lf_x_lo", [P, NC, T], F32R)
        w1_hi, w1_lo = alloc("lf_w1_hi", [P, NC, F], F32R), alloc("lf_w1_lo", [P, NC, F], F32R)
        b1t_hi, b1t_lo = alloc("lf_B1T_hi", [P, F], F32R), alloc("lf_B1T_lo", [P, F], F32R)
        ra_hi, ra_lo = alloc("lf_ra_hi", [P, NC, E + ER], F32R), alloc("lf_ra_lo", [P, NC, E + ER], F32R)
        b1 = alloc("lf_b1", [P, NF])
        w2 = alloc("lf_w2", [P, NF, D])
        a2t = alloc("lf_A2T", [P, NF, ER])
        b2t = alloc("lf_B2T", [P, D])
        b2 = alloc("lf_b2", [P, D])
        low_hi = alloc("lf_low_hi", [P, 2, T], F32R)
        low_lo = alloc("lf_low_lo", [P, 2, T], F32R)
        hits = alloc("lf_hits", [P, 2, T])
        weights = alloc("lf_weights", [P, 2, T])
        wsum = alloc("lf_wsum", [P, NT])
        loaded = semaphore("lf_loaded")
        hi_copied = semaphore("lf_hi_copied")
        lo_copied = semaphore("lf_lo_copied")
        split_steps = semaphore("lf_split_steps")

        with ExitStack() as stage:
            def st(name, shape, dt=F32):
                return stage.enter_context(nc.sbuf_tensor(name, shape, dt))

            br, order = st("lf_br", [P, E]), st("lf_order", [P, E])
            choose = st("lf_choose", [NQ, 3, P])
            choose_r = st("lf_choose_r", [NQ, 3, P], F32R)
            weigh = st("lf_weigh", [NQ, 2, P])
            with ExitStack() as inner:
                def sb(name, shape, dt=F32):
                    return inner.enter_context(nc.sbuf_tensor(name, shape, dt))

                x_norm = sb("lf_x_norm", [P, NT, D])
                router_a1 = sb("lf_router_a1", [P, NC, E + ER])
                w1 = sb("lf_w1", [P, NC, F])
                b1t = sb("lf_B1T", [P, F])
                psum_t = inner.enter_context(nc.psum_tensor("lf_psum_t", [P, NC, T], F32))
                loads = (
                    (router_a1[:], w["lf_router_a1"].rearrange("(c p) n -> p c n", p=P)),
                    (w1[:], w["L0_ffn_W1"].rearrange("(c p) n -> p c n", p=P)),
                    (b1t[:], w["lf_B1T"]),
                    (choose[:], w["c_choose"]),
                    (weigh[:], w["c_weigh"]),
                    (b1[:], w["lf_b1"]),
                    (w2[:], w["L0_ffn_W2"].rearrange("(c p) n -> p c n", p=P)),
                    (a2t[:], w["lf_A2T"].rearrange("(c p) n -> p c n", p=P)),
                    (b2t[:], w["lf_B2T"]),
                    (br[:], w["lf_br"][0, :].partition_broadcast(P)),
                    (b2[:], w["lf_b2"][0, :].partition_broadcast(P)),
                    (order[:], w["c_order"][0, :].partition_broadcast(P)),
                )

                def split_weights(pool):
                    pool.wait_ge(loaded, 16 * len(loads))
                    for n, (hi, lo, whole) in enumerate(((ra_hi, ra_lo, router_a1), (w1_hi, w1_lo, w1),
                                                         (b1t_hi, b1t_lo, b1t))):
                        nc.gpsimd.tensor_copy(hi[:], whole[:]).then_inc(split_steps, 1)
                        pool.wait_ge(split_steps, 2 * n + 1)
                        nc.gpsimd.tensor_tensor(lo[:], whole[:], hi[:].bitcast(F32), ALU.subtract).then_inc(split_steps, 1)
                    nc.gpsimd.tensor_copy(choose_r[:], choose[:]).then_inc(split_steps, 1)

                layer_norm_tokens(nc, ln, sb, "lf_ln", x_tok, ident, x_norm, psum_t,
                                  copy_split(nc, x_hi, x_lo, hi_copied, lo_copied), loads, loaded, split_weights)

            with ExitStack() as inner:
                def sb(name, shape, dt=F32):
                    return inner.enter_context(nc.sbuf_tensor(name, shape, dt))

                prob = sb("lf_prob", [P, NT, E])
                rest = sb("lf_rest", [P, NT, E])
                chosen = sb("lf_chosen", [P, NT, NQ])
                chosenT, chosenT_r = sb("lf_chosenT", [NQ, T]), sb("lf_chosenT_r", [NQ, T], F32R)
                weight = sb("lf_weight", [P, 2, NT])
                rank = sb("lf_rank", [P, NT, E])
                best = sb("lf_best", [P, NT])
                total = sb("lf_total", [P, NT])
                t1_hi, t1_lo = sb("lf_t1_hi", [P, T], F32R), sb("lf_t1_lo", [P, T], F32R)
                banks = inner.enter_context(nc.psum_tensor("lf_banks", [P, 8, BT], F32))
                logits = banks[:, 0, 0:NT * E].rearrange("p (i e) -> p i e", e=E)
                logits_ready = semaphore("lf_logits_ready")
                shifted_ready = semaphore("lf_shifted_ready")
                exp_ready = semaphore("lf_exp_ready")
                chain = semaphore("lf_chain")
                t1_psum = semaphore("lf_t1_psum")
                t1_hi_ready = semaphore("lf_t1_hi_ready")
                t1_lo_ready = semaphore("lf_t1_lo_ready")
                chosen_ready = semaphore("lf_chosen_ready")
                chosen_psum = semaphore("lf_chosen_psum")
                chosen_copied = semaphore("lf_chosen_copied")
                spread_psum = semaphore("lf_spread_psum")
                spread_copied = semaphore("lf_spread_copied")
                low_steps = semaphore("lf_low_steps")

                def Q_BANK(b):
                    return (5 + b) % 8

                with nc.Block() as block:
                    @block.tensor
                    def _(pe):
                        for i in range(NT):
                            for c in range(NC):
                                last = three(nc, logits[:, i, :], x_hi[:, c, bass.ts(i, P)], x_lo[:, c, bass.ts(i, P)],
                                             ra_hi[:, c, 0:E], ra_lo[:, c, 0:E], start=(c == 0), stop=(c == NC - 1))
                        last.then_inc(logits_ready, 1)
                        for b in range(NB):
                            for c in range(NC):
                                last = three(nc, banks[:, 1 + b, :], ra_hi[:, c, E:E + ER], ra_lo[:, c, E:E + ER],
                                             x_hi[:, c, bass.ts(b, BT)], x_lo[:, c, bass.ts(b, BT)],
                                             start=(c == 0), stop=(c == NC - 1))
                            last.then_inc(t1_psum, 1)
                        pe.wait_ge(chosen_ready, 1)
                        for b in range(NB):
                            for j in range(TPB):
                                last = nc.tensor.transpose(banks[0:NQ, Q_BANK(b), bass.ts(j, P)],
                                                           chosen[:, b * TPB + j, :], ident[:])
                            last.then_inc(chosen_psum, 1)
                        pe.wait_ge(t1_lo_ready, NB)
                        for b in range(NB):
                            tok = bass.ts(b, BT)
                            pe.wait_ge(chosen_copied, 2 * b + 2)
                            for k in range(5):
                                n = 5 * b + k
                                if n == 4:
                                    pe.wait_ge(chosen_copied, 2 * NB)
                                if n >= 8:
                                    ob, ok = divmod(n - 8, 5)
                                    if ok == 2:
                                        pe.wait_ge(low_steps, 4 * ob + 4)
                                    else:
                                        pe.wait_ge(spread_copied, 4 * ob + (ok + 1 if ok < 2 else ok))
                                out = banks[:, (1 + n) % 8, :]
                                if k < 3:
                                    last = nc.tensor.matmul(out, choose_r[:, k, :], chosenT_r[:, tok], start=True, stop=True)
                                else:
                                    last = nc.tensor.matmul(out, weigh[:, k - 3, :], chosenT[:, tok], start=True, stop=True)
                                last.then_inc(spread_psum, 1)

                    @block.scalar
                    def _(act):
                        act.wait_ge(shifted_ready, 1)
                        nc.scalar.activation(prob[:], prob[:], ACT.Exp).then_inc(exp_ready, 1)
                        for b in range(NB):
                            act.wait_ge(t1_psum, b + 1)
                            nc.scalar.activation(t1_hi[:, bass.ts(b, BT)], banks[:, 1 + b, :], ACT.Copy,
                                                 scale=SCALING).then_inc(t1_hi_ready, 1)
                        for b in range(NB):
                            tok = bass.ts(b, BT)
                            act.wait_ge(chosen_psum, b + 1)
                            for dst in (chosenT, chosenT_r):
                                nc.scalar.activation(dst[:, tok], banks[0:NQ, Q_BANK(b), :],
                                                     ACT.Copy).then_inc(chosen_copied, 1)
                        for b in range(NB):
                            for k in (0, 1, 3, 4):
                                n = 5 * b + k
                                act.wait_ge(spread_psum, n + 1)
                                dst = (hits, hits, None, weights, weights)[k]
                                nc.scalar.activation(dst[:, (0, 1, None, 0, 1)[k], bass.ts(b, BT)],
                                                     banks[:, (1 + n) % 8, :], ACT.Copy).then_inc(spread_copied, 1)

                    @block.vector
                    def _(dve):
                        steps = Steps(chain)

                        def after(instruction):
                            dve.wait_ge(steps.sem, steps.add(instruction))

                        wide = [P, NT, E]
                        hit = [chosen[:, :, j * E:(j + 1) * E] for j in range(2)]
                        dve.wait_ge(logits_ready, 1)
                        after(nc.vector.tensor_tensor(prob[:], logits, br[:].unsqueeze(1).to_broadcast(wide), ALU.add))
                        after(nc.vector.tensor_reduce(best[:], prob[:], AX.X, ALU.max))
                        nc.vector.tensor_tensor(prob[:], prob[:], best[:].unsqueeze(2).to_broadcast(wide),
                                                ALU.subtract).then_inc(shifted_ready, 1)
                        dve.wait_ge(exp_ready, 1)
                        after(nc.vector.tensor_reduce(total[:], prob[:], AX.X, ALU.add))
                        after(nc.vector.reciprocal(total[:], total[:]))
                        after(nc.vector.tensor_tensor(prob[:], prob[:], total[:].unsqueeze(2).to_broadcast(wide),
                                                      ALU.mult))
                        choose_largest(nc, dve, steps, prob[:], order[:], weight[:, 0, :], hit[0], rank[:], best[:])
                        after(nc.vector.scalar_tensor_tensor(rest[:], hit[0], -2.0, prob[:], ALU.mult, ALU.add))
                        choose_largest(nc, dve, steps, rest[:], order[:], weight[:, 1, :], hit[1], rank[:], best[:])
                        nc.vector.tensor_tensor(wsum[:], weight[:, 0, :], weight[:, 1, :], ALU.add)
                        for j in range(2):
                            last = nc.vector.tensor_tensor(chosen[:, :, (2 + j) * E:(3 + j) * E], hit[j],
                                                           weight[:, j, :].unsqueeze(2).to_broadcast(wide), ALU.mult)
                        last.then_inc(chosen_ready, 1)
                        for b in range(NB):
                            tok = bass.ts(b, BT)
                            dve.wait_ge(t1_hi_ready, b + 1)
                            nc.vector.scalar_tensor_tensor(t1_lo[:, tok], banks[:, 1 + b, :], SCALING,
                                                           t1_hi[:, tok].bitcast(F32), ALU.mult,
                                                           ALU.subtract).then_inc(t1_lo_ready, 1)
                        dve.wait_ge(t1_lo_ready, NB)
                        parts = ((low_hi, t1_hi), (low_lo, t1_lo))
                        for b in range(NB):
                            tok = bass.ts(b, BT)
                            dve.wait_ge(spread_copied, 4 * b + 1)
                            for dst, src in parts:
                                nc.vector.tensor_tensor(dst[:, 0, tok], src[:, tok].bitcast(F32), hits[:, 0, tok],
                                                        ALU.mult).then_inc(low_steps, 1)
                            dve.wait_ge(spread_psum, 5 * b + 3)
                            for dst, src in parts:
                                nc.vector.tensor_tensor(dst[:, 1, tok], src[:, tok].bitcast(F32),
                                                        banks[:, (1 + 5 * b + 2) % 8, :], ALU.mult).then_inc(low_steps, 1)

        with ExitStack() as inner:
            def sb(name, shape, dt=F32):
                return inner.enter_context(nc.sbuf_tensor(name, shape, dt))

            def ps(name, shape):
                return inner.enter_context(nc.psum_tensor(name, shape, F32))

            hidden = sb("lf_hidden", [P, 2, NF, BT])
            mix = sb("lf_mix", [P, NF, BT])
            t2 = sb("lf_t2", [P, 2, BT])
            bias = sb("lf_bias", [P, 2, D])
            psum_h = ps("lf_psum_h", [P, 4, BT])
            psum_t2 = ps("lf_psum_t2", [P, 2, BT])
            psum_d = ps("lf_psum_d", [P, 2, BT])
            h_psum = semaphore("lf_h_psum")
            h_ready = semaphore("lf_h_ready")
            weighed = semaphore("lf_weighed")
            mixed = semaphore("lf_mixed")
            t2_psum = semaphore("lf_t2_psum")
            t2_steps = semaphore("lf_t2_steps")
            d_psum = semaphore("lf_d_psum")
            added = semaphore("lf_added")
            biased_rows = semaphore("lf_biased_rows")
            biased = semaphore("lf_biased")

            with nc.Block() as block:
                @block.gpsimd
                def _(pool):
                    for i in range(NT):
                        if i >= 2:
                            pool.wait_ge(biased, i - 1)
                        nc.gpsimd.tensor_scalar(bias[:, i % 2, :], b2[:], wsum[:, i:i + 1], None,
                                                ALU.mult).then_inc(biased_rows, 1)
                        pool.wait_ge(biased_rows, i + 1)
                        nc.gpsimd.tensor_tensor(x_tok[:, i, :], x_tok[:, i, :], bias[:, i % 2, :],
                                                ALU.add).then_inc(biased, 1)

                @block.tensor
                def _(pe):
                    with pe.Fori(0, NB) as b:
                        tok = bass.ts(b, BT)

                        def first(f):
                            if f >= 4:
                                pe.wait_ge(h_ready, b * 2 * NF + 2 * (f - 4) + 2)
                            for c in range(NC):
                                three(nc, psum_h[:, f % 4, :], w1_hi[:, c, bass.ts(f, P)], w1_lo[:, c, bass.ts(f, P)],
                                      x_hi[:, c, tok], x_lo[:, c, tok], start=(c == 0), stop=False)
                            three(nc, psum_h[:, f % 4, :], b1t_hi[:, bass.ts(f, P)], b1t_lo[:, bass.ts(f, P)],
                                  low_hi[:, 0, tok], low_lo[:, 0, tok], start=False).then_inc(h_psum, 1)

                        def second(f):
                            pe.wait_ge(h_ready, b * 2 * NF + 2 * f + 1)
                            three(nc, psum_h[:, f % 4, :], b1t_hi[:, bass.ts(f, P)], b1t_lo[:, bass.ts(f, P)],
                                  low_hi[:, 1, tok], low_lo[:, 1, tok], start=False,
                                  skip_group_check=True).then_inc(h_psum, 1)

                        def down_rank(f):
                            pe.wait_ge(weighed, b * 2 * NF + 2 * f + 2)
                            for j in range(2):
                                last = nc.tensor.matmul(psum_t2[:, j, :], a2t[:, f, :], hidden[:, j, f, :],
                                                        start=(f == 0), stop=(f == NF - 1))
                            return last

                        first(0)
                        for f in range(NF):
                            if f + 1 < NF:
                                first(f + 1)
                            second(f)
                            if f >= 2:
                                down_rank(f - 2)
                        down_rank(NF - 2)
                        down_rank(NF - 1).then_inc(t2_psum, 1)
                        for i in range(TPB):
                            if i >= 2:
                                pe.wait_ge(added, b * TPB + i - 1)
                            for f in range(NF):
                                if i == 0:
                                    pe.wait_ge(mixed, b * NF + f + 1)
                                nc.tensor.matmul(psum_d[:, i % 2, 0:D], mix[:, f, bass.ts(i, P)], w2[:, f, :],
                                                 start=(f == 0), stop=False)
                            if i == 0:
                                pe.wait_ge(t2_steps, b * 3 + 3)
                            nc.tensor.matmul(psum_d[:, i % 2, 0:D], t2[:, 0, bass.ts(i, P)], b2t[:],
                                             start=False, stop=True).then_inc(d_psum, 1)
                        pe.wait_ge(added, b * TPB + TPB)

                @block.scalar
                def _(act):
                    with act.Fori(0, NB) as b:
                        def gelu(n, f, j):
                            act.wait_ge(h_psum, b * 2 * NF + n + 1)
                            nc.scalar.activation(hidden[:, j, f, :], psum_h[:, f % 4, :], ACT.Gelu_apprx_tanh,
                                                 bias=b1[:, f:f + 1]).then_inc(h_ready, 1)

                        for f in range(NF):
                            gelu(0 if f == 0 else 2 * f - 1, f, 0)
                            gelu(2 * f + 2 if f + 1 < NF else 2 * NF - 1, f, 1)

                @block.vector
                def _(dve):
                    dve.wait_ge(biased, NT)
                    with dve.Fori(0, NB) as b:
                        tok = bass.ts(b, BT)
                        for f in range(NF):
                            for j in range(2):
                                dve.wait_ge(h_ready, b * 2 * NF + 2 * f + j + 1)
                                nc.vector.tensor_tensor(hidden[:, j, f, :], hidden[:, j, f, :], weights[:, j, tok],
                                                        ALU.mult).then_inc(weighed, 1)
                            dve.wait_ge(weighed, b * 2 * NF + 2 * f + 2)
                            nc.vector.tensor_tensor(mix[:, f, :], hidden[:, 0, f, :], hidden[:, 1, f, :],
                                                    ALU.add).then_inc(mixed, 1)
                        dve.wait_ge(t2_psum, b + 1)
                        for j in range(2):
                            nc.vector.scalar_tensor_tensor(t2[:, j, :], psum_t2[:, j, :], SCALING, hits[:, j, tok],
                                                           ALU.mult, ALU.mult).then_inc(t2_steps, 1)
                        dve.wait_ge(t2_steps, b * 3 + 2)
                        nc.vector.tensor_tensor(t2[:, 0, :], t2[:, 0, :], t2[:, 1, :], ALU.add).then_inc(t2_steps, 1)
                        for i in range(TPB):
                            row = x_tok[:, bass.ds(b * TPB + i, 1), :].rearrange("p a d -> p (a d)")
                            dve.wait_ge(d_psum, b * TPB + i + 1)
                            nc.vector.tensor_tensor(row, psum_d[:, i % 2, 0:D], row, ALU.add).then_inc(added, 1)


def attention(nc, w, x_tok, ident, ln):
    NH, HD = 16, 128
    SCALE = 1.0 / float(HD) ** 0.5
    BLK = 32
    NSC = P // BLK
    QT = T // P
    KT = T // P
    BQ = BT // P
    KPT = KT // BQ
    LAG = 5
    NPROB = 8
    with ExitStack() as ctx:
        def alloc(name, shape, dt=F32):
            return ctx.enter_context(nc.sbuf_tensor(name, shape, dt))

        def semaphore(name):
            return ctx.enter_context(nc.semaphore(name))

        x_hi = alloc("at_x_hi", [P, NC, T], F32R)
        x_lo = alloc("at_x_lo", [P, NC, T], F32R)
        cols = alloc("at_cols", [P, 3, NH])
        loaded = semaphore("at_loaded")
        hi_copied = semaphore("at_hi_copied")
        lo_copied = semaphore("at_lo_copied")

        with ExitStack() as inner:
            def sb(name, shape, dt=F32):
                return inner.enter_context(nc.sbuf_tensor(name, shape, dt))

            x_norm = sb("at_x_norm", [P, NT, D])
            wo_codes = sb("at_wo_codes", [P, NH, D])
            wo_scales = sb("at_wo_scales", [P, NH, D])
            bv_wide = sb("at_bv_wide", [P, NH, P])
            bo = sb("at_bo", [P, D])
            loads = [
                (cols[:], w["at_cols"].rearrange("p (m h) -> p m h", m=3)),
                (bo[:], w["at_bo"][0, :].partition_broadcast(P)),
                (wo_codes[:], w["at_wo_codes"].rearrange("(h p) n -> p h n", p=P)),
            ]
            scales_o = w["at_wo_scales"].rearrange("(h q) n -> q h n", q=NSC)
            for q in range(NSC):
                loads.append((wo_scales[q * BLK:(q + 1) * BLK], scales_o[q].partition_broadcast(BLK)))

            def emit(name, eng, bank, psum_t, transposed, value):
                c, b = divmod(bank, NB)
                src = psum_t[:, c, bass.ts(b, BT)]
                hi, lo = x_hi[:, c, bass.ts(b, BT)], x_lo[:, c, bass.ts(b, BT)]
                if name == "scalar":
                    eng.wait_ge(transposed, value)
                    nc.scalar.activation(hi, src, ACT.Copy).then_inc(hi_copied, 1)
                else:
                    eng.wait_ge(hi_copied, bank + 1)
                    nc.vector.tensor_tensor(lo, src, hi.bitcast(F32), ALU.subtract).then_inc(lo_copied, 1)

            with ExitStack() as ps_ctx:
                psum_t = ps_ctx.enter_context(nc.psum_tensor("at_psum_t", [P, NC, T], F32))
                layer_norm_tokens(nc, ln, sb, "at_ln", x_tok, ident, x_norm, psum_t, emit, loads, loaded)

            with ExitStack() as ps_ctx:
                psum_b = ps_ctx.enter_context(nc.psum_tensor("at_psum_b", [P, BT], F32))
                wo_scaled = semaphore("at_wo_scaled")
                bv_spread = semaphore("at_bv_spread")
                bv_psum = semaphore("at_bv_psum")
                bias_ready = semaphore("at_bias_ready")
                biased = semaphore("at_biased")
                with nc.Block() as block:
                    @block.vector
                    def _(dve):
                        nc.vector.tensor_tensor(wo_codes[:], wo_codes[:], wo_scales[:], ALU.mult).then_inc(wo_scaled, 1)
                        dve.wait_ge(bv_psum, 1)
                        nc.vector.tensor_tensor(bo[:], psum_b[:, 0:D], bo[:], ALU.add).then_inc(bias_ready, 1)
                        dve.wait_ge(bias_ready, 1)
                        nc.vector.tensor_tensor(x_tok[:], x_tok[:], bo[:].unsqueeze(1).to_broadcast([P, NT, D]),
                                                ALU.add).then_inc(biased, 1)

                    @block.gpsimd
                    def _(pool):
                        nc.gpsimd.tensor_copy(bv_wide[:], cols[:, 2, :].unsqueeze(2).to_broadcast([P, NH, P])
                                              ).then_inc(bv_spread, 1)

                    @block.tensor
                    def _(pe):
                        pe.wait_ge(bv_spread, 1)
                        pe.wait_ge(wo_scaled, 1)
                        for h in range(NH):
                            last = nc.tensor.matmul(psum_b[:, 0:D], bv_wide[:, h, :], wo_codes[:, h, :],
                                                    start=(h == 0), stop=(h == NH - 1))
                        last.then_inc(bv_psum, 1)

        with ExitStack() as inner:
            def sb(name, shape, dt=F32):
                return inner.enter_context(nc.sbuf_tensor(name, shape, dt))

            def ps(name, shape):
                return inner.enter_context(nc.psum_tensor(name, shape, F32))

            codes, scales = sb("at_codes", [P, 2, NC, HD]), sb("at_scales", [P, 2, NC, HD])
            w_hi, w_lo = sb("at_w_hi", [P, 2, NC, HD], F32R), sb("at_w_lo", [P, 2, NC, HD], F32R)
            v_codes, v_scales = (t[:].rearrange("p m c n -> p (m c n)").rearrange("p (c n) -> p c n", c=NC)
                                 for t in (codes, scales))
            o_codes, o_scales = (t[:, 0].rearrange("p c n -> p (c n)") for t in (codes, scales))
            wv_hi, wv_lo = sb("at_wv_hi", [P, NC, 2 * HD], F32R), sb("at_wv_lo", [P, NC, 2 * HD], F32R)
            wo_hi, wo_lo = sb("at_wo_hi", [P, D], F32R), sb("at_wo_lo", [P, D], F32R)
            bias = sb("at_bias", [P, 2])
            q_hi, q_lo = sb("at_q_hi", [P, T], F32R), sb("at_q_lo", [P, T], F32R)
            k_hi, k_lo = sb("at_k_hi", [P, T], F32R), sb("at_k_lo", [P, T], F32R)
            v_hi, v_lo = sb("at_v_hi", [P, KT, 2 * HD], F32R), sb("at_v_lo", [P, KT, 2 * HD], F32R)
            prob = [sb(f"at_prob{j}", [P, T]) for j in range(NPROB)]
            pT_hi, pT_lo = sb("at_pT_hi", [P, 3, BT], F32R), sb("at_pT_lo", [P, 3, BT], F32R)
            oT_hi, oT_lo = sb("at_oT_hi", [P, BT], F32R), sb("at_oT_lo", [P, BT], F32R)
            factor = sb("at_factor", [P, NC])
            part_min = sb("at_part_min", [P, 2, 4])
            shift = sb("at_shift", [P, 2])
            half_sum = sb("at_half_sum", [P, QT, 2])
            rsum = sb("at_rsum", [P, QT])
            psum_s = ps("at_psum_s", [P, 4, BT])
            psum_p = ps("at_psum_p", [P, 2, BT])
            psum_o = ps("at_psum_o", [P, BT])
            psum_x = ps("at_psum_x", [P, BT])

            w_loaded = semaphore("at_w_loaded")
            wv_loaded = semaphore("at_wv_loaded")
            wo_loaded = semaphore("at_wo_loaded")
            w_split = semaphore("at_w_split")
            q_factor = semaphore("at_q_factor")
            wv_split = semaphore("at_wv_split")
            wo_split = semaphore("at_wo_split")
            bias_ready = semaphore("at_bias_copied")
            qk_psum = semaphore("at_qk_psum")
            qk_hi = semaphore("at_qk_hi")
            qk_lo = semaphore("at_qk_lo")
            v_psum = semaphore("at_v_psum")
            v_hi_ready = semaphore("at_v_hi_ready")
            v_lo_ready = semaphore("at_v_lo_ready")
            scored = semaphore("at_scored")
            min_steps = semaphore("at_min_steps")
            exp_done = semaphore("at_exp_done")
            sum_steps = semaphore("at_sum_steps")
            p_transposed = semaphore("at_p_transposed")
            pT_hi_ready = semaphore("at_pT_hi_ready")
            pT_lo_ready = semaphore("at_pT_lo_ready")
            pv_done = semaphore("at_pv_done")
            oT_hi_ready = semaphore("at_oT_hi_ready")
            oT_lo_ready = semaphore("at_oT_lo_ready")
            wo_psum = semaphore("at_wo_psum")
            added = semaphore("at_added")
            N_W = 1 + NSC
            NQK = 2 * NB
            NV = KT // 2

            def pT_buf(m, j):
                return (m % 2 + j) % 3

            def run(eng, slot, finish):
                def lower(hu, hs, odd):
                    for i in range(LAG):
                        slot(i, hs, None if hu is None else QT - LAG + i, hu, odd, True, None)

                def upper(h, begun, odd, v):
                    for i in range(LAG, QT):
                        slot(i, h, i - LAG, h, odd, begun, v if i == LAG else None)

                def pair(g, begun):
                    upper(g * 2, begun, 0, g)
                    lower(g * 2, g * 2 + 1, 0)
                    upper(g * 2 + 1, True, 1, None)

                lower(None, 0, 1)
                pair(0, False)
                with eng.Fori(1, NH // 2) as g:
                    lower(g * 2 - 1, g * 2, 1)
                    pair(g, True)
                lower(NH - 1, None, 1)
                finish(NH - 1)

            with nc.Block() as block:
                @block.sync
                def _(sp):
                    def load_v(g):
                        col = bass.ts(g, 2 * HD)
                        sp.dma_start(v_codes, w["at_wv_codes"].rearrange("(c p) n -> p c n", p=P)[:, :, col]
                                     ).then_inc(wv_loaded, 16)
                        sc = w["at_wv_scales"].rearrange("(c q) n -> q c n", q=NSC)
                        for q in range(NSC):
                            sp.dma_start(v_scales[q * BLK:(q + 1) * BLK],
                                         sc[q][:, col].partition_broadcast(BLK)).then_inc(wv_loaded, 16)

                    def load(h):
                        col = bass.ts(h, HD)
                        for m, name in enumerate("qk"):
                            sp.dma_start(codes[:, m], w[f"at_w{name}_codes"].rearrange("(c p) n -> p c n", p=P)[:, :, col]
                                         ).then_inc(w_loaded, 16)
                            sc = w[f"at_w{name}_scales"].rearrange("(c q) n -> q c n", q=NSC)
                            for q in range(NSC):
                                sp.dma_start(scales[q * BLK:(q + 1) * BLK, m],
                                             sc[q][:, col].partition_broadcast(BLK)).then_inc(w_loaded, 16)

                    def load_o(h):
                        sp.dma_start(o_codes, w["at_wo_codes"][bass.ts(h, HD), :]).then_inc(wo_loaded, 16)
                        for q in range(NSC):
                            sp.dma_start(o_scales[q * BLK:(q + 1) * BLK],
                                         w["at_wo_scales"][bass.ds(h * NSC + q, 1), :].rearrange("a n -> (a n)")
                                         .partition_broadcast(BLK)).then_inc(wo_loaded, 16)

                    load(0)
                    sp.wait_ge(w_split, 3)
                    load_v(0)
                    sp.wait_ge(wv_split, 3)
                    load_o(0)
                    sp.wait_ge(wo_split, 3)
                    load(1)
                    sp.wait_ge(w_split, 6)
                    load_o(1)
                    with sp.Fori(1, NH // 2) as g:
                        sp.wait_ge(wo_split, g * 6)
                        load(g * 2)
                        sp.wait_ge(w_split, g * 6 + 3)
                        load_v(g)
                        sp.wait_ge(wv_split, g * 3 + 3)
                        load_o(g * 2)
                        sp.wait_ge(wo_split, g * 6 + 3)
                        load(g * 2 + 1)
                        sp.wait_ge(w_split, g * 6 + 6)
                        load_o(g * 2 + 1)

                @block.gpsimd
                def _(pool):
                    def split(whole_hi, whole, scale, lo, steps, n):
                        nc.gpsimd.tensor_tensor(whole_hi, whole, scale, ALU.mult).then_inc(steps, 1)
                        nc.gpsimd.tensor_tensor(whole, whole, scale, ALU.mult).then_inc(steps, 1)
                        pool.wait_ge(steps, n + 2)
                        nc.gpsimd.tensor_tensor(lo, whole, whole_hi.bitcast(F32), ALU.subtract).then_inc(steps, 1)

                    def split_head(h, first, g=None):
                        pool.wait_ge(w_loaded, h * (32 * N_W) + 32 * N_W)
                        if not first:
                            pool.wait_ge(qk_psum, h * NQK)
                        nc.gpsimd.tensor_tensor(scales[:, 0], scales[:, 0],
                                                factor[:].unsqueeze(2).to_broadcast([P, NC, HD]),
                                                ALU.mult).then_inc(q_factor, 1)
                        pool.wait_ge(q_factor, h + 2)
                        split(w_hi[:], codes[:], scales[:], w_lo[:], w_split, h * 3)
                        if g is not None:
                            pool.wait_ge(wv_loaded, g * (16 * N_W) + 16 * N_W)
                            if not first:
                                pool.wait_ge(v_psum, g * NV)
                            split(wv_hi[:], v_codes, v_scales, wv_lo[:], wv_split, g * 3)
                        pool.wait_ge(wo_loaded, h * (16 * N_W) + 16 * N_W)
                        if not first:
                            pool.wait_ge(wo_psum, h * QT)
                        split(wo_hi[:], o_codes, o_scales, wo_lo[:], wo_split, h * 3)

                    nc.gpsimd.memset(factor[:], -SCALE).then_inc(q_factor, 1)
                    pool.wait_ge(q_factor, 1)
                    split_head(0, True, 0)
                    split_head(1, False)
                    with pool.Fori(1, NH // 2) as g:
                        split_head(g * 2, False, g)
                        split_head(g * 2 + 1, False)

                @block.tensor
                def _(pe):
                    def three(out, a_hi, a_lo, b_hi, b_lo, start=True, stop=True):
                        nc.tensor.matmul(out, a_hi, b_hi, start=start, stop=False)
                        nc.tensor.matmul(out, a_hi, b_lo, start=False, stop=False)
                        return nc.tensor.matmul(out, a_lo, b_hi, start=False, stop=stop)

                    def qk(h, first, after_first_bank):
                        pe.wait_ge(w_split, h * 3 + 3)
                        for m in range(2):
                            for b in range(NB):
                                if m == 1:
                                    pe.wait_ge(qk_lo, h * NQK + b + 1)
                                elif b % 2 == 0 and not first:
                                    pe.wait_ge(exp_done, h * (2 * QT) - 1 + b // 2)
                                for c in range(NC):
                                    last = three(psum_s[:, b, :], w_hi[:, m, c, :], w_lo[:, m, c, :],
                                                 x_hi[:, c, bass.ts(b, BT)], x_lo[:, c, bass.ts(b, BT)],
                                                 start=(c == 0), stop=(c == NC - 1))
                                last.then_inc(qk_psum, 1)
                                if m == 0 and b == 0:
                                    after_first_bank()

                    def v_pair(g, after_first_bank):
                        pe.wait_ge(wv_split, g * 3 + 3)
                        for n in range(NV):
                            b = n % NB
                            if n >= NB:
                                pe.wait_ge(v_lo_ready, g * NV + n - NB + 1)
                            elif b % 2 == 0:
                                pe.wait_ge(exp_done, g * (4 * QT) + 2 * LAG - 1 + b // 2)
                            for j in range(2):
                                i = n * 2 + j
                                for c in range(NC):
                                    last = three(psum_s[:, b, bass.ts(j, 2 * HD)], x_hi[:, c, bass.ts(i, P)],
                                                 x_lo[:, c, bass.ts(i, P)], wv_hi[:, c, :], wv_lo[:, c, :],
                                                 start=(c == 0), stop=(c == NC - 1))
                            last.then_inc(v_psum, 1)
                            if n == 0:
                                after_first_bank()

                    def score(i, h, n, v):
                        if i == 0:
                            if n == 0:
                                pe.wait_ge(qk_lo, h * NQK + NQK)
                        elif v is not None:
                            pe.wait_ge(v_lo_ready, v * NV + NV - NB + n + 1)
                        else:
                            pe.wait_ge(exp_done, h * (2 * QT) + (2 * i - 1 + n // 2))
                        three(psum_s[:, n, :], q_hi[:, bass.ts(i, P)], q_lo[:, bass.ts(i, P)],
                              k_hi[:, bass.ts(n, BT)], k_lo[:, bass.ts(n, BT)]).then_inc(scored, 1)

                    def turn(m, h, j):
                        if j == 2:
                            pe.wait_ge(pT_lo_ready, h * (QT * KPT) + (m * KPT + 1))
                        if m % BQ == 0 and j == 0:
                            pe.wait_ge(exp_done, h * (2 * QT) + 2 * (m + BQ))
                        kk = (m % BQ) * KPT + j
                        for t in range(BQ):
                            buf = prob[(m - m % BQ + t) % NPROB]
                            last = nc.tensor.transpose(psum_p[:, j % 2, bass.ts(t, P)], buf[:, bass.ts(kk, P)], ident[:])
                        last.then_inc(p_transposed, 1)

                    def weigh(m, h, j, odd):
                        pe.wait_ge(pT_lo_ready, h * (QT * KPT) + (m * KPT + j + 1))
                        kk = (m % BQ) * KPT + j
                        if kk == 0:
                            pe.wait_ge(oT_lo_ready, h * (QT // BQ) + m // BQ)
                        half = bass.ts(odd, HD)
                        three(psum_o[:], v_hi[:, kk, half], v_lo[:, kk, half], pT_hi[:, pT_buf(m, j), :], pT_lo[:, pT_buf(m, j), :],
                              start=(kk == 0), stop=(kk == KT - 1)).then_inc(pv_done, 1)

                    def project(i, h):
                        b = i // BQ
                        pe.wait_ge(oT_lo_ready, h * (QT // BQ) + b + 1)
                        pe.wait_ge(added, h * QT + i)
                        if i == 0:
                            pe.wait_ge(wo_split, h * 3 + 3)
                        tile = bass.ts(i % BQ, P)
                        three(psum_x[:, 0:D], oT_hi[:, tile], oT_lo[:, tile], wo_hi[:], wo_lo[:]).then_inc(wo_psum, 1)

                    def slot(i, hs, m, hu, odd, begun, v):
                        projects = v is not None or (i == 0 and hs is not None)
                        if hu is not None:
                            turn(m, hu, 0)
                        if hs is not None and not projects:
                            score(i, hs, 0, v)
                            score(i, hs, 1, v)

                        def weigh_last():
                            if m is not None and m > 0:
                                weigh(m - 1, hu, KPT - 1, odd)
                            elif m == 0 and begun:
                                weigh(QT - 1, hu - 1, KPT - 1, 1 - odd)

                        def project_tile():
                            if m is not None and m >= BQ:
                                project(m - BQ, hu)
                            elif m is not None and begun:
                                project(QT - BQ + m, hu - 1)

                        if projects:
                            if v is not None:
                                v_pair(v, weigh_last)
                            else:
                                qk(hs, hu is None, weigh_last)
                            if hu is not None:
                                turn(m, hu, 1)
                                turn(m, hu, 2)
                                weigh(m, hu, 0, odd)
                            project_tile()
                            for n in range(4):
                                score(i, hs, n, v)
                        else:
                            weigh_last()
                            if hs is not None:
                                score(i, hs, 2, v)
                            if hu is not None:
                                turn(m, hu, 1)
                            if hs is not None:
                                score(i, hs, 3, v)
                            if hu is not None:
                                turn(m, hu, 2)
                                weigh(m, hu, 0, odd)
                            project_tile()
                        if hu is not None:
                            weigh(m, hu, 1, odd)
                            turn(m, hu, 3)
                            weigh(m, hu, 2, odd)

                    def finish(h):
                        weigh(QT - 1, h, KPT - 1, 1)
                        for t in range(BQ):
                            project(QT - BQ + t, h)

                    run(pe, slot, finish)

                @block.scalar
                def _(act):
                    def qk(h):
                        for m, factor in enumerate((-SCALE, 1.0)):
                            nc.scalar.activation(bias[:, m:m + 1], cols[:, m, bass.ds(h, 1)], ACT.Copy,
                                                 scale=factor).then_inc(bias_ready, 1)
                        act.wait_ge(bias_ready, h * 2 + 2)
                        for m in range(2):
                            for b in range(NB):
                                act.wait_ge(qk_psum, h * NQK + (m * NB + b + 1))
                                nc.scalar.activation((q_hi, k_hi)[m][:, bass.ts(b, BT)], psum_s[:, b, :],
                                                     ACT.Identity, bias=bias[:, m:m + 1]).then_inc(qk_hi, 1)

                    def v_pair(g):
                        for n in range(NV):
                            act.wait_ge(v_psum, g * NV + n + 1)
                            nc.scalar.activation(v_hi[:, 2 * n:2 * n + 2, :],
                                                 psum_s[:, n % NB, :].rearrange("p (j d) -> p j d", j=2),
                                                 ACT.Copy).then_inc(v_hi_ready, 1)

                    def hi(m, h, j):
                        act.wait_ge(p_transposed, h * (QT * KPT) + (m * KPT + j + 1))
                        nc.scalar.activation(pT_hi[:, pT_buf(m, j), :], psum_p[:, j % 2, :], ACT.Copy).then_inc(pT_hi_ready, 1)

                    def out_hi(b, h):
                        act.wait_ge(pv_done, h * (QT * KPT) + (b + 1) * KT)
                        act.wait_ge(wo_psum, h * QT + b * BQ)
                        nc.scalar.activation(oT_hi[:], psum_o[:], ACT.Copy).then_inc(oT_hi_ready, 1)

                    def exp(i, h, half):
                        act.wait_ge(min_steps, h * (5 * QT) + 5 * (i + 1))
                        nc.scalar.activation(prob[i % NPROB][:, bass.ts(half, T // 2)],
                                             psum_s[:, 2 * half:2 * half + 2, :].rearrange("p a b -> p (a b)"),
                                             ACT.Exp, bias=shift[:, i % 2:i % 2 + 1], scale=-1.0,
                                             accum_out=half_sum[:, i, half:half + 1]).then_inc(exp_done, 1)

                    def slot(i, hs, m, hu, odd, begun, v):
                        if hu is not None:
                            hi(m, hu, 0)
                            if m >= BQ and m % BQ == 0:
                                out_hi(m // BQ - 1, hu)
                            elif m == 0 and begun:
                                out_hi(QT // BQ - 1, hu - 1)
                        if v is not None:
                            v_pair(v)
                        elif i == 0 and hs is not None:
                            qk(hs)
                        if hu is not None:
                            hi(m, hu, 1)
                            hi(m, hu, 2)
                        if hs is not None:
                            exp(i, hs, 0)
                        if hu is not None:
                            hi(m, hu, 3)
                        if hs is not None:
                            exp(i, hs, 1)

                    def finish(h):
                        out_hi(QT // BQ - 1, h)

                    run(act, slot, finish)

                @block.vector
                def _(dve):
                    def qk(h):
                        for m in range(2):
                            hi, lo = ((q_hi, q_lo), (k_hi, k_lo))[m]
                            for b in range(NB):
                                tok = bass.ts(b, BT)
                                dve.wait_ge(qk_hi, h * NQK + (m * NB + b + 1))
                                nc.vector.scalar_tensor_tensor(lo[:, tok], psum_s[:, b, :], bias[:, m:m + 1],
                                                               hi[:, tok].bitcast(F32), ALU.add,
                                                               ALU.subtract).then_inc(qk_lo, 1)

                    def v_pair(g):
                        for n in range(NV):
                            part = slice(2 * n, 2 * n + 2)
                            dve.wait_ge(v_hi_ready, g * NV + n + 1)
                            nc.vector.tensor_tensor(v_lo[:, part, :], psum_s[:, n % NB, :].rearrange("p (j d) -> p j d", j=2),
                                                    v_hi[:, part, :].bitcast(F32), ALU.subtract).then_inc(v_lo_ready, 1)

                    def lo(m, h, j):
                        dve.wait_ge(pT_hi_ready, h * (QT * KPT) + (m * KPT + j + 1))
                        nc.vector.tensor_tensor(pT_lo[:, pT_buf(m, j), :], psum_p[:, j % 2, :], pT_hi[:, pT_buf(m, j), :].bitcast(F32),
                                                ALU.subtract).then_inc(pT_lo_ready, 1)

                    def out_lo(b, h):
                        dve.wait_ge(oT_hi_ready, h * (QT // BQ) + b + 1)
                        nc.vector.tensor_tensor(oT_lo[:], psum_o[:], oT_hi[:].bitcast(F32),
                                                ALU.subtract).then_inc(oT_lo_ready, 1)

                    def smallest(i, h, n):
                        dve.wait_ge(scored, h * (4 * QT) + (4 * i + n + 1))
                        nc.vector.tensor_reduce(part_min[:, i % 2, n:n + 1], psum_s[:, n, :], AX.X,
                                                ALU.min).then_inc(min_steps, 1)

                    def row_shift(i, h):
                        dve.wait_ge(min_steps, h * (5 * QT) + (5 * i + 4))
                        nc.vector.tensor_reduce(shift[:, i % 2:i % 2 + 1], part_min[:, i % 2, :], AX.X,
                                                ALU.min).then_inc(min_steps, 1)

                    def row_sums(b, h):
                        part = slice(b * BQ, (b + 1) * BQ)
                        dve.wait_ge(exp_done, h * (2 * QT) + 2 * BQ * (b + 1))
                        nc.vector.tensor_tensor(rsum[:, part], half_sum[:, part, 0], half_sum[:, part, 1],
                                                ALU.add).then_inc(sum_steps, 1)
                        dve.wait_ge(sum_steps, h * (2 * (QT // BQ)) + (2 * b + 1))
                        nc.vector.reciprocal(rsum[:, part], rsum[:, part]).then_inc(sum_steps, 1)

                    def add(i, h):
                        dve.wait_ge(wo_psum, h * QT + i + 1)
                        nc.vector.scalar_tensor_tensor(x_tok[:, i, :], psum_x[:, 0:D], rsum[:, i:i + 1], x_tok[:, i, :],
                                                       ALU.mult, ALU.add).then_inc(added, 1)

                    def slot(i, hs, m, hu, odd, begun, v):
                        projects = v is not None or (i == 0 and hs is not None)

                        def first_sums():
                            if hs is not None and i > 0 and i % BQ == 0:
                                row_sums(i // BQ - 1, hs)
                            elif hu is not None and i == 0:
                                row_sums(QT // BQ - 1, hu)

                        def first_turn():
                            if hu is not None:
                                lo(m, hu, 0)
                                if m >= BQ and m % BQ == 0:
                                    out_lo(m // BQ - 1, hu)
                                elif m == 0 and begun:
                                    out_lo(QT // BQ - 1, hu - 1)

                        if projects:
                            first_turn()
                            first_sums()
                            if v is not None:
                                v_pair(v)
                            else:
                                qk(hs)
                            if hu is not None:
                                lo(m, hu, 1)
                                lo(m, hu, 2)
                            for n in range(4):
                                smallest(i, hs, n)
                            row_shift(i, hs)
                        else:
                            if hs is not None:
                                smallest(i, hs, 0)
                                smallest(i, hs, 1)
                            first_sums()
                            first_turn()
                            if hs is not None:
                                smallest(i, hs, 2)
                            if hu is not None:
                                lo(m, hu, 1)
                            if hs is not None:
                                smallest(i, hs, 3)
                                row_shift(i, hs)
                        if hu is not None:
                            if not projects:
                                lo(m, hu, 2)
                            if m >= BQ:
                                add(m - BQ, hu)
                            elif begun:
                                add(QT - BQ + m, hu - 1)
                            lo(m, hu, 3)

                    def finish(h):
                        out_lo(QT // BQ - 1, h)
                        for t in range(BQ):
                            add(QT - BQ + t, h)

                    run(dve, slot, finish)


def expert_ffn(nc, w, x_tok, ident, ln):
    E, F = 8, 512
    NF = F // P
    NBK = NT + E - 1
    with ExitStack() as ctx:
        def alloc(name, shape, dt=F32):
            return ctx.enter_context(nc.sbuf_tensor(name, shape, dt))

        def semaphore(name):
            return ctx.enter_context(nc.semaphore(name))

        rows_in = nc.dram_tensor("ef_rows_in", (NBK * P, D), F32, kind="Internal").ap()
        rows_out = nc.dram_tensor("ef_rows_out", (NBK * P, D), F32, kind="Internal").ap()
        x_norm = alloc("ef_x_norm", [P, NT, D])
        gate_up = alloc("ef_gate_up", [P, E, NC, 2 * F])
        down = alloc("ef_down", [P, E, NF, D])
        slot = alloc("ef_slot", [P, NT], mybir.dt.int32)
        block_expert = alloc("ef_block_expert", [P, NBK], mybir.dt.int32)
        experts_loaded = semaphore("ef_experts_loaded")
        rows_zeroed = semaphore("ef_rows_zeroed")
        scattered = semaphore("ef_scattered")

        with ExitStack() as mid:
            def mb(name, shape, dt=F32):
                return mid.enter_context(nc.sbuf_tensor(name, shape, dt))

            xT = mb("ef_xT", [P, NC, T])
            router = mb("ef_router", [P, NC, E])
            shared_gu = mb("ef_shared_gu", [P, NC, 2 * F])
            shared_down = mb("ef_shared_down", [P, NF, D])
            order = mb("ef_order", [P, E])
            earlier = mb("ef_earlier", [P, P])
            ones = mb("ef_ones", [P, P])
            limits = mb("ef_limits", [P, NT])
            numbers = mb("ef_numbers", [P, NBK])
            loaded = semaphore("ef_loaded")
            copied = semaphore("ef_copied")
            loads = (
                (router[:], w["ef_router"].rearrange("(c p) n -> p c n", p=P)),
                (shared_gu[:], w["ef_shared_gate_up"].rearrange("(c p) n -> p c n", p=P)),
                (shared_down[:], w["ef_shared_down"].rearrange("(c p) n -> p c n", p=P)),
                (order[:], w["c_order"][0, :].partition_broadcast(P)),
                (earlier[:], w["c_earlier"]),
                (ones[:], w["c_ones"]),
                (limits[:], w["c_limits"][0, :].partition_broadcast(P)),
                (numbers[:], w["c_numbers"][0, :].partition_broadcast(P)),
            )
            with ExitStack() as inner:
                psum_t = inner.enter_context(nc.psum_tensor("ef_psum_t", [P, NC, T], F32))
                layer_norm_tokens(nc, ln,
                                  lambda n, s, d: inner.enter_context(nc.sbuf_tensor(n, s, d)),
                                  "ef_ln", x_tok, ident, x_norm, psum_t, copy_banks(nc, xT, copied), loads, loaded)

            with ExitStack() as inner:
                def sb(name, shape, dt=F32):
                    return inner.enter_context(nc.sbuf_tensor(name, shape, dt))

                def ps(name, shape):
                    return inner.enter_context(nc.psum_tensor(name, shape, F32))

                zeros = sb("ef_zeros", [P, D])
                logits = sb("ef_logits", [P, NT, E])
                hit = sb("ef_hit", [P, NT, E])
                rank = sb("ef_rank", [P, NT, E])
                best = sb("ef_best", [P, NT])
                top = sb("ef_top", [P, NT])
                score = sb("ef_score", [P, NT])
                ends = sb("ef_ends", [P, E, NT])
                place = sb("ef_place", [P, NT, E])
                wide_e = sb("ef_wide_e", [P, E, NT])
                blocks = sb("ef_blocks", [P, E])
                block_ends = sb("ef_block_ends", [P, E])
                first_row = sb("ef_first_row", [P, E])
                ones_e = sb("ef_ones_e", [P, NT])
                slot_f = sb("ef_slot_f", [P, NT])
                past = sb("ef_past", [P, NBK, E])
                expert_f = sb("ef_expert_f", [P, NBK])
                silu_g = sb("ef_silu_g", [P, 2, BT])
                hidden = sb("ef_hidden", [P, NF, BT])
                psum_r = ps("ef_psum_r", [P, NT, E])
                psum_k = ps("ef_psum_k", [P, 2, NT * E])
                psum_g = ps("ef_psum_g", [P, 2, BT])
                psum_u = ps("ef_psum_u", [P, 2, BT])
                psum_y = ps("ef_psum_y", [P, BT])
                zeros_ready = semaphore("ef_zeros_ready")
                ones_ready = semaphore("ef_ones_ready")
                routed = semaphore("ef_routed")
                chain = semaphore("ef_chain")
                hit_ready = semaphore("ef_hit_ready")
                top_ready = semaphore("ef_top_ready")
                counted = semaphore("ef_counted")
                scored = semaphore("ef_scored")
                scaled = semaphore("ef_scaled")
                slots_ready = semaphore("ef_slots_ready")
                gu_psum = semaphore("ef_gu_psum")
                silu_ready = semaphore("ef_silu_ready")
                hidden_ready = semaphore("ef_hidden_ready")
                y_psum = semaphore("ef_y_psum")
                y_added = semaphore("ef_y_added")

                with nc.Block() as block:
                    @block.sync
                    def _(sp):
                        sp.wait_ge(zeros_ready, 1)
                        for j in range(NBK):
                            sp.dma_start(rows_in[j * P:(j + 1) * P, :], zeros[:]).then_inc(rows_zeroed, 16)
                        for e in range(E):
                            sp.dma_start(gate_up[:, e], w["ef_gate_up"][e].rearrange("(c p) n -> p c n", p=P)
                                         ).then_inc(experts_loaded, 16)
                            sp.dma_start(down[:, e], w["ef_down"][e].rearrange("(c p) n -> p c n", p=P)
                                         ).then_inc(experts_loaded, 16)

                    @block.gpsimd
                    def _(pool):
                        nc.gpsimd.memset(zeros[:], 0.0).then_inc(zeros_ready, 1)
                        nc.gpsimd.memset(ones_e[:], 1.0).then_inc(ones_ready, 1)
                        pool.wait_ge(scored, 1)
                        for i in range(NT):
                            nc.gpsimd.tensor_scalar(x_norm[:, i, :], x_norm[:, i, :], score[:, i:i + 1], None,
                                                    ALU.mult).then_inc(scaled, 1)
                        pool.wait_ge(rows_zeroed, 16 * NBK)
                        pool.wait_ge(slots_ready, 1)
                        for i in range(NT):
                            pool.wait_ge(scaled, i + 1)
                            pool.indirect_dma_start(
                                out=rows_in, out_offset=bass.IndirectOffsetOnAxis(ap=slot[:, i:i + 1], axis=0),
                                in_=x_norm[:, i, :], in_offset=None, bounds_check=NBK * P - 1
                            ).then_inc(scattered, 16)

                    @block.scalar
                    def _(act):
                        act.wait_ge(top_ready, 1)
                        nc.scalar.activation(score[:], top[:], ACT.Sigmoid).then_inc(scored, 1)
                        with act.Fori(0, NB) as b:
                            for f in range(NF):
                                act.wait_ge(gu_psum, b * NF + f + 1)
                                nc.scalar.activation(silu_g[:, f % 2, :], psum_g[:, f % 2, :],
                                                     ACT.Silu).then_inc(silu_ready, 1)

                    @block.vector
                    def _(dve):
                        steps = Steps(chain)

                        def after(instruction):
                            dve.wait_ge(steps.sem, steps.add(instruction))

                        wide = [P, NT, E]
                        dve.wait_ge(routed, 1)
                        after(nc.vector.tensor_copy(logits[:], psum_r[:]))
                        choose_largest(nc, dve, steps, logits[:], order[:], top[:], hit[:], rank[:], best[:])
                        nc.vector.tensor_copy(top[:], top[:]).then_inc(top_ready, 1)
                        nc.vector.tensor_copy(hit[:], hit[:]).then_inc(hit_ready, 1)
                        dve.wait_ge(counted, 1)
                        dve.wait_ge(ones_ready, 1)
                        counts = psum_k[:, 1, :].rearrange("p (i e) -> p e i", e=E)
                        for e in range(E):
                            nc.vector.tensor_tensor_scan(ends[:, e, :], ones_e[:], counts[:, e, :], 0.0,
                                                         ALU.mult, ALU.add).then_inc(steps.sem, 1)
                            steps.n += 1
                        dve.wait_ge(steps.sem, steps.n)
                        after(nc.vector.tensor_tensor(place[:], ends[:].rearrange("p e i -> p i e"),
                                                      psum_k[:, 1, :].rearrange("p (i e) -> p i e", e=E), ALU.subtract))
                        after(nc.vector.tensor_tensor(place[:], psum_k[:, 0, :].rearrange("p (i e) -> p i e", e=E),
                                                      place[:], ALU.add))
                        after(nc.vector.tensor_tensor(wide_e[:], ends[:, :, NT - 1:NT].to_broadcast([P, E, NT]),
                                                      limits[:].unsqueeze(1).to_broadcast([P, E, NT]), ALU.is_gt))
                        after(nc.vector.tensor_reduce(blocks[:], wide_e[:], AX.X, ALU.add))
                        after(nc.vector.tensor_tensor_scan(block_ends[:], ones_e[:, 0:E], blocks[:], 0.0,
                                                           ALU.mult, ALU.add))
                        after(nc.vector.tensor_tensor(first_row[:], block_ends[:], blocks[:], ALU.subtract))
                        after(nc.vector.scalar_tensor_tensor(
                            place[:], first_row[:].unsqueeze(1).to_broadcast(wide), float(P), place[:],
                            ALU.mult, ALU.add))
                        after(nc.vector.tensor_tensor(place[:], place[:], hit[:], ALU.mult))
                        after(nc.vector.tensor_reduce(slot_f[:], place[:], AX.X, ALU.add))
                        nc.vector.tensor_copy(slot[:], slot_f[:]).then_inc(slots_ready, 1)
                        after(nc.vector.tensor_tensor(
                            past[:], block_ends[:].unsqueeze(1).to_broadcast([P, NBK, E]),
                            numbers[:].unsqueeze(2).to_broadcast([P, NBK, E]), ALU.is_le))
                        after(nc.vector.tensor_reduce(expert_f[:], past[:], AX.X, ALU.add))
                        after(nc.vector.tensor_scalar(block_expert[:], expert_f[:], float(E - 1), None, ALU.min))
                        with dve.Fori(0, NB) as b:
                            for f in range(NF):
                                dve.wait_ge(silu_ready, b * NF + f + 1)
                                nc.vector.tensor_tensor(hidden[:, f, :], psum_u[:, f % 2, :], silu_g[:, f % 2, :],
                                                        ALU.mult).then_inc(hidden_ready, 1)
                            for j in range(TPB):
                                dve.wait_ge(y_psum, b * TPB + j + 1)
                                row = x_tok[:, bass.ds(b * TPB + j, 1), :].rearrange("p a d -> p (a d)")
                                nc.vector.tensor_tensor(row, psum_y[:, 0:D], row, ALU.add).then_inc(y_added, 1)

                    @block.tensor
                    def _(pe):
                        for i in range(NT):
                            for c in range(NC):
                                last = nc.tensor.matmul(psum_r[:, i, :], xT[:, c, bass.ts(i, P)], router[:, c, :],
                                                        start=(c == 0), stop=(c == NC - 1))
                        last.then_inc(routed, 1)

                        def up(b, f):
                            if f >= 2:
                                pe.wait_ge(hidden_ready, b * NF + f - 1)
                            for out, off in ((psum_g, 0), (psum_u, F)):
                                for c in range(NC):
                                    last = nc.tensor.matmul(out[:, f % 2, :], shared_gu[:, c, off + f * P:off + (f + 1) * P],
                                                            xT[:, c, bass.ts(b, BT)], start=(c == 0), stop=(c == NC - 1))
                            last.then_inc(gu_psum, 1)

                        pe.wait_ge(hit_ready, 1)
                        hits = hit[:].rearrange("p i e -> p (i e)")
                        nc.tensor.matmul(psum_k[:, 0, :], earlier[:], hits, start=True, stop=True)
                        nc.tensor.matmul(psum_k[:, 1, :], ones[:], hits, start=True, stop=True).then_inc(counted, 1)
                        with pe.Fori(0, NB) as b:
                            for f in range(NF):
                                up(b, f)
                            for j in range(TPB):
                                pe.wait_ge(hidden_ready, b * NF + NF)
                                if j >= 1:
                                    pe.wait_ge(y_added, b * TPB + j)
                                for f in range(NF):
                                    last = nc.tensor.matmul(psum_y[:, 0:D], hidden[:, f, bass.ts(j, P)],
                                                            shared_down[:, f, :], start=(f == 0), stop=(f == NF - 1))
                                last.then_inc(y_psum, 1)
                            pe.wait_ge(y_added, b * TPB + TPB)

        with ExitStack() as inner:
            def sb(name, shape, dt=F32):
                return inner.enter_context(nc.sbuf_tensor(name, shape, dt))

            def ps(name, shape):
                return inner.enter_context(nc.psum_tensor(name, shape, F32))

            rows = sb("ef_rows", [P, 2, D])
            rowsT = sb("ef_rowsT", [P, 2, NC, P])
            silu_g = sb("ef_silu_x", [P, 2, F])
            hidden = sb("ef_hidden_x", [P, 2, F])
            hiddenT = sb("ef_hiddenT", [P, 2, NF, P])
            result = sb("ef_result", [P, 2, D])
            back = x_norm
            psum_xt = ps("ef_psum_xt", [P, NC, P])
            psum_gu = ps("ef_psum_gu", [P, 2, 2, F])
            psum_ht = ps("ef_psum_ht", [P, NF, P])
            psum_d = ps("ef_psum_d", [P, BT])
            rows_loaded = [semaphore(f"ef_rows_loaded{k}") for k in range(2)]
            x_transposed = semaphore("ef_x_transposed")
            rowsT_ready = semaphore("ef_rowsT_ready")
            gu_psum = semaphore("ef_gu_psum_x")
            silu_ready = semaphore("ef_silu_x_ready")
            hidden_ready = semaphore("ef_hidden_x_ready")
            h_transposed = semaphore("ef_h_transposed")
            hiddenT_ready = semaphore("ef_hiddenT_ready")
            d_psum = semaphore("ef_d_psum")
            result_ready = semaphore("ef_result_ready")
            rows_stored = [semaphore(f"ef_rows_stored{k}") for k in range(2)]
            gathered = [semaphore(f"ef_gathered{g}") for g in range(NB)]
            added = semaphore("ef_added")

            def blocks(eng, body):
                with eng.Fori(0, NBK // 2) as pair:
                    body(pair * 2, 0)
                    body(pair * 2 + 1, 1)
                body(NBK - 1, 0)

            with nc.Block() as block:
                @block.sync
                def _(sp):
                    def load(j, k):
                        sp.dma_start(rows[:, k, :], rows_in[bass.ts(j, P), :]).then_inc(rows_loaded[k], 16)

                    sp.wait_ge(scattered, 16 * NT)
                    load(0, 0)
                    load(1, 1)
                    with sp.Fori(1, NBK // 2) as pair:
                        for k in range(2):
                            sp.wait_ge(x_transposed, pair * 2 + (k - 1))
                            load(pair * 2 + k, k)
                    sp.wait_ge(x_transposed, NBK - 2)
                    load(NBK - 1, 0)

                @block.tensor
                def _(pe):
                    pe.wait_ge(experts_loaded, 16 * 2 * E)

                    def up(j, k, count):
                        e = pe.value_load(block_expert[0:1, bass.ds(j, 1)], min_val=0, max_val=E - 1)
                        pe.wait_ge(rows_loaded[k], count)
                        for c in range(NC):
                            last = nc.tensor.transpose(psum_xt[:, c, :], rows[:, k, bass.ts(c, P)], ident[:])
                        last.then_inc(x_transposed, 1)
                        pe.wait_ge(rowsT_ready, j + 1)
                        for half in range(2):
                            for c in range(NC):
                                wt = gate_up[:, bass.ds(e, 1), c, bass.ts(half, F)].rearrange("p a n -> p (a n)")
                                last = nc.tensor.matmul(psum_gu[:, k, half, :], rowsT[:, k, c, :], wt,
                                                        start=(c == 0), stop=(c == NC - 1))
                        last.then_inc(gu_psum, 1)
                        return e

                    def dn(j, k, e):
                        pe.wait_ge(hidden_ready, j + 1)
                        for c in range(NF):
                            last = nc.tensor.transpose(psum_ht[:, c, :], hidden[:, k, bass.ts(c, P)], ident[:])
                        last.then_inc(h_transposed, 1)
                        pe.wait_ge(hiddenT_ready, j + 1)
                        if k == 1:
                            pe.wait_ge(result_ready, j)
                        for c in range(NF):
                            wt = down[:, bass.ds(e, 1), c, :].rearrange("p a n -> p (a n)")
                            last = nc.tensor.matmul(psum_d[:, 0:D], hiddenT[:, k, c, :], wt,
                                                    start=(c == 0), stop=(c == NF - 1))
                        last.then_inc(d_psum, 1)

                    with pe.Fori(0, NBK // 2) as pair:
                        e0 = up(pair * 2, 0, pair * 16 + 16)
                        e1 = up(pair * 2 + 1, 1, pair * 16 + 16)
                        dn(pair * 2, 0, e0)
                        dn(pair * 2 + 1, 1, e1)
                        pe.wait_ge(result_ready, pair * 2 + 2)
                    dn(NBK - 1, 0, up(NBK - 1, 0, 16 * (NBK // 2 + 1)))

                @block.scalar
                def _(act):
                    def up(j, k):
                        act.wait_ge(x_transposed, j + 1)
                        nc.scalar.activation(rowsT[:, k], psum_xt[:], ACT.Copy).then_inc(rowsT_ready, 1)
                        act.wait_ge(gu_psum, j + 1)
                        nc.scalar.activation(silu_g[:, k, :], psum_gu[:, k, 0, :], ACT.Silu).then_inc(silu_ready, 1)

                    def dn(j, k):
                        act.wait_ge(h_transposed, j + 1)
                        nc.scalar.activation(hiddenT[:, k], psum_ht[:], ACT.Copy).then_inc(hiddenT_ready, 1)

                    with act.Fori(0, NBK // 2) as pair:
                        up(pair * 2, 0)
                        up(pair * 2 + 1, 1)
                        dn(pair * 2, 0)
                        dn(pair * 2 + 1, 1)
                    up(NBK - 1, 0)
                    dn(NBK - 1, 0)

                @block.vector
                def _(dve):
                    def up(j, k):
                        dve.wait_ge(silu_ready, j + 1)
                        nc.vector.tensor_tensor(hidden[:, k, :], psum_gu[:, k, 1, :], silu_g[:, k, :],
                                                ALU.mult).then_inc(hidden_ready, 1)

                    def dn(j, k, stored):
                        dve.wait_ge(d_psum, j + 1)
                        if stored is not None:
                            dve.wait_ge(rows_stored[k], stored)
                        nc.vector.tensor_copy(result[:, k, :], psum_d[:, 0:D]).then_inc(result_ready, 1)

                    up(0, 0)
                    up(1, 1)
                    dn(0, 0, None)
                    dn(1, 1, None)
                    with dve.Fori(1, NBK // 2) as pair:
                        up(pair * 2, 0)
                        up(pair * 2 + 1, 1)
                        dn(pair * 2, 0, pair * 16)
                        dn(pair * 2 + 1, 1, pair * 16)
                    up(NBK - 1, 0)
                    dn(NBK - 1, 0, 16 * (NBK // 2))
                    for g in range(NB):
                        tiles = slice(g * TPB, (g + 1) * TPB)
                        dve.wait_ge(gathered[g], 16 * TPB)
                        nc.vector.tensor_tensor(x_tok[:, tiles, :], x_tok[:, tiles, :], back[:, tiles, :],
                                                ALU.add).then_inc(added, 1)

                @block.gpsimd
                def _(pool):
                    def store(j, k):
                        pool.wait_ge(result_ready, j + 1)
                        pool.dma_start(rows_out[bass.ts(j, P), :], result[:, k, :]).then_inc(rows_stored[k], 16)

                    blocks(pool, store)
                    for k in range(2):
                        pool.wait_ge(rows_stored[k], 16 * ((NBK + 1 - k) // 2))
                    for i in range(NT):
                        pool.indirect_dma_start(
                            out=back[:, i, :], out_offset=None, in_=rows_out,
                            in_offset=bass.IndirectOffsetOnAxis(ap=slot[:, i:i + 1], axis=0),
                            bounds_check=NBK * P - 1).then_inc(gathered[i // TPB], 16)


def build(nc, w, out, parts=(1, 2, 3, 4)):
    with ExitStack() as ctx:
        x_tok = ctx.enter_context(nc.sbuf_tensor("x_tok", [P, NT, D], F32))
        ident = ctx.enter_context(nc.sbuf_tensor("ident", [P, P], F32))
        x_loaded = ctx.enter_context(nc.semaphore("x_loaded"))
        stored = ctx.enter_context(nc.semaphore("stored"))
        ln = LayerNorms(lambda name: ctx.enter_context(nc.semaphore(name)))
        with nc.Block() as block:
            @block.sync
            def _(sp):
                sp.dma_start(x_tok[:], w["L0_attn_x"].rearrange("(i p) d -> p i d", p=P)).then_inc(x_loaded, 16)
                sp.dma_start(ident[:], w["c_ident"]).then_inc(x_loaded, 16)
                sp.wait_ge(x_loaded, 32)

        if 1 in parts:
            time_mix(nc, w, x_tok, ident, ln)
        if 2 in parts:
            lora_ffn(nc, w, x_tok, ident, ln)
        if 3 in parts:
            attention(nc, w, x_tok, ident, ln)
        if 4 in parts:
            expert_ffn(nc, w, x_tok, ident, ln)

        with nc.Block() as block:
            @block.sync
            def _(sp):
                sp.dma_start(out.rearrange("(i p) d -> p i d", p=P), x_tok[:]).then_inc(stored, 16)
                sp.wait_ge(stored, 16)


def lay_out(inputs):
    import numpy as np

    a = {k: np.asarray(v) for k, v in inputs.items()}
    H, K, V, E, R, F = 16, 8, 8, 8, 16, 1024

    def col(x):
        return x.reshape(-1, P).T

    w = {"L0_attn_x": a["L0_attn_x"].reshape(T, D)}
    for k in ("L0_attn_Wx1", "L0_attn_Ww_b", "L0_attn_Wg_b", "L0_attn_Wo"):
        w[k] = a[k]
    w["Wx2T"] = a["L0_attn_Wx2"].transpose(1, 2, 0).reshape(-1, D)
    w["tm_proj"] = np.concatenate([a["L0_attn_" + k] for k in ("Wr", "Ww_a", "Wk", "Wv", "Wg_a")], axis=1)
    w["tm_cols"] = np.concatenate(
        [col(a["L0_attn_mu_x"]), col(a["L0_attn_x_bias"]), col(a["L0_attn_bw"]), col(a["L0_attn_bg"]),
         col(a["L0_attn_bonus"]), np.tile(a["L0_attn_ln_w"], H)[:, None], np.tile(a["L0_attn_ln_b"], H)[:, None]], axis=1)
    same = np.kron(np.eye(H), np.ones((V, K))).astype(np.float32)
    pick = np.zeros((P, V, P), np.float32)
    for v in range(V):
        pick[v::V, v, :] = same[v::V, :]
    w["c_spread"] = pick
    w["c_gather"] = pick.transpose(2, 1, 0)
    w["c_heads"] = same
    w["c_ident"] = np.eye(P, dtype=np.float32)
    w["lf_router_a1"] = np.concatenate([a["L0_ffn_Wr"], a["L0_ffn_A1"].transpose(2, 0, 1).reshape(D, E * R)], axis=1)
    w["lf_br"] = a["L0_ffn_br"][None, :]
    w["L0_ffn_W1"] = a["L0_ffn_W1"]
    w["lf_b1"] = col(a["L0_ffn_b1"])
    w["lf_B1T"] = a["L0_ffn_B1"].transpose(0, 2, 1).reshape(E * R, F)
    w["L0_ffn_W2"] = a["L0_ffn_W2"]
    w["lf_A2T"] = a["L0_ffn_A2"].transpose(2, 0, 1).reshape(F, E * R)
    rows = np.kron(np.eye(E), np.ones((1, R)))
    none, all_ = np.zeros((E, P)), np.ones((E, P))
    w["c_choose"] = np.stack([np.concatenate(q) for q in ((rows, none, none, none), (none, rows, none, none),
                                                          (-rows, rows, none, none))], axis=1).astype(np.float32)
    w["c_weigh"] = np.stack([np.concatenate(q) for q in ((none, none, all_, none), (none, none, none, all_))],
                            axis=1).astype(np.float32)
    w["lf_b2"] = a["L0_ffn_b2"][None, :]
    w["lf_B2T"] = a["L0_ffn_B2"].transpose(0, 2, 1).reshape(E * R, D)
    for n in "qkvo":
        w[f"at_w{n}_codes"] = a[f"L1_attn_w{n}_codes"]
        w[f"at_w{n}_scales"] = a[f"L1_attn_w{n}_scales"]
    w["at_cols"] = np.concatenate([col(a["L1_attn_b" + n]) for n in "qkv"], axis=1)
    w["at_bo"] = a["L1_attn_bo"][None, :]
    w["ef_router"] = a["L1_ffn_router_w"].T
    w["ef_gate_up"] = a["L1_ffn_gate_up_proj"]
    w["ef_down"] = a["L1_ffn_down_proj"]
    w["ef_shared_gate_up"] = np.concatenate([a["L1_ffn_shared_gate_w"], a["L1_ffn_shared_up_w"]], axis=1)
    w["ef_shared_down"] = a["L1_ffn_shared_down_w"]
    w["c_earlier"] = np.triu(np.ones((P, P), np.float32), 1)
    w["c_limits"] = np.arange(0, T, P, dtype=np.float32)[None, :]
    w["c_numbers"] = np.arange(NT + E - 1, dtype=np.float32)[None, :]
    w["c_order"] = np.arange(E, 0, -1, dtype=np.float32)[None, :]
    w["c_ones"] = np.ones((P, P), np.float32)
    return {k: np.ascontiguousarray(v) for k, v in w.items()}


def kernel(**inputs):
    import concourse.bacc as _bacc
    from concourse.bass_utils import run_bass_kernel_spmd as _run

    nc = _bacc.Bacc("TRN2", target_bir_lowering=False, num_devices=1)
    arrays = lay_out(inputs)
    w = {k: nc.dram_tensor(f"in_{k}", v.shape, mybir.dt.from_np(v.dtype), kind="ExternalInput").ap()
         for k, v in arrays.items()}
    out = nc.dram_tensor("out_dram", (T, D), F32, kind="ExternalOutput").ap()
    build(nc, w, out)
    r = _run(nc, [{f"in_{k}": v for k, v in arrays.items()}], core_ids=[0])
    return r.results[0]["out_dram"].reshape(1, T, D)
```
